# Optimizing a Trainium2 kernel written in Bass

```python
import numpy as np
import jax
import jax.numpy as jnp

def _softmax(x, axis=-1):
    return jax.nn.softmax(x, axis=axis)

def _gelu(x):
    return jax.nn.gelu(x, approximate=True)

def _silu(x):
    return jax.nn.silu(x)

def _sigmoid(x):
    return jax.nn.sigmoid(x)

def _layernorm(x, axis=-1, eps=1e-05):
    m = jnp.mean(x, axis=axis, keepdims=True)
    v = jnp.var(x, axis=axis, keepdims=True)
    return (x - m) / jnp.sqrt(v + eps)

def _scatter_add(tgt, idx, src, axis=0):
    return tgt.at[idx].add(src)

def _segment_sum(src, seg, n):
    return jax.ops.segment_sum(src, seg, n)
kernel_name = 'mk_gps_d2_gnn_r16_280b8b'

def setup_inputs(seed: int=0):
    np.random.seed(seed)
    _w = jnp.asarray

    def _rec_inputs():
        import jax
        import jax.numpy as jnp
        _gk = jax.random.key(seed)
        x = -0.0001126 + 1 * jax.random.normal(jax.random.fold_in(_gk, 1), (3125, 256), jnp.float32)
        src = jax.random.randint(jax.random.fold_in(_gk, 2), (50000,), 0, 3125, jnp.int32)
        dst = jax.random.randint(jax.random.fold_in(_gk, 3), (50000,), 0, 3125, jnp.int32)
        _o = jnp.argsort(dst, stable=True)
        src = src[_o]
        dst = dst[_o]
        edge_type_8 = jax.random.randint(jax.random.fold_in(_gk, 12), (50000,), 0, 8, jnp.int32)
        return (x, src, dst, edge_type_8)
    x, src, dst, edge_type_8 = _rec_inputs()

    def _L0_gnn_setup():
        import jax, jax.numpy as jnp
        import numpy as np
        N, E, R, H, D = (1875, 18750, 8, 8, 32)
        IN_F = 256
        NEG_SLOPE = 0.2
        key = jax.random.key(seed)
        k = jax.random.split(key, 6)
        x = jax.random.normal(k[0], (N, IN_F), dtype=jnp.float32)
        W = jax.random.normal(k[1], (R, H * D, IN_F), dtype=jnp.float32) * 0.05
        attn_src = jax.random.normal(k[2], (H, D), dtype=jnp.float32) * 0.1
        attn_dst = jax.random.normal(k[3], (H, D), dtype=jnp.float32) * 0.1
        edge_index = jax.random.randint(k[4], (2, E), 0, N, dtype=jnp.int64) if jax.config.read('jax_enable_x64') else jax.random.randint(k[4], (2, E), 0, N, dtype=jnp.int32)
        edge_type = jax.random.randint(k[5], (E,), 0, R, dtype=edge_index.dtype)
        return dict(x=x, W=W, attn_src=attn_src, attn_dst=attn_dst, edge_index=edge_index, edge_type=edge_type)
    _L0_gnn_all = _L0_gnn_setup()
    _L0_gnn_in = {k: v for k, v in _L0_gnn_all.items() if k in ('W', 'attn_src', 'attn_dst')}
    del _L0_gnn_all

    def _L0_mix_setup():
        import jax, jax.numpy as jnp
        import numpy as np
        HEADS = 4
        DIM_HEAD = 32
        key = jax.random.key(seed)
        k1, k2, k3 = jax.random.split(key, 3)
        B, L, D = (16, 512, 256)
        hidden = HEADS * DIM_HEAD
        x = jax.random.normal(k1, (B, L, D), dtype=jnp.float32)
        W_qkv = jax.random.normal(k2, (D, 3 * hidden), dtype=jnp.float32) * D ** (-0.5)
        W_out = jax.random.normal(k3, (hidden, D), dtype=jnp.float32) * hidden ** (-0.5)
        b_out = jnp.zeros((D,), dtype=jnp.float32)
        return {'x': x, 'W_qkv': W_qkv, 'W_out': W_out, 'b_out': b_out}
    _L0_mix_all = _L0_mix_setup()
    _L0_mix_in = {k: v for k, v in _L0_mix_all.items() if k in ('W_qkv', 'W_out', 'b_out')}
    del _L0_mix_all

    def _L0_ffn_setup():
        import jax, jax.numpy as jnp
        import numpy as np
        B, S, D, F, E, K = (8, 128, 256, 1024, 8, 2)
        key = jax.random.key(seed)
        ks = jax.random.split(key, 10)
        s = 0.02
        return {'x': jax.random.normal(ks[0], (B, S, D), dtype=jnp.float32), 'Wr': jax.random.normal(ks[1], (D, E), dtype=jnp.float32) * s, 'W1s': jax.random.normal(ks[2], (D, F), dtype=jnp.float32) * s, 'b1s': jnp.zeros((F,), dtype=jnp.float32), 'W2s': jax.random.normal(ks[3], (F, D), dtype=jnp.float32) * s, 'b2s': jnp.zeros((D,), dtype=jnp.float32), 'W1p': jax.random.normal(ks[4], (E, D, F), dtype=jnp.float32) * s, 'b1p': jnp.zeros((E, F), dtype=jnp.float32), 'W2p': jax.random.normal(ks[5], (E, F, D), dtype=jnp.float32) * s, 'b2p': jnp.zeros((E, D), dtype=jnp.float32)}
    _L0_ffn_all = _L0_ffn_setup()
    _L0_ffn_in = {k: v for k, v in _L0_ffn_all.items() if k in ('Wr', 'W1s', 'b1s', 'W2s', 'b2s', 'W1p', 'b1p', 'W2p', 'b2p')}
    del _L0_ffn_all

    def _L1_gnn_setup():
        import jax, jax.numpy as jnp
        import numpy as np
        N, E, D = (625, 20000, 256)

        def _add_self_loops(src, dst, n):
            loop = jnp.arange(n, dtype=src.dtype)
            return (jnp.concatenate([src, loop]), jnp.concatenate([dst, loop]))

        def _gcn_conv(x, W, b, src, dst, n):
            xw = x @ W
            deg = jax.ops.segment_sum(jnp.ones(src.shape[0], x.dtype), dst, num_segments=n)
            dinv = jnp.where(deg > 0, jax.lax.rsqrt(deg), 0.0)
            norm = dinv[src] * dinv[dst]
            agg = jax.ops.segment_sum(xw[src] * norm[:, None], dst, num_segments=n)
            return agg + b

        def _gat_conv(x, W, a_src, a_dst, b, src, dst, n):
            xw = x @ W
            e = jax.nn.leaky_relu((xw @ a_src)[src] + (xw @ a_dst)[dst], 0.2)
            m = jax.ops.segment_max(e, dst, num_segments=n)
            ex = jnp.exp(e - m[dst])
            s = jax.ops.segment_sum(ex, dst, num_segments=n)
            alpha = ex / (s[dst] + 1e-16)
            agg = jax.ops.segment_sum(alpha[:, None] * xw[src], dst, num_segments=n)
            return agg + b
        key = jax.random.key(seed)
        ks = jax.random.split(key, 6)
        return {'event_emb': jax.random.normal(ks[0], (N, D), jnp.float32), 'edge_index': jax.random.randint(ks[1], (2, E), 0, N), 'W1': jax.random.normal(ks[2], (D, D), jnp.float32) / np.sqrt(D).astype(np.float32), 'b1': jnp.zeros((D,), jnp.float32), 'W2': jax.random.normal(ks[3], (D, D), jnp.float32) / np.sqrt(D).astype(np.float32), 'att_src': jax.random.normal(ks[4], (D,), jnp.float32) / np.sqrt(D).astype(np.float32), 'att_dst': jax.random.normal(ks[5], (D,), jnp.float32) / np.sqrt(D).astype(np.float32), 'b2': jnp.zeros((D,), jnp.float32)}
    _L1_gnn_all = _L1_gnn_setup()
    _L1_gnn_in = {k: v for k, v in _L1_gnn_all.items() if k in ('W1', 'b1', 'W2', 'att_src', 'att_dst', 'b2')}
    del _L1_gnn_all

    def _L1_mix_setup():
        import jax, jax.numpy as jnp
        import numpy as np
        DIM = 256
        HEADS = 4
        HEAD_DIM = DIM // HEADS
        MLP_HIDDEN = DIM * 3
        B, N = (8, 256)
        EPS = 1e-05

        def _layernorm(x, g, b):
            mu = jnp.mean(x, axis=-1, keepdims=True)
            var = jnp.mean(jnp.square(x - mu), axis=-1, keepdims=True)
            return (x - mu) * jax.lax.rsqrt(var + EPS) * g + b
        key = jax.random.key(seed)
        ks = jax.random.split(key, 8)
        s = 0.02
        return {'x': jax.random.normal(ks[0], (B, N, DIM), dtype=jnp.float32), 'w_qkv': jax.random.normal(ks[1], (DIM, 3 * DIM), dtype=jnp.float32) * s, 'b_qkv': jnp.zeros((3 * DIM,), dtype=jnp.float32), 'norm_g': jnp.ones((DIM,), dtype=jnp.float32), 'norm_b': jnp.zeros((DIM,), dtype=jnp.float32), 'w_fc1': jax.random.normal(ks[2], (DIM, MLP_HIDDEN), dtype=jnp.float32) * s, 'b_fc1': jnp.zeros((MLP_HIDDEN,), dtype=jnp.float32), 'w_fc2': jax.random.normal(ks[3], (MLP_HIDDEN, DIM), dtype=jnp.float32) * s, 'b_fc2': jnp.zeros((DIM,), dtype=jnp.float32)}
    _L1_mix_all = _L1_mix_setup()
    _L1_mix_in = {k: v for k, v in _L1_mix_all.items() if k in ('w_qkv', 'b_qkv', 'norm_g', 'norm_b', 'w_fc1', 'b_fc1', 'w_fc2', 'b_fc2')}
    del _L1_mix_all

    def _L1_ffn_setup():
        import jax, jax.numpy as jnp
        import numpy as np
        B, S, D = (8, 256, 256)
        H = 4 * D
        CAPACITY = 0.5
        key = jax.random.key(seed)
        ks = jax.random.split(key, 6)
        x = jax.random.normal(ks[0], (B, S, D), dtype=jnp.float32)
        attention_mask = jnp.zeros((B, 1, 1, S), dtype=jnp.float32)
        wr = jax.random.normal(ks[1], (D, 1), dtype=jnp.float32) * 0.02
        br = jnp.zeros((1,), dtype=jnp.float32)
        w1 = jax.random.normal(ks[2], (D, H), dtype=jnp.float32) * 0.02
        b1 = jnp.zeros((H,), dtype=jnp.float32)
        w2 = jax.random.normal(ks[3], (H, D), dtype=jnp.float32) * 0.02
        b2 = jnp.zeros((D,), dtype=jnp.float32)
        return {'x': x, 'attention_mask': attention_mask, 'wr': wr, 'br': br, 'w1': w1, 'b1': b1, 'w2': w2, 'b2': b2}
    _L1_ffn_all = _L1_ffn_setup()
    _L1_ffn_in = {k: v for k, v in _L1_ffn_all.items() if k in ('attention_mask', 'wr', 'br', 'w1', 'b1', 'w2', 'b2')}
    del _L1_ffn_all
    return {'x': x, 'src': src, 'dst': dst, 'edge_type_8': edge_type_8, 'L0_gnn_W': _L0_gnn_in['W'], 'L0_gnn_attn_src': _L0_gnn_in['attn_src'], 'L0_gnn_attn_dst': _L0_gnn_in['attn_dst'], 'L0_mix_W_qkv': _L0_mix_in['W_qkv'], 'L0_mix_W_out': _L0_mix_in['W_out'], 'L0_mix_b_out': _L0_mix_in['b_out'], 'L0_ffn_Wr': _L0_ffn_in['Wr'], 'L0_ffn_W1s': _L0_ffn_in['W1s'], 'L0_ffn_b1s': _L0_ffn_in['b1s'], 'L0_ffn_W2s': _L0_ffn_in['W2s'], 'L0_ffn_b2s': _L0_ffn_in['b2s'], 'L0_ffn_W1p': _L0_ffn_in['W1p'], 'L0_ffn_b1p': _L0_ffn_in['b1p'], 'L0_ffn_W2p': _L0_ffn_in['W2p'], 'L0_ffn_b2p': _L0_ffn_in['b2p'], 'L1_gnn_W1': _L1_gnn_in['W1'], 'L1_gnn_b1': _L1_gnn_in['b1'], 'L1_gnn_W2': _L1_gnn_in['W2'], 'L1_gnn_att_src': _L1_gnn_in['att_src'], 'L1_gnn_att_dst': _L1_gnn_in['att_dst'], 'L1_gnn_b2': _L1_gnn_in['b2'], 'L1_mix_w_qkv': _L1_mix_in['w_qkv'], 'L1_mix_b_qkv': _L1_mix_in['b_qkv'], 'L1_mix_norm_g': _L1_mix_in['norm_g'], 'L1_mix_norm_b': _L1_mix_in['norm_b'], 'L1_mix_w_fc1': _L1_mix_in['w_fc1'], 'L1_mix_b_fc1': _L1_mix_in['b_fc1'], 'L1_mix_w_fc2': _L1_mix_in['w_fc2'], 'L1_mix_b_fc2': _L1_mix_in['b_fc2'], 'L1_ffn_attention_mask': _L1_ffn_in['attention_mask'], 'L1_ffn_wr': _L1_ffn_in['wr'], 'L1_ffn_br': _L1_ffn_in['br'], 'L1_ffn_w1': _L1_ffn_in['w1'], 'L1_ffn_b1': _L1_ffn_in['b1'], 'L1_ffn_w2': _L1_ffn_in['w2'], 'L1_ffn_b2': _L1_ffn_in['b2']}

def reference(x, src, dst, edge_type_8, L0_gnn_W, L0_gnn_attn_src, L0_gnn_attn_dst, L0_mix_W_qkv, L0_mix_W_out, L0_mix_b_out, L0_ffn_Wr, L0_ffn_W1s, L0_ffn_b1s, L0_ffn_W2s, L0_ffn_b2s, L0_ffn_W1p, L0_ffn_b1p, L0_ffn_W2p, L0_ffn_b2p, L1_gnn_W1, L1_gnn_b1, L1_gnn_W2, L1_gnn_att_src, L1_gnn_att_dst, L1_gnn_b2, L1_mix_w_qkv, L1_mix_b_qkv, L1_mix_norm_g, L1_mix_norm_b, L1_mix_w_fc1, L1_mix_b_fc1, L1_mix_w_fc2, L1_mix_b_fc2, L1_ffn_attention_mask, L1_ffn_wr, L1_ffn_br, L1_ffn_w1, L1_ffn_b1, L1_ffn_w2, L1_ffn_b2):
    import jax
    import jax.numpy as jnp

    def _L0_gnn_ref(x, W, attn_src, attn_dst, edge_index, edge_type):
        import jax, jax.numpy as jnp
        import numpy as np
        N, E, R, H, D = (1875, 18750, 8, 8, 32)
        IN_F = 256
        NEG_SLOPE = 0.2
        n = x.shape[0]
        r = W.shape[0]
        h, d = attn_src.shape
        h_all = jnp.einsum('nf,rof->rno', x, W).reshape(r, n, h, d)
        src, dst = (edge_index[0], edge_index[1])
        h_src = h_all[edge_type, src]
        h_dst = h_all[edge_type, dst]
        scores = jnp.einsum('ehd,hd->eh', h_src, attn_src) + jnp.einsum('ehd,hd->eh', h_dst, attn_dst)
        scores = jnp.where(scores > 0, scores, NEG_SLOPE * scores)
        amax = jnp.maximum(jax.ops.segment_max(scores, dst, num_segments=n), 0.0)
        w = jnp.exp(scores - amax[dst])
        denom = jax.ops.segment_sum(w, dst, num_segments=n) + 1e-12
        w = w / denom[dst]
        msg = h_src * w[..., None]
        out = jax.ops.segment_sum(msg, dst, num_segments=n)
        return out.reshape(n, h * d)

    def _L0_mix_ref(x, W_qkv, W_out, b_out):
        import jax, jax.numpy as jnp
        import numpy as np
        HEADS = 4
        DIM_HEAD = 32
        B, L, D = x.shape
        scale = DIM_HEAD ** (-0.5)
        qkv = jnp.einsum('bld,df->blf', x, W_qkv)
        qkv = qkv.reshape(B, L, 3, HEADS, DIM_HEAD)
        q = jnp.transpose(qkv[:, :, 0], (0, 2, 1, 3)) * scale
        k = jax.nn.softmax(jnp.transpose(qkv[:, :, 1], (0, 2, 1, 3)), axis=2)
        v = jnp.transpose(qkv[:, :, 2], (0, 2, 1, 3))
        context = jnp.einsum('bhld,bhle->bhde', k, v)
        out = jnp.einsum('bhde,bhld->bhle', context, q)
        out = jnp.transpose(out, (0, 2, 1, 3)).reshape(B, L, HEADS * DIM_HEAD)
        return jnp.einsum('blf,fd->bld', out, W_out) + b_out

    def _L0_ffn_ref(x, Wr, W1s, b1s, W2s, b2s, W1p, b1p, W2p, b2p):
        import jax, jax.numpy as jnp
        import numpy as np
        B, S, D, F, E, K = (8, 128, 256, 1024, 8, 2)
        gelu = lambda t: jax.nn.gelu(t, approximate=False)
        shared = gelu(x @ W1s + b1s) @ W2s + b2s
        rw = jax.nn.softmax(x @ Wr, axis=-1)
        topw, topi = jax.lax.top_k(rw, K)
        topw = topw / jnp.sum(topw, axis=-1, keepdims=True)
        mask = jnp.sum(jax.nn.one_hot(topi, E, dtype=topw.dtype) * topw[..., None], axis=-2)
        h = gelu(jnp.einsum('bsd,edf->bsef', x, W1p) + b1p)
        priv = jnp.einsum('bsef,efd->bsed', h, W2p) + b2p
        routed = jnp.einsum('bsed,bse->bsd', priv, mask)
        return shared + routed

    def _L1_gnn_ref(event_emb, edge_index, W1, b1, W2, att_src, att_dst, b2):
        import jax, jax.numpy as jnp
        import numpy as np
        N, E, D = (625, 20000, 256)

        def _add_self_loops(src, dst, n):
            loop = jnp.arange(n, dtype=src.dtype)
            return (jnp.concatenate([src, loop]), jnp.concatenate([dst, loop]))

        def _gcn_conv(x, W, b, src, dst, n):
            xw = x @ W
            deg = jax.ops.segment_sum(jnp.ones(src.shape[0], x.dtype), dst, num_segments=n)
            dinv = jnp.where(deg > 0, jax.lax.rsqrt(deg), 0.0)
            norm = dinv[src] * dinv[dst]
            agg = jax.ops.segment_sum(xw[src] * norm[:, None], dst, num_segments=n)
            return agg + b

        def _gat_conv(x, W, a_src, a_dst, b, src, dst, n):
            xw = x @ W
            e = jax.nn.leaky_relu((xw @ a_src)[src] + (xw @ a_dst)[dst], 0.2)
            m = jax.ops.segment_max(e, dst, num_segments=n)
            ex = jnp.exp(e - m[dst])
            s = jax.ops.segment_sum(ex, dst, num_segments=n)
            alpha = ex / (s[dst] + 1e-16)
            agg = jax.ops.segment_sum(alpha[:, None] * xw[src], dst, num_segments=n)
            return agg + b
        n = event_emb.shape[0]
        src, dst = _add_self_loops(edge_index[0], edge_index[1], n)
        x = jax.nn.relu(_gcn_conv(event_emb, W1, b1, src, dst, n))
        x = jax.nn.relu(_gat_conv(x, W2, att_src, att_dst, b2, src, dst, n))
        return x

    def _L1_mix_ref(x, w_qkv, b_qkv, norm_g, norm_b, w_fc1, b_fc1, w_fc2, b_fc2):
        import jax, jax.numpy as jnp
        import numpy as np
        DIM = 256
        HEADS = 4
        HEAD_DIM = DIM // HEADS
        MLP_HIDDEN = DIM * 3
        B, N = (8, 256)
        EPS = 1e-05

        def _layernorm(x, g, b):
            mu = jnp.mean(x, axis=-1, keepdims=True)
            var = jnp.mean(jnp.square(x - mu), axis=-1, keepdims=True)
            return (x - mu) * jax.lax.rsqrt(var + EPS) * g + b
        Bx, Nx, C = x.shape
        scale = HEAD_DIM ** (-0.5)
        qkv = (x @ w_qkv + b_qkv).reshape(Bx, Nx, 3, HEADS, HEAD_DIM)
        qkv = jnp.transpose(qkv, (2, 0, 3, 1, 4))
        q, k, v = (qkv[0], qkv[1], qkv[2])
        k = k * scale
        attn = jnp.einsum('bhnd,bhne->bhde', k, v)
        attn = jax.nn.softmax(attn, axis=-1)
        xf = jnp.einsum('bhde,bhne->bhnd', attn, q)
        xf = jnp.transpose(xf, (0, 2, 1, 3)).reshape(Bx, Nx, C)
        x = x + xf
        h = _layernorm(x, norm_g, norm_b)
        h = jax.nn.gelu(h @ w_fc1 + b_fc1, approximate=False) @ w_fc2 + b_fc2
        return x + h

    def _L1_ffn_ref(x, attention_mask, wr, br, w1, b1, w2, b2):
        import jax, jax.numpy as jnp
        import numpy as np
        B, S, D = (8, 256, 256)
        H = 4 * D
        CAPACITY = 0.5
        b, s, d = x.shape
        weights = (jnp.einsum('bsd,do->bso', x, wr) + br)[..., 0]
        k = max(1, int(CAPACITY * s))
        kk = k - 1 if k > 1 else 1
        _, idx = jax.lax.top_k(weights, k)
        sel_idx = idx[:, :kk]
        sel = jnp.take_along_axis(x, sel_idx[:, :, None], axis=1)
        h = jax.nn.gelu(jnp.einsum('bkd,dh->bkh', sel, w1) + b1)
        y = jnp.einsum('bkh,hd->bkd', h, w2) + b2
        w_sel = jnp.take_along_axis(weights, sel_idx, axis=1)
        y = y * w_sel[..., None]
        batch_idx = jnp.arange(b)[:, None]
        processed = jnp.zeros_like(x).at[batch_idx, sel_idx].set(y)
        return processed + x
    edge_index = jnp.stack([src, dst])
    xn = _layernorm(x, axis=-1)
    x = x + _L0_gnn_ref(xn, L0_gnn_W, L0_gnn_attn_src, L0_gnn_attn_dst, edge_index, edge_type_8) + _L0_mix_ref(xn[None], L0_mix_W_qkv, L0_mix_W_out, L0_mix_b_out)[0]
    x = x + _L0_ffn_ref(_layernorm(x, axis=-1)[None], L0_ffn_Wr, L0_ffn_W1s, L0_ffn_b1s, L0_ffn_W2s, L0_ffn_b2s, L0_ffn_W1p, L0_ffn_b1p, L0_ffn_W2p, L0_ffn_b2p)[0]
    xn = _layernorm(x, axis=-1)
    x = x + _L1_gnn_ref(xn, edge_index, L1_gnn_W1, L1_gnn_b1, L1_gnn_W2, L1_gnn_att_src, L1_gnn_att_dst, L1_gnn_b2) + _L1_mix_ref(xn[None], L1_mix_w_qkv, L1_mix_b_qkv, L1_mix_norm_g, L1_mix_norm_b, L1_mix_w_fc1, L1_mix_b_fc1, L1_mix_w_fc2, L1_mix_b_fc2)[0]
    x = x + _L1_ffn_ref(_layernorm(x, axis=-1)[None], L1_ffn_attention_mask, L1_ffn_wr, L1_ffn_br, L1_ffn_w1, L1_ffn_b1, L1_ffn_w2, L1_ffn_b2)[0]
    return x

_drawn_inputs = setup_inputs


def setup_inputs(seed=0):
    import zlib

    import numpy as np

    out = dict(_drawn_inputs(seed))
    spreads = {'L0_mix_b_out': (0.0, 0.1),
     'L0_ffn_b1s': (0.0, 0.1),
     'L0_ffn_b2s': (0.0, 0.1),
     'L0_ffn_b1p': (0.0, 0.326),
     'L0_ffn_b2p': (0.0, 0.1),
     'L1_gnn_b1': (0.0, 0.471),
     'L1_gnn_b2': (0.0, 0.1),
     'L1_mix_b_qkv': (0.0, 0.1),
     'L1_mix_norm_g': (1.0, 0.6),
     'L1_mix_norm_b': (0.0, 0.8),
     'L1_mix_b_fc1': (0.0, 0.523),
     'L1_mix_b_fc2': (0.0, 0.1),
     'L1_ffn_b1': (0.0, 0.8),
     'L1_ffn_b2': (0.0, 0.8)}
    factors = {'L1_gnn_att_src': 28.575,
     'L1_gnn_att_dst': 39.653,
     'L1_ffn_wr': 5.737,
     'L1_ffn_w1': 7.051,
     'L1_ffn_w2': 6.562}
    for name, (base, spread) in spreads.items():
        noise = np.random.default_rng([zlib.crc32(name.encode()), seed]).standard_normal(out[name].shape)
        drawn = base * np.exp(spread * noise) if base else spread * noise
        out[name] = jnp.asarray(drawn.astype(out[name].dtype))
    for name, factor in factors.items():
        out[name] = (out[name] * factor).astype(out[name].dtype)
    return out
```

```python
import itertools
from contextlib import ExitStack, contextmanager

import concourse.bass as bass
from concourse import mybir

ALU = mybir.AluOpType
ACT = mybir.ActivationFunctionType
AX = mybir.AxisListType
F32 = mybir.dt.float32
I32 = mybir.dt.int32
U32 = mybir.dt.uint32

P = 128
N = 3125
D = 256
DC = D // P
NT = (N + P - 1) // P
NP = NT * P
TAIL = N - (NT - 1) * P
U = 5
assert NT % U == 0
CREDIT = 5
NEG = -1.0e30
R0, H0, D0 = 8, 8, 32
EPS = 1e-5
STAGES = itertools.count()


def before(u, slots, unroll=U):
    d = 1
    while ((u - d) % unroll) % slots != u % slots:
        d += 1
    return d


def earlier(i, u, slots, unroll=U):
    mine = [v for v in range(unroll) if v % slots == u % slots]
    return i * len(mine) + mine.index(u)


@contextmanager
def stage(nc, *names):
    here = next(STAGES)
    sems = [nc.alloc_semaphore(f"{n}_{here}") for n in names]
    with nc.Block() as block:
        yield (block, *sems)
    nc.clear_and_free_semaphores(sems)
    nc.all_engine_barrier()


class Mem:

    def __init__(self, nc):
        self.nc, self.ctx = nc, ExitStack()

    def __enter__(self):
        return self

    def __exit__(self, *a):
        return self.ctx.__exit__(*a)

    def sb(self, name, shape, dt=F32):
        return self.ctx.enter_context(self.nc.sbuf_tensor(name, shape, dt))

    def ps(self, name, shape, dt=F32):
        return self.ctx.enter_context(self.nc.psum_tensor(name, shape, dt))


def constants(nc, c, x, x_in):
    with Mem(nc) as m, stage(nc, "x_zeroed", "x_loaded", "iotas", "chain") as (block, x_zeroed, x_loaded, iotas, chain):
        part = c.part

        @block.gpsimd
        def _(pool):
            pool.iota(c.iota[:], [[1, P]], 0, 0, allow_small_or_imprecise_dtypes=True)
            pool.iota(part[:], [[0, 1]], 0, 1, allow_small_or_imprecise_dtypes=True)
            pool.iota(c.head[:], [[P, DC], [-D0, H0]], 0, 1, allow_small_or_imprecise_dtypes=True)
            pool.iota(c.token[:], [[P, NT]], 0, 1, allow_small_or_imprecise_dtypes=True).then_inc(iotas, 1)

        @block.sync
        def _(sp):
            full = (NT - 1) * P
            sp.dma_start(x[:, 0:NT - 1, :], x_in[0:full].rearrange("(t p) d -> p t d", p=P)).then_inc(x_loaded, 16)
            sp.wait_ge(x_zeroed, 1)
            sp.dma_start(x[0:TAIL, NT - 1, :], x_in[full:N]).then_inc(x_loaded, 16)
            sp.wait_ge(x_loaded, 32)

        @block.vector
        def _(dve):
            dve.memset(x[:, NT - 1, :], 0.0).then_inc(x_zeroed, 1)
            dve.memset(c.ones[:], 1.0)
            dve.wait_ge(iotas, 1)
            dve.tensor_scalar(c.ident[:], c.iota[:], part[:, 0:1], None, ALU.is_equal)
            dve.tensor_scalar(c.valid[:], c.token[:], float(N), None, ALU.is_lt).then_inc(chain, 1)
            dve.tensor_scalar(c.headge[:], c.head[:], 0.0, None, ALU.is_ge).then_inc(chain, 1)
            dve.wait_ge(chain, 2)
            dve.tensor_scalar(c.mask[:], c.valid[:], -1.0, -NEG, ALU.add, ALU.mult)
            dve.scalar_tensor_tensor(out=c.head32[:], in0=c.head[:], scalar=float(D0), in1=c.headge[:],
                                     op0=ALU.is_lt, op1=ALU.mult)


class Consts:
    def __init__(self, m):
        self.part = m.sb("part", [P, 1])
        self.iota = m.sb("iota", [P, P])
        self.head = m.sb("head", [P, DC, H0])
        self.headge = m.sb("headge", [P, DC, H0])
        self.head32 = m.sb("head32", [P, DC, H0])
        self.token = m.sb("token", [P, NT])
        self.valid = m.sb("valid", [P, NT])
        self.mask = m.sb("mask", [P, NT])
        self.ones = m.sb("ones", [P, P])
        self.ident = m.sb("ident", [P, P])


def layer_norm(nc, tag, c, x, xnt, xn=None, gain=None, bias=None):
    with Mem(nc) as m, stage(nc, *(tag + n for n in (
            "stats", "moments", "std", "rstd", "normed", "turned", "kept", "evacuated"))) as (
            block, stats, moments, std, rstd, normed, turned, kept, evacuated):
        st = m.sb(tag + "st", [P, NT, 6])
        mean2, mean, gap, gap2, m2, var, vareps, sd, r0, r1, r2, r3, rs = (
            m.sb(tag + n, [P, NT]) for n in ("mean2", "mean", "gap", "gap2", "m2", "var", "vareps", "sd", "r0", "r1", "r2", "r3", "rs"))
        slot = m.sb(tag + "slot", [P, U, D])
        turn = m.ps(tag + "turn", [P, U, 512])

        @block.vector
        def _(dve):
            with dve.Fori(0, NT // U) as i:
                for u in range(U):
                    dve.bn_stats(st[:, i * U + u, :], x[:, i * U + u, :]).then_inc(stats, 1)
            dve.wait_ge(stats, NT)
            dve.tensor_tensor(mean2[:], st[:, :, 1], st[:, :, 4], ALU.add).then_inc(moments, 1)
            dve.tensor_tensor(gap[:], st[:, :, 1], st[:, :, 4], ALU.subtract).then_inc(moments, 1)
            dve.tensor_tensor(m2[:], st[:, :, 2], st[:, :, 5], ALU.add).then_inc(moments, 1)
            dve.wait_ge(moments, 3)
            dve.tensor_scalar(mean[:], mean2[:], 0.5, None, ALU.mult).then_inc(moments, 1)
            dve.scalar_tensor_tensor(out=gap2[:], in0=gap[:], scalar=D / 4.0, in1=gap[:],
                                     op0=ALU.mult, op1=ALU.mult).then_inc(moments, 1)
            dve.wait_ge(moments, 5)
            dve.tensor_tensor(var[:], gap2[:], m2[:], ALU.add).then_inc(moments, 1)
            dve.wait_ge(moments, 6)
            dve.tensor_scalar(vareps[:], var[:], 1.0 / D, EPS, ALU.mult, ALU.add).then_inc(moments, 1)
            dve.wait_ge(std, 1)
            dve.reciprocal(r0[:], sd[:]).then_inc(moments, 1)
            dve.wait_ge(moments, 8)
            dve.tensor_tensor(r1[:], r0[:], r0[:], ALU.mult).then_inc(moments, 1)
            dve.wait_ge(moments, 9)
            dve.tensor_tensor(r2[:], r1[:], vareps[:], ALU.mult).then_inc(moments, 1)
            dve.wait_ge(moments, 10)
            dve.tensor_scalar(r3[:], r2[:], -0.5, 1.5, ALU.mult, ALU.add).then_inc(moments, 1)
            dve.wait_ge(moments, 11)
            dve.tensor_tensor(rs[:], r0[:], r3[:], ALU.mult).then_inc(rstd, 1)
            dve.wait_ge(rstd, 1)
            with dve.Fori(0, NT // U) as i:
                for u in range(U):
                    t = i * U + u
                    dve.wait_ge(turned, t - U + 1 + CREDIT)
                    if xn is not None:
                        dve.wait_ge(kept, t - U + 1 + CREDIT)
                    dve.tensor_scalar(slot[:, u, :], x[:, t, :], mean[:, bass.ts(t, 1)], rs[:, bass.ts(t, 1)],
                                      ALU.subtract, ALU.mult).then_inc(normed, 1)

        @block.gpsimd
        def _(pool):
            if xn is None:
                return
            pool.sem_inc(kept, CREDIT)
            with pool.Fori(0, NT // U) as i:
                for u in range(U):
                    t = i * U + u
                    pool.wait_ge(normed, t + 1)
                    pool.tensor_copy(xn[:, t, :], slot[:, u, :]).then_inc(kept, 1)

        @block.tensor
        def _(pe):
            pe.sem_inc(turned, CREDIT)
            with pe.Fori(0, NT // U) as i:
                for u in range(U):
                    t = i * U + u
                    pe.wait_ge(normed, t + 1)
                    pe.wait_ge(evacuated, t - U + 1 + CREDIT)
                    for k in range(DC):
                        last = pe.transpose(turn[:, u, k * P:(k + 1) * P], slot[:, u, k * P:(k + 1) * P], c.ident[:])
                    last.then_inc(turned, 1)

        @block.scalar
        def _(act):
            act.wait_ge(moments, 7)
            act.activation(sd[:], vareps[:], ACT.Sqrt).then_inc(std, 1)
            act.sem_inc(evacuated, CREDIT)
            with act.Fori(0, NT // U) as i:
                for u in range(U):
                    t = i * U + u
                    act.wait_ge(turned, t + 1 + CREDIT)
                    for k in range(DC):
                        dst = xnt[:, k, bass.ts(t, P)]
                        src = turn[:, u, k * P:(k + 1) * P]
                        if gain is None:
                            last = act.copy(dst, src)
                        else:
                            last = act.activation(dst, src, ACT.Identity, scale=gain[:, k:k + 1], bias=bias[:, k:k + 1])
                    last.then_inc(evacuated, 1)


HV = R0 * D
CS, CT, CK, CV = HV, HV + R0 * H0, HV + 2 * R0 * H0, HV + 2 * R0 * H0 + P
COLS0 = CV + P
CHUNKS0 = [(lo, min(lo + 512, COLS0)) for lo in range(0, COLS0, 512)]


def weights0(nc, c, a, cat):
    with Mem(nc) as m, stage(nc, "w_loaded", "av_loaded", "kv_loaded", "blocked", "turned", "kept", "scored") as (
            block, w_loaded, av_loaded, kv_loaded, blocked, turned, kept, scored):
        w = m.sb("w0", [P, R0 * DC, D])
        av = m.sb("av0", [P, 2, DC])
        heads = m.sb("heads0", [P, DC, 2, H0])
        turn = m.ps("turn0", [P, 2, 512])
        score = m.ps("score0", [P, DC, R0, 2 * H0])

        @block.sync
        def _(sp):
            sp.dma_start(w[:], a["L0_gnn_W"].rearrange("r o f -> (r o) f").rearrange("(q p) f -> p q f", p=P)).then_inc(w_loaded, 16)
            for s, n in enumerate(("attn_src", "attn_dst")):
                sp.dma_start(av[:, s, :], a["L0_gnn_" + n].rearrange("h d -> (h d)").rearrange("(k p) -> p k", p=P),
                             allow_slow_non_contiguous=True).then_inc(av_loaded, 16)
            sp.dma_start(cat[:, :, CK:COLS0], a["L0_mix_W_qkv"].rearrange("(k p) j -> p k j", p=P)[:, :, P:3 * P]).then_inc(kv_loaded, 16)
            sp.wait_ge(kv_loaded, 16)

        @block.vector
        def _(dve):
            dve.wait_ge(av_loaded, 32)
            for k in range(DC):
                for s in range(2):
                    dve.tensor_scalar(heads[:, k, s, :], c.head32[:, k, :], av[:, s, k:k + 1], None,
                                      ALU.mult).then_inc(blocked, 1)
            dve.wait_ge(scored, 1)
            for k in range(DC):
                for s in range(2):
                    dst = cat[:, k, CS + s * R0 * H0:CS + (s + 1) * R0 * H0].rearrange("p (r h) -> p r h", h=H0)
                    dve.tensor_copy(dst, score[:, k, :, s * H0:(s + 1) * H0])

        @block.tensor
        def _(pe):
            pe.wait_ge(w_loaded, 16)
            for r in range(R0):
                if r >= 2:
                    pe.wait_ge(kept, r - 1)
                for k in range(DC):
                    for o in range(DC):
                        last = pe.transpose(turn[:, r % 2, (k * DC + o) * P:(k * DC + o + 1) * P],
                                            w[:, r * DC + o, k * P:(k + 1) * P], c.ident[:])
                last.then_inc(turned, 1)
            pe.wait_ge(blocked, 2 * DC)
            for r in range(R0):
                for k in range(DC):
                    for o in range(DC):
                        last = pe.matmul(score[:, k, r, :], w[:, r * DC + o, k * P:(k + 1) * P],
                                         heads[:, o, :, :].rearrange("p s h -> p (s h)"), start=(o == 0), stop=(o == DC - 1))
            last.then_inc(scored, 1)

        @block.scalar
        def _(act):
            for r in range(R0):
                act.wait_ge(turned, r + 1)
                act.copy(cat[:, :, r * D:(r + 1) * D], turn[:, r % 2, :].rearrange("p (k o) -> p k o", k=DC)).then_inc(kept, 1)


def project0(nc, c, xnt, cat, values, source_scores, target, keys, vals):
    nb = len(CHUNKS0)
    with Mem(nc) as m, stage(nc, "staged", "used", "multiplied", "by_act", "by_dve", "stored0", "stored1", "zeroed") as (
            block, staged, used, multiplied, by_act, by_dve, stored0, stored1, zeroed):
        stored = (stored0, stored1)
        slot = m.sb("xslot0", [P, 2, DC, P])
        hv = m.sb("hv0", [P, 2, HV])
        ss = m.sb("ss0", [P, 2, R0 * H0])
        acc = m.ps("acc0", [P, nb, 512])
        vrows = values.rearrange("(r t p) d -> t p r d", r=R0, p=P)
        srows = source_scores.rearrange("(r t p) h -> t p r h", r=R0, p=P)

        @block.gpsimd
        def _(pool):
            with pool.Fori(0, NT // U) as i:
                for u in range(U):
                    t = i * U + u
                    pool.wait_ge(used, t - before(u, 2) + 1 + CREDIT)
                    pool.tensor_copy(slot[:, u % 2], xnt[:, :, bass.ts(t, P)]).then_inc(staged, 1)

        @block.tensor
        def _(pe):
            pe.sem_inc(used, CREDIT)
            with pe.Fori(0, NT // U) as i:
                for u in range(U):
                    t = i * U + u
                    pe.wait_ge(staged, t + 1)
                    pe.wait_ge(by_act, t + CREDIT)
                    pe.wait_ge(by_dve, t + CREDIT)
                    for b, (lo, hi) in enumerate(CHUNKS0):
                        for k in range(DC):
                            last = pe.matmul(acc[:, b, 0:hi - lo], slot[:, u % 2, k, :], cat[:, k, lo:hi],
                                             start=(k == 0), stop=(k == DC - 1))
                        if b < nb - 1:
                            last.then_inc(multiplied, 1)
                    last.then_inc(used, 1)

        @block.scalar
        def _(act):
            act.sem_inc(by_act, CREDIT)
            with act.Fori(0, NT // U) as i:
                for u in range(U):
                    t = i * U + u
                    act.wait_ge(stored[u % 2], earlier(i, u, 2) * 32 + 16)
                    for b in range(2):
                        act.wait_ge(multiplied, t * (nb - 1) + b + 1)
                        last = act.copy(hv[:, u % 2, b * 512:(b + 1) * 512], acc[:, b, :])
                    last.then_inc(by_act, 1)

        @block.vector
        def _(dve):
            dve.memset(target[:, NT, :], 0.0).then_inc(zeroed, 1)
            dve.sem_inc(by_dve, CREDIT)
            with dve.Fori(0, NT // U) as i:
                for u in range(U):
                    t = i * U + u
                    dve.wait_ge(stored[u % 2], earlier(i, u, 2) * 32 + 16)
                    for b in range(2, 4):
                        dve.wait_ge(multiplied, t * (nb - 1) + b + 1)
                        dve.tensor_copy(hv[:, u % 2, b * 512:(b + 1) * 512], acc[:, b, :])
                    dve.wait_ge(used, t + 1 + CREDIT)
                    dve.tensor_copy(ss[:, u % 2, :], acc[:, 4, CS - HV:CT - HV])
                    dve.tensor_copy(target[:, t, :], acc[:, 4, CT - HV:CK - HV])
                    dve.tensor_scalar(keys[:, t, :], acc[:, 4, CK - HV:CV - HV], c.mask[:, bass.ts(t, 1)], None, ALU.add)
                    dve.tensor_copy(vals[:, t, :], acc[:, 4, CV - HV:COLS0 - HV]).then_inc(by_dve, 1)

        @block.sync
        def _(sp):
            for q in stored:
                sp.sem_inc(q, 16)
            with sp.Fori(0, NT // U) as i:
                for u in range(U):
                    t = i * U + u
                    sp.wait_ge(by_act, t + 1 + CREDIT)
                    sp.wait_ge(by_dve, t + 1 + CREDIT)
                    sp.dma_start(vrows[t], hv[:, u % 2, :].rearrange("p (r d) -> p r d", r=R0)).then_inc(stored[u % 2], 16)
                    sp.dma_start(srows[t], ss[:, u % 2, :].rearrange("p (r h) -> p r h", r=R0)).then_inc(stored[u % 2], 16)
            for n, q in enumerate(stored):
                sp.wait_ge(q, 16 + 32 * (NT // U) * len(range(n, U, 2)))


def linear_attention0(nc, c, a, keys, vals, g):
    scale = 32 ** -0.5
    with Mem(nc) as m, stage(nc, "loaded", "dve_did", "pe_did", "act_did", "exped") as (
            block, loaded, dve_did, pe_did, act_did, exped):
        wq = m.sb("wq0", [P, DC, P])
        wqt = m.sb("wqt0", [P, DC, P])
        wo = m.sb("wo0", [P, D])
        part_max = m.sb("pmax0", [P, P])
        col_max = m.sb("cmax0", [P, 1])
        diag = m.sb("diag0", [P, P])
        max_row = m.sb("maxrow0", [P, P])
        inv = m.sb("inv0", [P, P])
        ctx = m.sb("ctx0", [P, P])
        ctx2 = m.sb("ctxs0", [P, P])
        mo = m.sb("mo0", [P, D])
        turn = m.ps("mt0", [P, 512])
        rows = m.ps("mr0", [P, 512])
        ctx_ps = m.ps("mc0", [P, 512])
        sum_ps = m.ps("ms0", [P, 512])
        mo_ps = m.ps("mm0", [P, 512])
        g_ps = m.ps("mg0", [P, DC, D])

        @block.sync
        def _(sp):
            sp.dma_start(wq[:], a["L0_mix_W_qkv"].rearrange("(k p) j -> p k j", p=P)[:, :, 0:P]).then_inc(loaded, 16)
            sp.dma_start(wo[:], a["L0_mix_W_out"]).then_inc(loaded, 16)

        @block.vector
        def _(dve):
            dve.tensor_reduce(part_max[:], keys[:].rearrange("p t d -> p d t"), AX.X, ALU.max).then_inc(dve_did, 1)
            dve.wait_ge(pe_did, 1)
            dve.tensor_reduce(col_max[:], turn[:, 0:P], AX.X, ALU.max).then_inc(dve_did, 1)
            dve.wait_ge(dve_did, 2)
            dve.tensor_scalar(diag[:], c.ident[:], col_max[:, 0:1], None, ALU.mult).then_inc(dve_did, 1)
            dve.wait_ge(pe_did, 2)
            dve.tensor_copy(max_row[:], rows[:, 0:P]).then_inc(dve_did, 1)
            dve.wait_ge(dve_did, 4)
            dve.tensor_tensor(keys[:], keys[:], max_row[:].unsqueeze(1).broadcast_to([P, NT, P]), ALU.subtract).then_inc(dve_did, 1)
            dve.wait_ge(pe_did, 4)
            dve.reciprocal(inv[:], sum_ps[:, 0:P]).then_inc(dve_did, 1)
            dve.wait_ge(dve_did, 6)
            dve.scalar_tensor_tensor(out=ctx[:], in0=ctx_ps[:, 0:P], scalar=scale, in1=inv[:], op0=ALU.mult, op1=ALU.mult).then_inc(dve_did, 1)
            dve.wait_ge(dve_did, 7)
            dve.tensor_tensor(ctx2[:].rearrange("p (h d) -> p h d", d=32), ctx[:].rearrange("p (h d) -> p h d", d=32),
                              c.head32[:, 0, 0:4].unsqueeze(2).broadcast_to([P, 4, 32]), ALU.mult).then_inc(dve_did, 1)
            dve.wait_ge(pe_did, 5)
            dve.tensor_copy(mo[:], mo_ps[:, 0:D]).then_inc(dve_did, 1)
            dve.wait_ge(pe_did, 6)
            dve.tensor_copy(g[:], g_ps[:])

        @block.scalar
        def _(act):
            act.wait_ge(pe_did, 3)
            act.copy(wqt[:], turn[:, P:P + DC * P].rearrange("p (k f) -> p k f", k=DC)).then_inc(act_did, 1)
            act.wait_ge(dve_did, 5)
            act.activation(keys[:], keys[:], ACT.Exp).then_inc(exped, 1)

        @block.tensor
        def _(pe):
            pe.wait_ge(dve_did, 1)
            pe.transpose(turn[:, 0:P], part_max[:], c.ident[:]).then_inc(pe_did, 1)
            pe.wait_ge(dve_did, 3)
            pe.matmul(rows[:, 0:P], c.ones[:], diag[:], start=True, stop=True).then_inc(pe_did, 1)
            pe.wait_ge(loaded, 32)
            for k in range(DC):
                last = pe.transpose(turn[:, (k + 1) * P:(k + 2) * P], wq[:, k, :], c.ident[:])
            last.then_inc(pe_did, 1)
            pe.wait_ge(exped, 1)
            for t in range(NT):
                pe.matmul(sum_ps[:, 0:P], c.ones[:], keys[:, t, :], start=(t == 0), stop=(t == NT - 1))
                last = pe.matmul(ctx_ps[:, 0:P], vals[:, t, :], keys[:, t, :], start=(t == 0), stop=(t == NT - 1))
            last.then_inc(pe_did, 1)
            pe.wait_ge(dve_did, 8)
            pe.matmul(mo_ps[:, 0:D], ctx2[:], wo[:], start=True, stop=True).then_inc(pe_did, 1)
            pe.wait_ge(dve_did, 9)
            pe.wait_ge(act_did, 1)
            for k in range(DC):
                last = pe.matmul(g_ps[:, k, :], wqt[:, k, :], mo[:], start=True, stop=True)
            last.then_inc(pe_did, 1)


def add_product(nc, tag, xnt, g, bias, c, x):
    with Mem(nc) as m, stage(nc, "staged", "multiplied", "added") as (block, staged, multiplied, added):
        slot = m.sb(tag + "slot", [P, 2, DC, P])
        acc = m.ps(tag + "acc", [P, 2, 512])

        @block.gpsimd
        def _(pool):
            with pool.Fori(0, NT // U) as i:
                for u in range(U):
                    t = i * U + u
                    pool.wait_ge(multiplied, t - before(u, 2) + 1 + CREDIT)
                    pool.tensor_copy(slot[:, u % 2], xnt[:, :, bass.ts(t, P)]).then_inc(staged, 1)

        @block.tensor
        def _(pe):
            pe.sem_inc(multiplied, CREDIT)
            with pe.Fori(0, NT // U) as i:
                for u in range(U):
                    t = i * U + u
                    pe.wait_ge(staged, t + 1)
                    pe.wait_ge(added, t - before(u, 2) + 1 + CREDIT)
                    for k in range(DC):
                        pe.matmul(acc[:, u % 2, 0:D], slot[:, u % 2, k, :], g[:, k, :], start=(k == 0), stop=False)
                    pe.matmul(acc[:, u % 2, 0:D], c.ones[0:1, :], bias[:], start=False, stop=True).then_inc(multiplied, 1)

        @block.vector
        def _(dve):
            dve.sem_inc(added, CREDIT)
            with dve.Fori(0, NT // U) as i:
                for u in range(U):
                    t = i * U + u
                    dve.wait_ge(multiplied, t + 1 + CREDIT)
                    dve.tensor_tensor(x[:, t, :], x[:, t, :], acc[:, u % 2, 0:D], ALU.add).then_inc(added, 1)


E = 50000
BLK = 256
NB = (E + BLK - 1) // BLK
G = NB + NT - 1
K2 = BLK // P
HALF = G // 2
assert G == 2 * HALF and HALF % U == 0 and HALF <= P
FAR = 4095
LOW = 24
BH = NB // 2


class Edges:

    def __init__(self, m):
        self.src = m.sb("e_src", [P, K2, G], I32)
        self.value_row = m.sb("e_row", [P, K2, G], I32)
        self.local = m.sb("e_local", [P, K2, G])
        self.rel = m.sb("e_rel", [P, K2, G])
        self.step = m.sb("e_step", [HALF, 2, BLK])
        self.back = m.sb("e_back", [HALF, 2, BLK])
        self.first = m.sb("e_first", [HALF, 2, BLK])
        self.last = m.sb("e_last", [HALF, 2, BLK])
        self.cont = m.sb("e_cont", [H0, G])
        self.over_prev = m.sb("e_over_prev", [H0, G])
        self.over_this = m.sb("e_over_this", [H0, G])
        self.tile = m.sb("e_tile", [1, G], I32)


def find_groups(nc, c, a, e, packed, tiles):
    with Mem(nc) as m, stage(nc, "zeroed", "loaded", "iotas", "packed", "stored", "counted", "chain",
                             "fetched", "tiles_out", "tiles_in", "turned", "kept") as (
            block, zeroed, loaded, iotas, packed_up, stored, counted, chain, fetched, tiles_out, tiles_in, turned, kept):
        raw = m.sb("g_raw", [BH, 3, 2, BLK], I32)
        sh = m.sb("g_sh", [BH, 2, 2, BLK], I32)
        pk = m.sb("g_pk", [BH, 2, BLK], I32)
        dstf = m.sb("g_dstf", [BH, 2, BLK])
        junk = m.sb("g_junk", [BH, 2, BLK])
        cnt = m.sb("g_cnt", [BH, NT + 1])
        off = m.sb("g_off", [P, NT + 1])
        offm = m.sb("g_offm", [P, 2, NT])
        offi = m.sb("g_offi", [P, 2, NT], I32)
        blki = m.sb("g_blki", [P, 2, NT], I32)
        blk = m.sb("g_blk", [P, 2, NT])
        some = m.sb("g_some", [P, NT])
        span = m.sb("g_span", [P, NT])
        num = m.sb("g_num", [P, NT])
        cum = m.sb("g_cum", [P, NT])
        base = m.sb("g_base", [P, NT])
        base2 = m.sb("g_base2", [P, NT])
        gid = m.sb("g_gid", [P, 2])
        tid = m.sb("g_tid", [P, NT])
        cmp = m.sb("g_cmp", [P, 2, NT])
        cmp2 = m.sb("g_cmp2", [P, 2, NT])
        cmp3 = m.sb("g_cmp3", [P, 2, NT])
        tile = m.sb("g_tile", [P, 2])
        rowf = m.sb("g_rowf", [P, 2])
        rowf2 = m.sb("g_rowf2", [P, 2])
        row = m.sb("g_row", [P, 2], I32)
        tilei = m.sb("g_tilei", [P, 2], I32)
        got = m.sb("g_got", [HALF, 2, BLK], I32)
        bits = m.sb("g_bits", [HALF, 3, 2, BLK], I32)
        f = m.sb("g_f", [HALF, 3, 2, BLK])
        vrow = m.sb("g_vrow", [HALF, 2, BLK])
        loc = m.sb("g_loc", [HALF, 2, BLK])
        ok0 = m.sb("g_ok0", [HALF, 2, BLK])
        ok = m.sb("g_ok", [HALF, 2, BLK])
        key0 = m.sb("g_key0", [HALF, 2, BLK])
        key = m.sb("g_key", [HALF, 2, BLK])
        tile128 = m.sb("g_t128", [P, 2])
        edge = m.sb("g_edge", [HALF, 2, BLK])
        runs = m.sb("g_runs", [HALF, 2])
        rep = m.sb("g_rep", [HALF, 2, 3, H0])
        rows = m.sb("g_rows", [H0, 3, G])
        same = m.sb("g_same", [H0, G])
        prev = m.sb("g_prev", [H0, G])
        this = m.sb("g_this", [H0, G])
        total = m.ps("g_total", [P, 512])
        turn = m.ps("g_turn", [P, 4, 512])
        trow = m.ps("g_trow", [P, 3, 512])

        @block.sync
        def _(sp):
            sp.wait_ge(zeroed, 1)
            cut = BH * BLK
            for n, name in enumerate(("src", "dst", "edge_type_8")):
                v = a[name]
                sp.dma_start(raw[:, n, 0, :], v[0:cut].rearrange("(b e) -> b e", e=BLK)).then_inc(loaded, 16)
                sp.dma_start(raw[0:BH - 1, n, 1, :], v[cut:(NB - 1) * BLK].rearrange("(b e) -> b e", e=BLK)).then_inc(loaded, 16)
                sp.dma_start(raw[BH - 1:BH, n, 1, 0:E - (NB - 1) * BLK],
                             v[(NB - 1) * BLK:E].rearrange("(b e) -> b e", b=1)).then_inc(loaded, 16)
            sp.wait_ge(packed_up, 1)
            for h in range(2):
                sp.dma_start(packed[h * BH:(h + 1) * BH], pk[:, h, :]).then_inc(stored, 16)
            sp.wait_ge(chain, 18)
            for h in range(2):
                sp.dma_start(tiles[0, h * HALF:(h + 1) * HALF].rearrange("(g a) -> g a", a=1), tilei[0:HALF, h:h + 1],
                             allow_slow_non_contiguous=True).then_inc(tiles_out, 16)
            sp.wait_ge(tiles_out, 32)
            sp.dma_start(e.tile[:], tiles).then_inc(tiles_in, 16)
            sp.wait_ge(tiles_in, 16)

        @block.gpsimd
        def _(pool):
            pool.iota(gid[:], [[HALF, 2]], 0, 1, allow_small_or_imprecise_dtypes=True)
            pool.iota(tid[:], [[1, NT]], 0, 0, allow_small_or_imprecise_dtypes=True).then_inc(iotas, 1)
            pool.wait_ge(stored, 32)
            pool.wait_ge(chain, 17)
            for h in range(2):
                pool.indirect_dma_start(got[:, h, :], None, packed, bass.IndirectOffsetOnAxis(row[0:HALF, h:h + 1], 0)).then_inc(fetched, 16)

        @block.tensor
        def _(pe):
            pe.wait_ge(counted, NT + 1)
            pe.matmul(total[:, 0:NT + 1], c.ones[0:BH, :], cnt[:], start=True, stop=True).then_inc(turned, 1)
            for q, (n, src) in enumerate(((22, f[:, 0]), (23, vrow), (24, loc), (22, f[:, 2]))):
                pe.wait_ge(chain, n)
                for h in range(2):
                    for k in range(K2):
                        last = pe.transpose(turn[:, q, (h * K2 + k) * P:(h * K2 + k) * P + HALF],
                                            src[:, h, k * P:(k + 1) * P], c.ident[0:HALF, 0:HALF])
                last.then_inc(turned, 1)
            pe.wait_ge(chain, 35)
            for q in range(3):
                for h in range(2):
                    last = pe.transpose(trow[0:H0, q, h * HALF:(h + 1) * HALF], rep[:, h, q, :], c.ident[0:HALF, 0:HALF])
            last.then_inc(turned, 1)

        @block.scalar
        def _(act):
            def spread(q):
                return turn[:, q, :].rearrange("p (h k g) -> p h k g", h=2, k=K2)[:, :, :, 0:HALF]
            for q, dst in enumerate((e.src, e.value_row, e.local, e.rel)):
                act.wait_ge(turned, q + 2)
                act.copy(dst[:].rearrange("p k (h g) -> p h k g", h=2), spread(q))
            act.wait_ge(turned, 6)
            act.copy(rows[:], trow[0:H0, :, 0:G]).then_inc(kept, 1)

        @block.vector
        def _(dve):
            done = [0]

            def link(ins):
                done[0] += 1
                ins.then_inc(chain, 1)
                dve.wait_ge(chain, done[0])

            dve.memset(raw[:, 1, 1, :], FAR)
            dve.memset(raw[:, 0, 1, :], 0)
            dve.memset(raw[:, 2, 1, :], 0).then_inc(zeroed, 1)
            dve.wait_ge(loaded, 16 * 9)
            link(dve.tensor_scalar(sh[:, 0], raw[:, 1], 12, None, ALU.logical_shift_left))
            link(dve.tensor_scalar(sh[:, 1], raw[:, 2], 24, None, ALU.logical_shift_left))
            link(dve.tensor_tensor(pk[:], sh[:, 0], raw[:, 0], ALU.bitwise_or))
            dve.tensor_tensor(pk[:], pk[:], sh[:, 1], ALU.bitwise_or).then_inc(packed_up, 1)
            link(dve.tensor_copy(dstf[:], raw[:, 1]))
            for t in range(NT + 1):
                if t:
                    dve.wait_ge(counted, t)
                dve.tensor_scalar(junk[:], dstf[:], float(t * P), 0.0, ALU.is_lt, ALU.add,
                                  accum_out=cnt[:, t:t + 1]).then_inc(counted, 1)
            dve.wait_ge(turned, 1)
            link(dve.tensor_copy(off[:], total[:, 0:NT + 1]))
            link(dve.tensor_copy(offm[:, 0], off[:, 0:NT]))
            link(dve.tensor_scalar(offm[:, 1], off[:, 1:NT + 1], -1.0, None, ALU.add))
            link(dve.tensor_copy(offi[:], offm[:]))
            link(dve.tensor_scalar(blki[:], offi[:], 8, None, ALU.arith_shift_right))
            link(dve.tensor_copy(blk[:], blki[:]))
            link(dve.tensor_tensor(some[:], off[:, 1:NT + 1], off[:, 0:NT], ALU.is_gt))
            dve.wait_ge(iotas, 1)
            link(dve.tensor_tensor(span[:], blk[:, 1], blk[:, 0], ALU.subtract))
            link(dve.scalar_tensor_tensor(out=num[:], in0=span[:], scalar=1.0, in1=some[:], op0=ALU.add, op1=ALU.mult))
            link(dve.tensor_tensor_scan(cum[:], c.ones[:, 0:NT], num[:], 0.0, ALU.mult, ALU.add))
            link(dve.tensor_tensor(base[:], blk[:, 0], cum[:], ALU.subtract))
            dve.tensor_tensor(base2[:], base[:], num[:], ALU.add).then_inc(counted, 1)
            dve.tensor_tensor(cmp[:], cum[:].unsqueeze(1).broadcast_to([P, 2, NT]),
                              gid[:].unsqueeze(2).broadcast_to([P, 2, NT]), ALU.is_le).then_inc(counted, 1)
            dve.wait_ge(counted, NT + 3)
            dve.tensor_reduce(tile[:], cmp[:], AX.X, ALU.add).then_inc(counted, 1)
            dve.wait_ge(counted, NT + 4)
            dve.tensor_tensor(cmp2[:], tid[:].unsqueeze(1).broadcast_to([P, 2, NT]),
                              tile[:].unsqueeze(2).broadcast_to([P, 2, NT]), ALU.is_equal).then_inc(counted, 1)
            dve.wait_ge(counted, NT + 5)
            dve.tensor_tensor(cmp3[:], cmp2[:], base2[:].unsqueeze(1).broadcast_to([P, 2, NT]), ALU.mult).then_inc(counted, 1)
            dve.wait_ge(counted, NT + 6)
            dve.tensor_reduce(rowf[:], cmp3[:], AX.X, ALU.add).then_inc(counted, 1)
            dve.wait_ge(counted, NT + 7)
            link(dve.tensor_tensor(rowf2[:], rowf[:], gid[:], ALU.add))
            link(dve.tensor_scalar(row[:], rowf2[:], float(NB - 1), None, ALU.min))
            link(dve.tensor_copy(tilei[:], tile[:]))
            dve.wait_ge(fetched, 32)
            link(dve.tensor_scalar(bits[:, 0], got[:], FAR, None, ALU.bitwise_and))
            link(dve.tensor_scalar(bits[:, 1], got[:], 12, FAR, ALU.logical_shift_right, ALU.bitwise_and))
            link(dve.tensor_scalar(bits[:, 2], got[:], 24, None, ALU.logical_shift_right))
            link(dve.tensor_copy(f[:], bits[:]))
            link(dve.scalar_tensor_tensor(out=vrow[:], in0=f[:, 2], scalar=float(NP), in1=f[:, 0], op0=ALU.mult, op1=ALU.add))
            dve.tensor_scalar(tile128[:], tile[:], float(-P), None, ALU.mult).then_inc(counted, 1)
            dve.wait_ge(counted, NT + 8)
            for h in range(2):
                ins = dve.tensor_scalar(loc[:, h], f[:, 1, h], tile128[0:HALF, h:h + 1], None, ALU.add)
                if h == 0:
                    ins.then_inc(counted, 1)
            link(ins)
            dve.wait_ge(counted, NT + 9)
            link(dve.tensor_scalar(ok0[:], loc[:], 0.0, None, ALU.is_ge))
            link(dve.scalar_tensor_tensor(out=ok[:], in0=loc[:], scalar=float(P), in1=ok0[:], op0=ALU.is_lt, op1=ALU.mult))
            link(dve.scalar_tensor_tensor(out=key0[:], in0=f[:, 1], scalar=1.0, in1=ok[:], op0=ALU.add, op1=ALU.mult))
            link(dve.tensor_scalar(key[:], key0[:], -1.0, None, ALU.add))
            link(dve.memset(edge[:, :, 0:1], 0.0))
            link(dve.tensor_tensor(edge[:, :, 1:BLK], key[:, :, 1:BLK], key[:, :, 0:BLK - 1], ALU.not_equal))
            link(dve.tensor_reduce(runs[:], edge[:], AX.X, ALU.add))
            link(dve.tensor_scalar(edge[:], edge[:], NEG, None, ALU.mult))
            link(dve.tensor_copy(rep[:, :, 0, :], key[:, :, 0:1].broadcast_to([HALF, 2, H0])))
            link(dve.tensor_copy(rep[:, :, 1, :], key[:, :, BLK - 1:BLK].broadcast_to([HALF, 2, H0])))
            link(dve.tensor_scalar(rep[:, :, 2, :], runs[:].unsqueeze(2).broadcast_to([HALF, 2, H0]), 0.0, None, ALU.is_equal))
            link(dve.tensor_copy(e.step[:], edge[:]))
            link(dve.memset(e.step[:, :, 0:1], NEG))
            link(dve.tensor_copy(e.back[:, :, 0:BLK - 1], edge[:, :, 1:BLK]))
            link(dve.memset(e.back[:, :, BLK - 1:BLK], NEG))
            link(dve.memset(e.last[:, :, BLK - 1:BLK], 0.0))
            for h in range(2):
                link(dve.tensor_tensor_scan(e.first[:, h], edge[:, h], edge[:, h], 0.0, ALU.min, ALU.min))
                link(dve.tensor_tensor_scan(e.last[:, h, 0:BLK - 1][:, ::-1], edge[:, h, 1:BLK][:, ::-1],
                                            edge[:, h, 1:BLK][:, ::-1], 0.0, ALU.min, ALU.min))
            dve.wait_ge(kept, 1)
            link(dve.memset(same[:], 0.0))
            link(dve.memset(prev[:], 0.0))
            link(dve.tensor_tensor(same[:, 1:G], rows[:, 0, 1:G], rows[:, 1, 0:G - 1], ALU.is_equal))
            link(dve.tensor_tensor(prev[:, 1:G], same[:, 1:G], rows[:, 2, 0:G - 1], ALU.mult))
            link(dve.tensor_tensor(this[:], same[:], rows[:, 2, :], ALU.mult))
            link(dve.tensor_scalar(e.cont[:], same[:], -1.0, -NEG, ALU.add, ALU.mult))
            link(dve.tensor_scalar(e.over_prev[:], prev[:], -1.0, -NEG, ALU.add, ALU.mult))
            link(dve.tensor_scalar(e.over_this[:], this[:], -1.0, -NEG, ALU.add, ALU.mult))


SLOPE = 0.2


def edge_scores(nc, tag, c, e, index, table, heads, target, by_relation, scores):
    width = R0 * heads if by_relation else 2
    with Mem(nc) as m, stage(nc, "indexed", "hot", "turned", "hot_kept", "matched", "chosen", "reduced", "summed", "scored",
                             "iotas", "begun", *(f"gathered{u}" for u in range(U))) as (
            block, indexed, hot, turned, hot_kept, matched, chosen, reduced, summed, scored, iotas, begun, *gathered):
        idx = m.sb(tag + "idx", [P, U, K2], I32)
        rows = m.sb(tag + "rows", [P, U, K2, heads])
        one = m.sb(tag + "one", [P, 2, K2, P])
        onet = m.sb(tag + "onet", [P, 2, K2, P])
        pick = m.sb(tag + "pick", [P, K2, width])
        red = m.sb(tag + "red", [P, K2, heads])
        tot = m.sb(tag + "tot", [P, K2, heads])
        rid = m.sb(tag + "rid", [P, R0, heads])
        turn = m.ps(tag + "turn", [P, 2, K2, 256])
        hit = m.ps(tag + "hit", [P, 2, 512])

        def hits(u):
            return hit[:, u % 2, 0:K2 * width].rearrange("p (k w) -> p k w", k=K2)

        @block.gpsimd
        def _(pool):
            pool.iota(rid[:], [[1, R0], [0, heads]], 0, 0, allow_small_or_imprecise_dtypes=True).then_inc(iotas, 1)
            with pool.Fori(0, G // U) as i:
                for u in range(U):
                    pool.wait_ge(indexed, i * U + u + 1)
                    pool.sem_inc(begun, 1)
                    for k in range(K2):
                        pool.indirect_dma_start(rows[:, u, k, :], None, table,
                                                bass.IndirectOffsetOnAxis(idx[:, u, k:k + 1], 0)).then_inc(gathered[u], 16)

        @block.scalar
        def _(act):
            act.sem_inc(hot_kept, CREDIT)

            def index_of(i, u):
                g = i * U + u
                act.wait_ge(scored, g - U + 1 + CREDIT)
                act.copy(idx[:, u, :], index[:, :, bass.ts(g, 1)].squeeze(2)).then_inc(indexed, 1)

            with act.Fori(0, G // U) as i:
                for u in range(U):
                    index_of(i, u)
                for u in range(U):
                    g = i * U + u
                    act.wait_ge(turned, g + 1)
                    act.wait_ge(matched, g - before(u, 2) + 1 + CREDIT)
                    act.copy(onet[:, u % 2], turn[:, u % 2, :, 0:P]).then_inc(hot_kept, 1)

        @block.tensor
        def _(pe):
            pe.sem_inc(matched, CREDIT)
            with pe.Fori(0, G // U) as i:
                for u in range(U):
                    g = i * U + u
                    tile = pe.value_load(e.tile[0:1, bass.ts(g, 1)], min_val=0, max_val=NT)
                    pe.wait_ge(hot, g + 1)
                    pe.wait_ge(hot_kept, g - before(u, 2) + 1 + CREDIT)
                    for k in range(K2):
                        last = pe.transpose(turn[:, u % 2, k, 0:P], one[:, u % 2, k, :], c.ident[:])
                    last.then_inc(turned, 1)
                    pe.wait_ge(hot_kept, g + 1 + CREDIT)
                    pe.wait_ge(scored, g - before(u, 2) + 1 + CREDIT)
                    for k in range(K2):
                        last = pe.matmul(hits(u)[:, k, :], onet[:, u % 2, k, :], target[:, tile, :], start=True, stop=True)
                    last.then_inc(matched, 1)

        @block.vector
        def _(dve):
            dve.wait_ge(iotas, 1)
            dve.sem_inc(scored, CREDIT)

            def one_hot(i, u):
                g = i * U + u
                if u >= 2:
                    dve.wait_ge(turned, g - 1)
                for k in range(K2):
                    last = dve.tensor_scalar(one[:, u % 2, k, :], c.iota[:], e.local[:, k, bass.ts(g, 1)], None, ALU.is_equal)
                last.then_inc(hot, 1)

            with dve.Fori(0, G // U) as i:
                for u in range(U):
                    g = i * U + u
                    if u == 0:
                        one_hot(i, 0)
                    if u + 1 < U:
                        one_hot(i, u + 1)
                    dve.wait_ge(matched, g + 1 + CREDIT)
                    dve.wait_ge(gathered[u], (i + 1) * 16 * K2)
                    if by_relation:
                        for k in range(K2):
                            last = dve.scalar_tensor_tensor(
                                out=pick[:, k, :], in0=rid[:].rearrange("p r h -> p (r h)"), scalar=e.rel[:, k, bass.ts(g, 1)],
                                in1=hits(u)[:, k, :], op0=ALU.is_equal, op1=ALU.mult)
                        last.then_inc(chosen, 1)
                        dve.wait_ge(chosen, g + 1)
                        dve.tensor_reduce(red[:], pick[:].rearrange("p k (r h) -> p k h r", h=heads), AX.X, ALU.add).then_inc(reduced, 1)
                        dve.wait_ge(reduced, g + 1)
                        dve.tensor_tensor(tot[:], red[:], rows[:, u], ALU.add).then_inc(summed, 1)
                    else:
                        dve.wait_ge(scored, g + CREDIT)
                        dve.tensor_tensor(tot[:], hits(u)[:, :, 0:1], rows[:, u], ALU.add).then_inc(summed, 1)
                    dve.wait_ge(summed, g + 1)
                    if not by_relation:
                        dve.tensor_copy(scores[:, :, g, 1:2], hits(u)[:, :, 1:2])
                    dve.scalar_tensor_tensor(out=scores[:, :, g, 0:heads], in0=tot[:], scalar=SLOPE, in1=tot[:],
                                             op0=ALU.mult, op1=ALU.max).then_inc(scored, 1)


def segment_softmax(nc, tag, c, e, heads, channels, scores):
    step = 512 // BLK
    pairs = [(h, q) for h in range(2) for q in range(0, channels, step)]
    with Mem(nc) as m, stage(nc, "turned", "kept", "scanned", "ends", "ends_turned", "rows", "carried", "carry_turned",
                             "carry_kept", "spread", "shifted", "exped", "back_turned", "back_kept") as (
            block, turned, kept, scanned, ends, ends_turned, rows_kept, carried, carry_turned,
            carry_kept, spread, shifted, exped, back_turned, back_kept):
        s = m.sb(tag + "s", [HALF, 2, channels, BLK])
        fwd = m.sb(tag + "fwd", [HALF, 2, heads, BLK])
        top = m.sb(tag + "top", [HALF, 2, heads, BLK])
        tip = m.sb(tag + "tip", [HALF, 2, 2, heads])
        tips = m.sb(tag + "tips", [heads, 2, G])
        inc = m.sb(tag + "inc", [heads, 2, G])
        car = m.sb(tag + "car", [heads, 2, G])
        carg = m.sb(tag + "carg", [HALF, 2, 2, heads])
        turn = m.ps(tag + "turn", [P, 4, 512])
        small = m.ps(tag + "small", [P, 512])
        small2 = m.ps(tag + "small2", [P, 512])

        @block.tensor
        def _(pe):
            for n, (h, q) in enumerate(pairs):
                if n >= 4:
                    pe.wait_ge(kept, n - 3)
                for j in range(step):
                    for k in range(K2):
                        last = pe.transpose(turn[0:HALF, n % 4, j * BLK + k * P:j * BLK + (k + 1) * P],
                                            scores[:, k, h * HALF:(h + 1) * HALF, q + j], c.ident[:])
                last.then_inc(turned, 1)
            pe.wait_ge(ends, 1)
            for d in range(2):
                for h in range(2):
                    last = pe.transpose(small[0:heads, d * G + h * HALF:d * G + (h + 1) * HALF], tip[:, h, d, :],
                                        c.ident[0:HALF, 0:HALF])
            last.then_inc(ends_turned, 1)
            pe.wait_ge(carried, 2)
            for h in range(2):
                for d in range(2):
                    last = pe.transpose(small2[0:HALF, (h * 2 + d) * heads:(h * 2 + d + 1) * heads],
                                        car[:, d, h * HALF:(h + 1) * HALF], c.ident[0:heads, 0:heads])
            last.then_inc(carry_turned, 1)
            pe.wait_ge(kept, len(pairs))
            for n, (h, q) in enumerate(pairs):
                pe.wait_ge(exped, h + 1)
                if n >= 4:
                    pe.wait_ge(back_kept, n - 3)
                for j in range(step):
                    for k in range(K2):
                        last = pe.transpose(turn[:, n % 4, (j * K2 + k) * P:(j * K2 + k) * P + HALF],
                                            s[:, h, q + j, k * P:(k + 1) * P], c.ident[0:HALF, 0:HALF])
                last.then_inc(back_turned, 1)

        @block.scalar
        def _(act):
            for n, (h, q) in enumerate(pairs):
                act.wait_ge(turned, n + 1)
                act.copy(s[:, h, q:q + step, :], turn[0:HALF, n % 4, :].rearrange("p (j e) -> p j e", j=step)).then_inc(kept, 1)
            for h in range(2):
                act.wait_ge(shifted, h + 1)
                act.activation(s[:, h], s[:, h], ACT.Exp, scale=-1.0).then_inc(exped, 1)
            for n, (h, q) in enumerate(pairs):
                act.wait_ge(back_turned, n + 1)
                src = turn[:, n % 4, :].rearrange("p (j k g) -> p j k g", j=step, k=K2)
                for j in range(step):
                    last = act.copy(scores[:, :, h * HALF:(h + 1) * HALF, q + j], src[:, j, :, 0:HALF])
                last.then_inc(back_kept, 1)

        @block.vector
        def _(dve):
            per = len(pairs) // 2
            for h in range(2):
                for q in range(heads):
                    dve.wait_ge(kept, h * per + q // step + 1)
                    dve.tensor_tensor_scan(fwd[:, h, q, :], e.step[:, h, :], s[:, h, q, :], 0.0, ALU.add, ALU.max).then_inc(scanned, 1)
            for h in range(2):
                for q in range(heads):
                    dve.wait_ge(scanned, h * heads + q + 1)
                    dve.tensor_tensor_scan(top[:, h, q, ::-1], e.back[:, h, ::-1], fwd[:, h, q, ::-1], 0.0,
                                           ALU.add, ALU.max).then_inc(scanned, 1)
            dve.wait_ge(scanned, 4 * heads)
            for h in range(2):
                dve.tensor_copy(tip[:, h, 0, :], fwd[:, h, :, BLK - 1])
                last = dve.tensor_copy(tip[:, h, 1, :], top[:, h, :, 0])
            last.then_inc(ends, 1)
            dve.wait_ge(ends_turned, 1)
            dve.tensor_copy(tips[:], small[0:heads, 0:2 * G].rearrange("p (d g) -> p d g", d=2)).then_inc(rows_kept, 1)
            dve.wait_ge(rows_kept, 1)
            dve.tensor_tensor(inc[:, 0, 1:G], tips[:, 0, 0:G - 1], e.cont[0:heads, 1:G], ALU.add)
            dve.tensor_tensor(inc[:, 1, 1:G], tips[:, 1, 1:G], e.cont[0:heads, 1:G], ALU.add)
            dve.memset(car[:, 0, 0:1], NEG)
            dve.memset(car[:, 1, G - 1:G], NEG).then_inc(rows_kept, 1)
            dve.wait_ge(rows_kept, 2)
            dve.tensor_tensor_scan(car[:, 0, 1:G], e.over_prev[0:heads, 1:G], inc[:, 0, 1:G], NEG, ALU.add, ALU.max).then_inc(carried, 1)
            dve.tensor_tensor_scan(car[:, 1, 0:G - 1][:, ::-1], e.over_this[0:heads, 1:G][:, ::-1], inc[:, 1, 1:G][:, ::-1],
                                   NEG, ALU.add, ALU.max).then_inc(carried, 1)
            dve.wait_ge(carry_turned, 1)
            dve.tensor_copy(carg[:], small2[0:HALF, 0:4 * heads].rearrange("p (h d q) -> p h d q", h=2, d=2)).then_inc(carry_kept, 1)
            dve.wait_ge(carry_kept, 1)
            for h in range(2):
                for q in range(heads):
                    dve.scalar_tensor_tensor(out=fwd[:, h, q, :], in0=e.first[:, h, :], scalar=carg[:, h, 0, q:q + 1],
                                             in1=top[:, h, q, :], op0=ALU.add, op1=ALU.max).then_inc(spread, 1)
                for q in range(heads):
                    dve.wait_ge(spread, 2 * heads * h + q + 1)
                    dve.scalar_tensor_tensor(out=top[:, h, q, :], in0=e.last[:, h, :], scalar=carg[:, h, 1, q:q + 1],
                                             in1=fwd[:, h, q, :], op0=ALU.add, op1=ALU.max).then_inc(spread, 1)
                dve.wait_ge(spread, 2 * heads * (h + 1))
                if heads == channels:
                    dve.scalar_tensor_tensor(out=s[:, h].rearrange("p q e -> p (q e)"), in0=top[:, h].rearrange("p q e -> p (q e)"),
                                             scalar=0.0, in1=s[:, h].rearrange("p q e -> p (q e)"),
                                             op0=ALU.max, op1=ALU.subtract).then_inc(shifted, 1)
                else:
                    dve.tensor_tensor(fwd[:, h, 0, :], top[:, h, 0, :], s[:, h, 1, :], ALU.max).then_inc(carry_kept, 1)
                    dve.wait_ge(carry_kept, h + 2)
                    dve.tensor_tensor(s[:, h], fwd[:, h, 0:1, :].broadcast_to([HALF, 2, BLK]), s[:, h], ALU.subtract).then_inc(shifted, 1)


def aggregate(nc, tag, c, e, index, table, heads, weights, extra, acc):
    wide = D + extra
    with Mem(nc) as m, stage(nc, "indexed", "hot", "weighted", "ones", "multiplied", "added", "zeroed", "begun",
                             *(f"gathered{u}" for u in range(U))) as (
            block, indexed, hot, weighted, ones_set, multiplied, added, zeroed, begun, *gathered):
        idx = m.sb(tag + "idx", [P, U, K2], I32)
        rows = m.sb(tag + "rows", [P, U, K2, D])
        one = m.sb(tag + "one", [P, 2, K2, P])
        msg = m.sb(tag + "msg", [P, 2, K2, wide]) if weights is not None else None
        part = m.ps(tag + "part", [P, 2, 512])

        @block.gpsimd
        def _(pool):
            with pool.Fori(0, G // U) as i:
                for u in range(U):
                    pool.wait_ge(indexed, i * U + u + 1)
                    pool.sem_inc(begun, 1)
                    for k in range(K2):
                        pool.indirect_dma_start(rows[:, u, k, :], None, table,
                                                bass.IndirectOffsetOnAxis(idx[:, u, k:k + 1], 0)).then_inc(gathered[u], 16)

        @block.scalar
        def _(act):
            act.wait_ge(zeroed, 1)
            with act.Fori(0, G // U) as i:
                for u in range(U):
                    g = i * U + u
                    act.wait_ge(added, g - U + 1 + CREDIT)
                    act.copy(idx[:, u, :], index[:, :, bass.ts(g, 1)].squeeze(2)).then_inc(indexed, 1)

        @block.tensor
        def _(pe):
            pe.sem_inc(multiplied, CREDIT)
            with pe.Fori(0, G // U) as i:
                for u in range(U):
                    g = i * U + u
                    pe.wait_ge(hot, g + 1)
                    if weights is None:
                        pe.wait_ge(gathered[u], (i + 1) * 16 * K2)
                    else:
                        pe.wait_ge(weighted, g + 1)
                    pe.wait_ge(added, g - before(u, 2) + 1 + CREDIT)
                    for k in range(K2):
                        rhs = rows[:, u, k, :] if weights is None else msg[:, u % 2, k, :]
                        last = pe.matmul(part[:, u % 2, 0:wide], one[:, u % 2, k, :], rhs, start=(k == 0), stop=(k == K2 - 1))
                    last.then_inc(multiplied, 1)

        @block.vector
        def _(dve):
            if weights is not None:
                dve.memset(msg[:], 1.0)
            dve.memset(acc[:], 0.0).then_inc(zeroed, 1)
            dve.wait_ge(zeroed, 1)
            dve.sem_inc(added, CREDIT)

            def prepare(i, u):
                g = i * U + u
                dve.wait_ge(multiplied, g - before(u, 2) + 1 + CREDIT)
                for k in range(K2):
                    last = dve.tensor_scalar(one[:, u % 2, k, :], c.iota[:], e.local[:, k, bass.ts(g, 1)], None, ALU.is_equal)
                last.then_inc(hot, 1)
                if weights is None:
                    return
                dve.wait_ge(gathered[u], (i + 1) * 16 * K2)
                n = weights.shape[3]
                dve.tensor_copy(msg[:, u % 2, :, D:D + n], weights[:, :, g, :])
                for k in range(K2):
                    if heads == 1:
                        last = dve.tensor_scalar(msg[:, u % 2, k, 0:D], rows[:, u, k, :], weights[:, k, g, 0:1], None, ALU.mult)
                    else:
                        last = dve.tensor_tensor(
                            msg[:, u % 2, k, 0:D].rearrange("p (h d) -> p h d", h=heads),
                            rows[:, u, k, :].rearrange("p (h d) -> p h d", h=heads),
                            weights[:, k, g, :].unsqueeze(2).broadcast_to([P, heads, D // heads]), ALU.mult)
                last.then_inc(weighted, 1)

            with dve.Fori(0, G // U) as i:
                for u in range(U):
                    g = i * U + u
                    if u == 0:
                        prepare(i, 0)
                    if u + 1 < U:
                        prepare(i, u + 1)
                    tile = dve.value_load(e.tile[0:1, bass.ts(g, 1)], min_val=0, max_val=NT)
                    dve.wait_ge(multiplied, g + 1 + CREDIT)
                    dve.wait_ge(added, g + CREDIT)
                    dve.tensor_tensor(acc[:, tile, :], acc[:, tile, :], part[:, u % 2, 0:wide], ALU.add).then_inc(added, 1)


def finish_attention0(nc, acc, x, degree):
    with Mem(nc) as m, stage(nc, "chain") as (block, chain):
        den = m.sb("f0_den", [P, NT, H0])
        inv = m.sb("f0_inv", [P, NT, H0])

        @block.vector
        def _(dve):
            dve.tensor_copy(degree[:], acc[:, 0:NT, D + H0])
            dve.tensor_scalar(den[:], acc[:, 0:NT, D:D + H0], 1e-12, None, ALU.add).then_inc(chain, 1)
            dve.wait_ge(chain, 1)
            dve.reciprocal(inv[:], den[:]).then_inc(chain, 1)
            dve.wait_ge(chain, 2)
            v = acc[:, 0:NT, 0:D].rearrange("p t (h d) -> p t h d", h=H0)
            dve.tensor_tensor(v, v, inv[:].unsqueeze(3).broadcast_to([P, NT, H0, D0]), ALU.mult).then_inc(chain, 1)
            dve.wait_ge(chain, 3)
            dve.tensor_tensor(x[:], x[:], acc[:, 0:NT, 0:D], ALU.add)


def project(nc, tag, c, xnt, w, width, out, bias=None, masked=0):
    with Mem(nc) as m, stage(nc, "staged", "multiplied", "kept", "biased") as (block, staged, multiplied, kept, biased):
        slot = m.sb(tag + "slot", [P, 2, DC, P])
        acc = m.ps(tag + "acc", [P, 2, 512])

        @block.gpsimd
        def _(pool):
            with pool.Fori(0, NT // U) as i:
                for u in range(U):
                    t = i * U + u
                    pool.wait_ge(multiplied, t - before(u, 2) + 1 + CREDIT)
                    pool.tensor_copy(slot[:, u % 2], xnt[:, :, bass.ts(t, P)]).then_inc(staged, 1)

        @block.tensor
        def _(pe):
            pe.sem_inc(multiplied, CREDIT)
            with pe.Fori(0, NT // U) as i:
                for u in range(U):
                    t = i * U + u
                    pe.wait_ge(staged, t + 1)
                    pe.wait_ge(kept, t - before(u, 2) + 1 + CREDIT)
                    for k in range(DC):
                        last = pe.matmul(acc[:, u % 2, 0:width], slot[:, u % 2, k, :], w[:, k, :], start=(k == 0),
                                         stop=(k == DC - 1 and bias is None))
                    if bias is not None:
                        last = pe.matmul(acc[:, u % 2, 0:width], c.ones[0:1, :], bias[:], start=False, stop=True)
                    last.then_inc(multiplied, 1)

        @block.vector
        def _(dve):
            dve.sem_inc(kept, CREDIT)
            with dve.Fori(0, NT // U) as i:
                for u in range(U):
                    t = i * U + u
                    dve.wait_ge(multiplied, t + 1 + CREDIT)
                    if masked:
                        last = dve.tensor_scalar(out[:, t, 0:masked], acc[:, u % 2, 0:masked], c.valid[:, bass.ts(t, 1)], None, ALU.mult)
                    if masked < width:
                        last = dve.tensor_copy(out[:, t, masked:width], acc[:, u % 2, masked:width])
                    last.then_inc(kept, 1)


NX = 8
TOP_BIG = 1.0e6


def route(nc, c, logits, one, best):
    with Mem(nc) as m, stage(nc, "chain", "exped") as (block, chain, exped):
        top = m.sb("r_top", [P, NT])
        total = m.sb("r_total", [P, NT])
        inv = m.sb("r_inv", [P, NT])
        rw = m.sb("r_rw", [P, NT, NX])
        same = m.sb("r_same", [P, NT, NX])
        place = m.sb("r_place", [P, NT, NX])
        first = m.sb("r_first", [P, NT])

        def wide(v):
            return v.unsqueeze(2).broadcast_to([P, NT, NX])

        numbers = c.iota[:, 0:NX].unsqueeze(1).broadcast_to([P, NT, NX])

        @block.scalar
        def _(act):
            act.wait_ge(chain, 2)
            act.activation(logits[:], logits[:], ACT.Exp).then_inc(exped, 1)

        @block.vector
        def _(dve):
            done = [0]

            def link(ins):
                done[0] += 1
                ins.then_inc(chain, 1)
                dve.wait_ge(chain, done[0])

            link(dve.tensor_reduce(top[:], logits[:], AX.X, ALU.max))
            link(dve.tensor_tensor(logits[:], logits[:], wide(top[:]), ALU.subtract))
            dve.wait_ge(exped, 1)
            link(dve.tensor_reduce(total[:], logits[:], AX.X, ALU.add))
            link(dve.reciprocal(inv[:], total[:]))
            link(dve.tensor_tensor(rw[:], logits[:], wide(inv[:]), ALU.mult))
            for n in range(2):
                link(dve.tensor_reduce(best[:, n], rw[:], AX.X, ALU.max))
                link(dve.tensor_tensor(same[:], rw[:], wide(best[:, n]), ALU.is_equal))
                link(dve.scalar_tensor_tensor(out=place[:], in0=same[:], scalar=-TOP_BIG, in1=numbers, op0=ALU.mult, op1=ALU.add))
                link(dve.tensor_reduce(first[:], place[:], AX.X, ALU.min))
                link(dve.tensor_scalar(first[:], first[:], TOP_BIG, None, ALU.add))
                link(dve.tensor_tensor(one[:, n], wide(first[:]), numbers, ALU.is_equal))
                if n == 0:
                    link(dve.scalar_tensor_tensor(out=rw[:], in0=one[:, 0], scalar=-4.0, in1=rw[:], op0=ALU.mult, op1=ALU.add))
            link(dve.tensor_tensor(total[:], best[:, 0], best[:, 1], ALU.add))
            link(dve.reciprocal(inv[:], total[:]))
            dve.tensor_tensor(best[:], best[:], inv[:].unsqueeze(1).broadcast_to([P, 2, NT]), ALU.mult)


GM = 256
NG = 2 * N // GM + NX
NSLOT = NG * GM
assert NG % 2 == 0


def place_tokens(nc, c, one, slots, expert):
    with Mem(nc) as m, stage(nc, "chain", "summed") as (block, chain, summed):
        tri = m.sb("pl_tri", [P, P])
        cnt = m.sb("pl_cnt", [P, NT, NX])
        keep = m.sb("pl_keep", [P, NX, NT])
        tot = m.sb("pl_tot", [P, NX, NT])
        cum = m.sb("pl_cum", [P, NX, NT])
        ng1, ng2, cumg, base, gid = (m.sb("pl_" + n, [P, NG]) for n in ("ng1", "ng2", "cumg", "base", "gid"))
        ngi = m.sb("pl_ngi", [P, NX], I32)
        pos = m.sb("pl_pos", [P, NX, NT])
        mine = m.sb("pl_mine", [P, 2, NT, NX])
        row = m.sb("pl_row", [P, 2, NT])
        spare = m.sb("pl_spare", [P, 2, NT])
        less = m.sb("pl_less", [P, NG, NX])
        ps = m.ps("pl_ps", [P, 2, 512])

        @block.tensor
        def _(pe):
            pe.wait_ge(chain, 3)
            flat = cnt[:].rearrange("p t e -> p (t e)")
            pe.matmul(ps[:, 0, 0:NT * NX], tri[:], flat, start=True, stop=True)
            pe.matmul(ps[:, 1, 0:NT * NX], c.ones[:], flat, start=True, stop=True).then_inc(summed, 1)

        @block.vector
        def _(dve):
            done = [0]

            def link(ins):
                done[0] += 1
                ins.then_inc(chain, 1)
                dve.wait_ge(chain, done[0])

            link(dve.tensor_scalar(tri[:], c.iota[:], c.part[:, 0:1], None, ALU.is_gt))
            link(dve.tensor_tensor(cnt[:], one[:, 0], one[:, 1], ALU.add))
            link(dve.tensor_tensor(cnt[:], cnt[:], c.valid[:].unsqueeze(2).broadcast_to([P, NT, NX]), ALU.mult))
            link(dve.memset(keep[:], 1.0))
            link(dve.memset(keep[:, :, 0:1], 0.0))
            dve.wait_ge(summed, 1)
            link(dve.tensor_copy(tot[:], ps[:, 1, 0:NT * NX].rearrange("p (t e) -> p e t", e=NX)))
            link(dve.tensor_tensor_scan(cum[:].rearrange("p e t -> p (e t)"), keep[:].rearrange("p e t -> p (e t)"),
                                        tot[:].rearrange("p e t -> p (e t)"), 0.0, ALU.mult, ALU.add))
            link(dve.tensor_scalar(ng1[:, 0:NX], cum[:, :, NT - 1], float(GM - 1), None, ALU.add))
            link(dve.tensor_copy(ngi[:], ng1[:, 0:NX]))
            link(dve.tensor_scalar(ngi[:], ngi[:], GM.bit_length() - 1, None, ALU.arith_shift_right))
            link(dve.tensor_copy(ng2[:, 0:NX], ngi[:]))
            link(dve.tensor_tensor_scan(cumg[:, 0:NX], c.ones[:, 0:NX], ng2[:, 0:NX], 0.0, ALU.mult, ALU.add))
            link(dve.tensor_tensor(base[:, 0:NX], cumg[:, 0:NX], ng2[:, 0:NX], ALU.subtract))
            link(dve.tensor_scalar(base[:, 0:NX], base[:, 0:NX], float(GM), None, ALU.mult))
            link(dve.tensor_tensor(pos[:], cum[:], tot[:], ALU.subtract))
            link(dve.tensor_tensor(pos[:], pos[:], base[:, 0:NX].unsqueeze(2).broadcast_to([P, NX, NT]), ALU.add))
            link(dve.tensor_tensor(pos[:], pos[:], ps[:, 0, 0:NT * NX].rearrange("p (t e) -> p e t", e=NX), ALU.add))
            for n in range(2):
                link(dve.tensor_tensor(mine[:, n], one[:, n], pos[:].rearrange("p e t -> p t e"), ALU.mult))
            link(dve.tensor_reduce(row[:], mine[:], AX.X, ALU.add))
            for n in range(2):
                link(dve.tensor_scalar(spare[:, n], c.token[:], float(NSLOT - N + n * P), None, ALU.add))
                link(dve.tensor_tensor(row[:, n], row[:, n], spare[:, n], ALU.subtract))
                link(dve.tensor_tensor(row[:, n], row[:, n], c.valid[:], ALU.mult))
                link(dve.tensor_tensor(row[:, n], row[:, n], spare[:, n], ALU.add))
            link(dve.tensor_copy(slots[:], row[:]))
            link(dve.tensor_tensor(less[:], cumg[:, 0:NX].unsqueeze(1).broadcast_to([P, NG, NX]),
                                   c.iota[:, 0:NG].unsqueeze(2).broadcast_to([P, NG, NX]), ALU.is_le))
            link(dve.tensor_reduce(gid[:], less[:], AX.X, ALU.add))
            dve.tensor_scalar(expert[:], gid[:], float(NX - 1), None, ALU.min)


def zero_rows(nc, rows, out_rows):
    with Mem(nc) as m, stage(nc, "zeroed", "stored") as (block, zeroed, stored):
        z = m.sb("z_z", [P, 8, D])

        @block.vector
        def _(dve):
            dve.memset(z[:], 0.0).then_inc(zeroed, 1)

        @block.sync
        def _(sp):
            sp.wait_ge(zeroed, 1)
            for q in range(NSLOT // (8 * P)):
                sp.dma_start(rows[q * 8 * P:(q + 1) * 8 * P].rearrange("(k p) d -> p k d", p=P), z[:]).then_inc(stored, 16)
            sp.dma_start(out_rows[NSLOT:].rearrange("(k p) d -> p k d", p=P), z[:, 0:2]).then_inc(stored, 16)
            sp.wait_ge(stored, 16 * (NSLOT // (8 * P) + 1))


def scatter_tokens(pool, xn, slots, rows, scattered):
    for n in range(2):
        for t in range(NT):
            pool.indirect_dma_start(rows, bass.IndirectOffsetOnAxis(slots[:, n, t:t + 1], 0), xn[:, t, :], None).then_inc(scattered, 16)
    pool.wait_ge(scattered, 16 * 2 * NT)


def run_experts(nc, c, rows, out_rows, expert, w1p, b1p, w2p, b2p, hidden):
    fb = hidden // P
    gt = GM // P
    with Mem(nc) as m, stage(nc, "loaded0", "loaded1", "turned", "kept", "up", "shaped", "down", "out0", "out1",
                             "stored0", "stored1") as (
            block, loaded0, loaded1, turned, kept, up, shaped, down, out0, out1, stored0, stored1):
        loaded, out_made, stored = (loaded0, loaded1), (out0, out1), (stored0, stored1)
        w1 = m.sb("x_w1", [P, 2, DC, hidden])
        w2 = m.sb("x_w2", [P, 2, fb, D])
        b1 = m.sb("x_b1", [P, 2, fb])
        b2 = m.sb("x_b2", [P, 2, D])
        xr = m.sb("x_xr", [P, 2, gt, D])
        xt = m.sb("x_xt", [P, DC, GM])
        hid = m.sb("x_hid", [P, fb, GM])
        y = m.sb("x_y", [P, 2, gt, D])
        turn = m.ps("x_turn", [P, DC, GM])
        up_ps = m.ps("x_up", [P, 3, 512])
        down_ps = m.ps("x_down", [P, gt, 512])

        @block.sync
        def _(sp):
            def load(b, g):
                e = sp.value_load(expert[0:1, bass.ds(g, 1)], min_val=0, max_val=NX - 1)
                sp.dma_start(xr[:, b], rows[bass.ds(g * GM, GM)].rearrange("(k p) d -> p k d", p=P)).then_inc(loaded[b], 16)
                sp.dma_start(w1[:, b], w1p[e].rearrange("(k p) f -> p k f", p=P)).then_inc(loaded[b], 16)
                sp.dma_start(b1[:, b], b1p[e].rearrange("(k p) -> p k", p=P), allow_slow_non_contiguous=True).then_inc(loaded[b], 16)
                sp.dma_start(w2[:, b], w2p[e].rearrange("(k p) f -> p k f", p=P)).then_inc(loaded[b], 16)
                sp.dma_start(b2[:, b], b2p[e].rearrange("(a d) -> a d", a=1).broadcast_to([P, D])).then_inc(loaded[b], 16)

            def save(b, g, i):
                sp.wait_ge(out_made[b], i + 1 + b)
                sp.dma_start(out_rows[bass.ds(g * GM, GM)].rearrange("(k p) d -> p k d", p=P), y[:, b]).then_inc(stored[b], 16)

            for b in range(2):
                sp.sem_inc(stored[b], 16)
                load(b, b)
            with sp.Fori(0, NG // 2 - 1) as i:
                for b in range(2):
                    save(b, i * 2 + b, i)
                    load(b, i * 2 + 2 + b)
            for b in range(2):
                save(b, NG - 2 + b, NG // 2 - 1)
            for b in range(2):
                sp.wait_ge(stored[b], 16 * (NG // 2 + 1))

        @block.tensor
        def _(pe):
            with pe.Fori(0, NG // 2) as i:
                for b in range(2):
                    g = i * 2 + b
                    pe.wait_ge(loaded[b], (i + 1) * 80)
                    pe.wait_ge(kept, g + 1)
                    for k in range(DC):
                        for j in range(gt):
                            last = pe.transpose(turn[:, k, j * P:(j + 1) * P], xr[:, b, j, k * P:(k + 1) * P], c.ident[:])
                    last.then_inc(turned, 1)
                    pe.wait_ge(kept, g + 2)
                    for f in range(fb):
                        pe.wait_ge(shaped, g * fb + f + 1 - before(f, 3, fb) + CREDIT)
                        for k in range(DC):
                            last = pe.matmul(up_ps[:, f % 3, 0:GM], w1[:, b, k, f * P:(f + 1) * P], xt[:, k, :], start=(k == 0), stop=(k == DC - 1))
                        last.then_inc(up, 1)
                    pe.wait_ge(shaped, (g + 1) * fb + CREDIT)
                    for j in range(gt):
                        pe.wait_ge(out_made[1 - b], i + 1)
                        for f in range(fb):
                            last = pe.matmul(down_ps[:, j, 0:D], hid[:, f, j * P:(j + 1) * P], w2[:, b, f, :], start=(f == 0), stop=(f == fb - 1))
                        last.then_inc(down, 1)

        @block.scalar
        def _(act):
            act.sem_inc(kept, 1)
            act.sem_inc(shaped, CREDIT)
            with act.Fori(0, NG // 2) as i:
                for b in range(2):
                    g = i * 2 + b
                    act.wait_ge(turned, g + 1)
                    act.copy(xt[:], turn[:]).then_inc(kept, 1)
                    for f in range(fb):
                        act.wait_ge(up, g * fb + f + 1)
                        act.activation(hid[:, f, :], up_ps[:, f % 3, 0:GM], ACT.Gelu, bias=b1[:, b, f:f + 1]).then_inc(shaped, 1)

        @block.vector
        def _(dve):
            dve.sem_inc(out_made[1], 1)
            with dve.Fori(0, NG // 2) as i:
                for b in range(2):
                    g = i * 2 + b
                    dve.wait_ge(stored[b], (i + 1) * 16)
                    for j in range(gt):
                        dve.wait_ge(down, g * gt + j + 1)
                        last = dve.tensor_tensor(y[:, b, j, :], down_ps[:, j, 0:D], b2[:, b, :], ALU.add)
                    last.then_inc(out_made[b], 1)


def gather_experts(nc, x, slots, best, out_rows):
    depth = 4
    with Mem(nc) as m, stage(nc, "added", *(f"got{s}" for s in range(depth))) as (block, added, *got):
        y = m.sb("y_y", [P, depth, 2, D])

        @block.gpsimd
        def _(pool):
            for t in range(NT):
                if t >= depth:
                    pool.wait_ge(added, 2 * (t - depth + 1))
                for n in range(2):
                    pool.indirect_dma_start(y[:, t % depth, n, :], None, out_rows,
                                            bass.IndirectOffsetOnAxis(slots[:, n, t:t + 1], 0)).then_inc(got[t % depth], 16)

        @block.vector
        def _(dve):
            for t in range(NT):
                dve.wait_ge(got[t % depth], 32 * (t // depth + 1))
                for n in range(2):
                    if n:
                        dve.wait_ge(added, 2 * t + 1)
                    dve.scalar_tensor_tensor(out=x[:, t, :], in0=y[:, t % depth, n, :], scalar=best[:, n, t:t + 1],
                                             in1=x[:, t, :], op0=ALU.mult, op1=ALU.add).then_inc(added, 1)


def mlp(nc, tag, c, xnt, x, act_func, hidden, weights, gate=None, scatter=None):
    fb = hidden // P
    chunk = U * P
    half = chunk // 2
    with Mem(nc) as m, stage(nc, "loaded", "up", "shaped", "down", "added", "biased", "scattered") as (
            block, loaded, up, shaped, down, added, biased, scattered):
        w1 = m.sb(tag + "w1", [P, DC, hidden])
        w2 = m.sb(tag + "w2", [P, fb, D])
        b1 = m.sb(tag + "b1", [P, fb])
        b2 = m.sb(tag + "b2", [P, D])
        hid = m.sb(tag + "hid", [P, fb, chunk])
        up_ps = m.ps(tag + "up", [P, 2, 2, 512])
        down_ps = m.ps(tag + "down", [P, 2, 512])

        @block.gpsimd
        def _(pool):
            if scatter is not None:
                scatter_tokens(pool, *scatter, scattered)

        @block.sync
        def _(sp):
            a1, c1, a2, c2 = weights
            sp.dma_start(w1[:], a1.rearrange("(k p) f -> p k f", p=P)).then_inc(loaded, 16)
            sp.dma_start(b1[:], columns_of(c1), allow_slow_non_contiguous=True).then_inc(loaded, 16)
            sp.dma_start(w2[:], a2.rearrange("(k p) f -> p k f", p=P)).then_inc(loaded, 16)
            sp.dma_start(b2[:], row_of(c2).broadcast_to([P, D])).then_inc(loaded, 16)

        @block.tensor
        def _(pe):
            pe.wait_ge(loaded, 64)
            with pe.Fori(0, NT // U) as j:
                for f in range(fb):
                    pe.wait_ge(shaped, j * fb + f - 2 + 1 + CREDIT)
                    for n in range(2):
                        for k in range(DC):
                            last = pe.matmul(up_ps[:, f % 2, n, 0:half], w1[:, k, f * P:(f + 1) * P],
                                             xnt[:, k, bass.ds(j * chunk + n * half, half)], start=(k == 0), stop=(k == DC - 1))
                    last.then_inc(up, 1)
                pe.wait_ge(shaped, (j + 1) * fb + CREDIT)
                for u in range(U):
                    pe.wait_ge(added, j * U + u - before(u, 2) + 1 + CREDIT)
                    for f in range(fb):
                        last = pe.matmul(down_ps[:, u % 2, 0:D], hid[:, f, u * P:(u + 1) * P], w2[:, f, :],
                                         start=(f == 0), stop=(f == fb - 1))
                    last.then_inc(down, 1)

        @block.scalar
        def _(act):
            act.sem_inc(shaped, CREDIT)
            with act.Fori(0, NT // U) as j:
                for f in range(fb):
                    act.wait_ge(up, j * fb + f + 1)
                    act.activation(hid[:, f, :].rearrange("p (n t) -> p n t", n=2), up_ps[:, f % 2, :, 0:half],
                                   act_func, bias=b1[:, f:f + 1]).then_inc(shaped, 1)

        @block.vector
        def _(dve):
            dve.sem_inc(added, CREDIT)
            dve.wait_ge(loaded, 64)
            with dve.Fori(0, NT // U) as j:
                for u in range(U):
                    t = j * U + u
                    weight = 1.0 if gate is None else gate[:, t, 0:1]
                    dve.scalar_tensor_tensor(out=x[:, t, :], in0=b2[:], scalar=weight,
                                             in1=x[:, t, :], op0=ALU.mult, op1=ALU.add).then_inc(biased, 1)
                    dve.wait_ge(biased, t + 1)
                    dve.wait_ge(down, t + 1)
                    dve.scalar_tensor_tensor(out=x[:, t, :], in0=down_ps[:, u % 2, 0:D], scalar=weight,
                                             in1=x[:, t, :], op0=ALU.mult, op1=ALU.add).then_inc(added, 1)


def load(nc, *pairs):
    with stage(nc, "loaded") as (block, loaded):
        @block.sync
        def _(sp):
            for dst, src in pairs:
                sp.dma_start(dst, src, allow_slow_non_contiguous=True).then_inc(loaded, 16)
            sp.wait_ge(loaded, 16 * len(pairs))


def row_of(v):
    return v.rearrange("(a d) -> a d", a=1)


def columns_of(v):
    return v.rearrange("(k p) -> p k", p=P)


def turn_tokens(nc, tag, c, x, xt):
    with Mem(nc) as m, stage(nc, "staged", "turned", "kept") as (block, staged, turned, kept):
        slot = m.sb(tag + "slot", [P, 2, D])
        turn = m.ps(tag + "turn", [P, 2, 512])

        @block.vector
        def _(dve):
            with dve.Fori(0, NT // U) as i:
                for u in range(U):
                    t = i * U + u
                    dve.wait_ge(turned, t - before(u, 2) + 1 + CREDIT)
                    dve.tensor_copy(slot[:, u % 2, :], x[:, t, :]).then_inc(staged, 1)

        @block.tensor
        def _(pe):
            pe.sem_inc(turned, CREDIT)
            with pe.Fori(0, NT // U) as i:
                for u in range(U):
                    t = i * U + u
                    pe.wait_ge(staged, t + 1)
                    pe.wait_ge(kept, t - before(u, 2) + 1 + CREDIT)
                    for k in range(DC):
                        last = pe.transpose(turn[:, u % 2, k * P:(k + 1) * P], slot[:, u % 2, k * P:(k + 1) * P], c.ident[:])
                    last.then_inc(turned, 1)

        @block.scalar
        def _(act):
            act.sem_inc(kept, CREDIT)
            with act.Fori(0, NT // U) as i:
                for u in range(U):
                    t = i * U + u
                    act.wait_ge(turned, t + 1 + CREDIT)
                    act.copy(xt[:, :, bass.ts(t, P)], turn[:, u % 2, 0:D].rearrange("p (k t) -> p k t", k=DC)).then_inc(kept, 1)


def source_table1(nc, h, degree, dinv, table):
    with Mem(nc) as m, stage(nc, "chain", "rooted", "stored") as (block, chain, rooted, stored):
        deg, root, r0, r1, r2, r3 = (m.sb("d_" + n, [P, NT]) for n in ("deg", "root", "r0", "r1", "r2", "r3"))

        @block.scalar
        def _(act):
            act.wait_ge(chain, 1)
            act.activation(root[:], deg[:], ACT.Sqrt).then_inc(rooted, 1)

        @block.vector
        def _(dve):
            dve.tensor_scalar(deg[:], degree[:], 1.0, None, ALU.add).then_inc(chain, 1)
            dve.wait_ge(rooted, 1)
            dve.reciprocal(r0[:], root[:]).then_inc(chain, 1)
            dve.wait_ge(chain, 2)
            dve.tensor_tensor(r1[:], r0[:], r0[:], ALU.mult).then_inc(chain, 1)
            dve.wait_ge(chain, 3)
            dve.tensor_tensor(r2[:], r1[:], deg[:], ALU.mult).then_inc(chain, 1)
            dve.wait_ge(chain, 4)
            dve.tensor_scalar(r3[:], r2[:], -0.5, 1.5, ALU.mult, ALU.add).then_inc(chain, 1)
            dve.wait_ge(chain, 5)
            dve.tensor_tensor(dinv[:], r0[:], r3[:], ALU.mult).then_inc(chain, 1)
            dve.wait_ge(chain, 6)
            dve.tensor_tensor(h[:], h[:], dinv[:].unsqueeze(2).broadcast_to([P, NT, D]), ALU.mult).then_inc(chain, 1)

        @block.sync
        def _(sp):
            sp.wait_ge(chain, 7)
            sp.dma_start(table.rearrange("(t p) d -> p t d", p=P), h[:]).then_inc(stored, 16)
            sp.wait_ge(stored, 16)


def finish_gcn(nc, acc, h, dinv, bias):
    with stage(nc, "chain") as (block, chain):
        @block.vector
        def _(dve):
            dve.tensor_tensor(h[:], h[:], acc[:, 0:NT, :], ALU.add).then_inc(chain, 1)
            dve.wait_ge(chain, 1)
            dve.tensor_tensor(h[:], h[:], dinv[:].unsqueeze(2).broadcast_to([P, NT, D]), ALU.mult).then_inc(chain, 1)
            dve.wait_ge(chain, 2)
            dve.tensor_tensor(h[:], h[:], bias[:].unsqueeze(1).broadcast_to([P, NT, D]), ALU.add).then_inc(chain, 1)
            dve.wait_ge(chain, 3)
            dve.tensor_scalar(h[:], h[:], 0.0, None, ALU.max)


def tables2(nc, h, att, tmp, target, source_scores, table):
    with Mem(nc) as m, stage(nc, "chain", "stored") as (block, chain, stored):
        sc = m.sb("t2_sc", [P, 2, NT])
        both = m.sb("t2_both", [P, NT])

        @block.vector
        def _(dve):
            dve.memset(target[:, NT, :], 0.0)
            for s in range(2):
                if s:
                    dve.wait_ge(chain, 2)
                dve.tensor_tensor(tmp[:, 0:NT, 0:D], h[:], att[:, s, :].unsqueeze(1).broadcast_to([P, NT, D]), ALU.mult).then_inc(chain, 1)
                dve.wait_ge(chain, 2 * s + 1)
                dve.tensor_reduce(sc[:, s, :], tmp[:, 0:NT, 0:D], AX.X, ALU.add).then_inc(chain, 1)
            dve.wait_ge(chain, 4)
            dve.tensor_copy(target[:, 0:NT, 0], sc[:, 1, :])
            dve.tensor_tensor(both[:], sc[:, 0, :], sc[:, 1, :], ALU.add).then_inc(chain, 1)
            dve.wait_ge(chain, 5)
            dve.scalar_tensor_tensor(out=target[:, 0:NT, 1], in0=both[:], scalar=SLOPE, in1=both[:], op0=ALU.mult, op1=ALU.max)

        @block.sync
        def _(sp):
            sp.dma_start(table.rearrange("(t p) d -> p t d", p=P), h[:]).then_inc(stored, 16)
            sp.wait_ge(chain, 4)
            sp.dma_start(source_scores.rearrange("(t p) a -> p (t a)", p=P), sc[:, 0, :], allow_slow_non_contiguous=True).then_inc(stored, 16)
            sp.wait_ge(stored, 32)


def finish_gat(nc, acc, h, degree, bias, x):
    with Mem(nc) as m, stage(nc, "chain") as (block, chain):
        some, n, inv_n, own, own2, own3, own4, den, den2, inv = (
            m.sb("fg_" + k, [P, NT]) for k in ("some", "n", "inv_n", "own", "own2", "own3", "own4", "den", "den2", "inv"))

        @block.vector
        def _(dve):
            done = [0]

            def link(ins):
                done[0] += 1
                ins.then_inc(chain, 1)
                dve.wait_ge(chain, done[0])

            def wide(v):
                return v[:].unsqueeze(2).broadcast_to([P, NT, D])

            link(dve.tensor_scalar(some[:], degree[:], 1.0, None, ALU.is_lt))
            link(dve.tensor_scalar(n[:], degree[:], 1.0, None, ALU.max))
            link(dve.reciprocal(inv_n[:], n[:]))
            link(dve.tensor_tensor(own[:], acc[:, 0:NT, D + 1], inv_n[:], ALU.mult))
            link(dve.tensor_tensor(own2[:], own[:], some[:], ALU.add))
            link(dve.tensor_tensor(den[:], acc[:, 0:NT, D], own2[:], ALU.add))
            link(dve.tensor_scalar(den2[:], den[:], 1e-16, None, ALU.add))
            link(dve.reciprocal(inv[:], den2[:]))
            link(dve.tensor_tensor(h[:], h[:], wide(own2), ALU.mult))
            link(dve.tensor_tensor(h[:], h[:], acc[:, 0:NT, 0:D], ALU.add))
            link(dve.tensor_tensor(h[:], h[:], wide(inv), ALU.mult))
            link(dve.tensor_tensor(h[:], h[:], bias[:].unsqueeze(1).broadcast_to([P, NT, D]), ALU.add))
            link(dve.scalar_tensor_tensor(out=x[:].rearrange("p t d -> p (t d)"), in0=h[:].rearrange("p t d -> p (t d)"), scalar=0.0,
                                          in1=x[:].rearrange("p t d -> p (t d)"), op0=ALU.max, op1=ALU.add))


H1, D1 = 4, 64


def channel_attention1(nc, c, kv, wq, bq, g, bias):
    with Mem(nc) as m, stage(nc, "dve_did", "pe_did", "exped") as (block, dve_did, pe_did, exped):
        wqt = m.sb("c_wqt", [P, DC, D])
        high = m.sb("c_high", [P, 1])
        highs = m.sb("c_highs", [P, P])
        own = m.sb("c_own", [P, P])
        off = m.sb("c_off", [P, P])
        att = m.sb("c_att", [P, DC, P])
        att2 = m.sb("c_att2", [P, DC, P])
        top = m.sb("c_top", [P, DC])
        total = m.sb("c_total", [P, DC])
        inv = m.sb("c_inv", [P, DC])
        attt = m.sb("c_attt", [P, DC, P])
        acc = m.ps("c_acc", [P, DC, 512])
        turn = m.ps("c_turn", [P, 512])
        turn2 = m.ps("c_turn2", [P, 512])
        gps = m.ps("c_g", [P, DC, D])
        bps = m.ps("c_b", [1, 512])

        @block.tensor
        def _(pe):
            for q in range(DC):
                for k in range(DC):
                    last = pe.transpose(turn[:, (q * DC + k) * P:(q * DC + k + 1) * P], wq[:, k, q * P:(q + 1) * P], c.ident[:])
            last.then_inc(pe_did, 1)
            for q in range(DC):
                for t in range(NT):
                    last = pe.matmul(acc[:, q, 0:P], kv[:, t, q * P:(q + 1) * P], kv[:, t, D + q * P:D + (q + 1) * P],
                                     start=(t == 0), stop=(t == NT - 1))
            last.then_inc(pe_did, 1)
            pe.wait_ge(dve_did, 6)
            for q in range(DC):
                last = pe.transpose(turn2[:, q * P:(q + 1) * P], att2[:, q, :], c.ident[:])
            last.then_inc(pe_did, 1)
            pe.wait_ge(dve_did, 7)
            for k in range(DC):
                for q in range(DC):
                    pe.matmul(gps[:, k, q * P:(q + 1) * P], wqt[:, q, k * P:(k + 1) * P], attt[:, q, :], start=True, stop=True)
            for q in range(DC):
                last = pe.matmul(bps[:, q * P:(q + 1) * P], bq[:, q:q + 1], attt[:, q, :], start=True, stop=True)
            last.then_inc(pe_did, 1)

        @block.scalar
        def _(act):
            act.wait_ge(dve_did, 4)
            act.activation(att[:], att[:], ACT.Exp).then_inc(exped, 1)

        @block.vector
        def _(dve):
            dve.tensor_scalar(high[:], c.part[:], float(D1), None, ALU.is_ge)
            dve.tensor_scalar(highs[:], c.iota[:], float(D1), None, ALU.is_ge).then_inc(dve_did, 1)
            dve.wait_ge(dve_did, 1)
            dve.tensor_scalar(own[:], highs[:], high[:, 0:1], None, ALU.is_equal).then_inc(dve_did, 1)
            dve.wait_ge(dve_did, 2)
            dve.tensor_scalar(off[:], own[:], -1.0, -NEG, ALU.add, ALU.mult)
            dve.wait_ge(pe_did, 1)
            dve.tensor_copy(wqt[:], turn[:].rearrange("p (q f) -> p q f", q=DC)).then_inc(dve_did, 1)
            dve.wait_ge(pe_did, 2)
            dve.wait_ge(dve_did, 3)
            for q in range(DC):
                last = dve.scalar_tensor_tensor(out=att[:, q, :], in0=acc[:, q, 0:P], scalar=D1 ** -0.5, in1=off[:], op0=ALU.mult, op1=ALU.add)
            last.then_inc(exped, 1)
            dve.wait_ge(exped, 1)
            dve.tensor_reduce(top[:], att[:], AX.X, ALU.max).then_inc(exped, 1)
            dve.wait_ge(exped, 2)
            dve.tensor_tensor(att[:], att[:], top[:].unsqueeze(2).broadcast_to([P, DC, P]), ALU.subtract).then_inc(dve_did, 1)
            dve.wait_ge(exped, 3)
            dve.tensor_reduce(total[:], att[:], AX.X, ALU.add).then_inc(exped, 1)
            dve.wait_ge(exped, 4)
            dve.reciprocal(inv[:], total[:]).then_inc(dve_did, 1)
            dve.wait_ge(dve_did, 5)
            dve.tensor_tensor(att2[:], att[:], inv[:].unsqueeze(2).broadcast_to([P, DC, P]), ALU.mult).then_inc(dve_did, 1)
            dve.wait_ge(pe_did, 3)
            dve.tensor_copy(attt[:], turn2[:, 0:DC * P].rearrange("p (q d) -> p q d", q=DC)).then_inc(dve_did, 1)
            dve.wait_ge(pe_did, 4)
            dve.tensor_copy(g[:], gps[:])
            dve.tensor_copy(bias[:], bps[:, 0:D])


TAKEN = max(1, N // 2) - 1


def select_top(nc, c, w, weights_row, gate):
    with Mem(nc) as m, stage(nc, "chain", "stored", "loaded", "counted", "turned") as (
            block, chain, stored, loaded, counted, turned):
        wide = m.sb("k_wide", [P, NP])
        above = m.sb("k_above", [P, NP])
        clean, cnt, low, cand, ind, scan, excl, pos, pos2, early, less, tie, sel = (
            m.sb("k_" + n, [P, NT]) for n in ("clean", "cnt", "low", "cand", "ind", "scan", "excl", "pos", "pos2", "early", "less", "tie", "sel"))
        best = m.sb("k_best", [P, 1])
        edge1 = m.sb("k_edge1", [1, 1])
        edge = m.sb("k_edge", [P, 1])
        quota = m.sb("k_quota", [P, 1])
        tri = m.sb("k_tri", [P, P])
        tp = m.ps("k_tp", [P, 512])
        bp = m.ps("k_bp", [P, 512])
        pp = m.ps("k_pp", [P, 2, 512])

        @block.sync
        def _(sp):
            sp.wait_ge(chain, 2)
            sp.dma_start(weights_row.rearrange("a (t p) -> p (a t)", p=P), clean[:], allow_slow_non_contiguous=True).then_inc(stored, 16)
            sp.wait_ge(stored, 16)
            sp.dma_start(wide[:], weights_row.broadcast_to([P, NP])).then_inc(loaded, 16)

        @block.tensor
        def _(pe):
            pe.wait_ge(chain, 5)
            pe.transpose(tp[0:1, 0:P], best[:], c.ident[:]).then_inc(turned, 1)
            pe.wait_ge(chain, 6)
            pe.matmul(bp[:, 0:1], c.ones[0:1, :], edge1[:], start=True, stop=True).then_inc(turned, 1)
            pe.wait_ge(chain, 10)
            pe.matmul(pp[:, 0, 0:NT], tri[:], ind[:], start=True, stop=True)
            pe.matmul(pp[:, 1, 0:NT], c.ones[:], ind[:], start=True, stop=True).then_inc(turned, 1)

        @block.vector
        def _(dve):
            done = [0]

            def link(ins):
                done[0] += 1
                ins.then_inc(chain, 1)
                dve.wait_ge(chain, done[0])

            link(dve.tensor_tensor(low[:], w, c.valid[:], ALU.mult))
            link(dve.tensor_tensor(clean[:], low[:], c.mask[:], ALU.add))
            dve.wait_ge(loaded, 16)
            with dve.Fori(0, NT // U) as i:
                for u in range(U):
                    t = i * U + u
                    dve.wait_ge(counted, t + 1)
                    dve.tensor_scalar(above[:], wide[:], clean[:, bass.ts(t, 1)], 0.0, ALU.is_gt, ALU.add,
                                      accum_out=cnt[:, bass.ts(t, 1)]).then_inc(counted, 1)
            dve.wait_ge(counted, NT + 1)
            link(dve.tensor_scalar(low[:], cnt[:], float(TAKEN), None, ALU.is_lt))
            link(dve.scalar_tensor_tensor(out=cand[:], in0=cnt[:], scalar=1.0, in1=low[:], op0=ALU.add, op1=ALU.mult))
            link(dve.tensor_reduce(best[:], cand[:], AX.X, ALU.max))
            dve.wait_ge(turned, 1)
            link(dve.tensor_reduce(edge1[:], tp[0:1, 0:P], AX.X, ALU.max))
            dve.wait_ge(turned, 2)
            link(dve.tensor_scalar(edge[:], bp[:, 0:1], -1.0, None, ALU.add))
            link(dve.tensor_scalar(quota[:], edge[:], -1.0, float(TAKEN), ALU.mult, ALU.add))
            link(dve.tensor_scalar(ind[:], cnt[:], edge[:, 0:1], None, ALU.is_equal))
            link(dve.tensor_scalar(tri[:], c.iota[:], c.part[:, 0:1], None, ALU.is_gt))
            dve.wait_ge(turned, 3)
            link(dve.tensor_tensor_scan(scan[:], c.ones[:, 0:NT], pp[:, 1, 0:NT], 0.0, ALU.mult, ALU.add))
            link(dve.tensor_tensor(excl[:], scan[:], pp[:, 1, 0:NT], ALU.subtract))
            link(dve.tensor_tensor(pos[:], excl[:], pp[:, 0, 0:NT], ALU.add))
            link(dve.tensor_scalar(early[:], pos[:], quota[:, 0:1], None, ALU.is_lt))
            link(dve.tensor_scalar(less[:], cnt[:], edge[:, 0:1], None, ALU.is_lt))
            link(dve.tensor_tensor(tie[:], early[:], ind[:], ALU.mult))
            link(dve.tensor_tensor(sel[:], tie[:], less[:], ALU.add))
            link(dve.tensor_tensor(gate[:], sel[:].unsqueeze(2), w.unsqueeze(2), ALU.mult))

        @block.scalar
        def _(act):
            act.sem_inc(counted, 1)


def add(nc, x, y):
    with stage(nc, "added") as (block, added):
        @block.vector
        def _(dve):
            dve.tensor_tensor(x[:], x[:], y[:], ALU.add)


def store(nc, x, out):
    with stage(nc, "stored") as (block, stored):
        @block.sync
        def _(sp):
            full = (NT - 1) * P
            sp.dma_start(out[0:full].rearrange("(t p) d -> p t d", p=P), x[:, 0:NT - 1, :]).then_inc(stored, 16)
            sp.dma_start(out[full:N], x[0:TAIL, NT - 1, :]).then_inc(stored, 16)
            sp.wait_ge(stored, 32)


def program(nc, a, out):
    packed = nc.dram_tensor("packed", [NB, BLK], I32).ap()
    tiles = nc.dram_tensor("tiles", [1, G], I32).ap()
    expert_in = nc.dram_tensor("expert_in", [NSLOT + 2 * P, D], F32).ap()
    expert_out = nc.dram_tensor("expert_out", [NSLOT + 2 * P, D], F32).ap()
    rows1 = nc.dram_tensor("rows1", [NP, D], F32).ap()
    rows2 = nc.dram_tensor("rows2", [NP, D], F32).ap()
    source_scores2 = nc.dram_tensor("source_scores2", [NP, 1], F32).ap()
    weights_row = nc.dram_tensor("weights_row", [1, NP], F32).ap()
    values = nc.dram_tensor("values0", [R0 * NP, D], F32).ap()
    source_scores = nc.dram_tensor("source_scores0", [R0 * NP, H0], F32).ap()
    with Mem(nc) as m:
        c = Consts(m)
        x = m.sb("x", [P, NT, D])
        xnt = m.sb("xnt", [P, DC, NP])
        e = Edges(m)
        degree = m.sb("degree", [P, NT])
        constants(nc, c, x, a["x"])
        zero_rows(nc, expert_in, expert_out)
        find_groups(nc, c, a, e, packed, tiles)
        layer_norm(nc, "ln0_", c, x, xnt)
        with Mem(nc) as m0:
            target = m0.sb("target0", [P, NT + 1, R0 * H0])
            with Mem(nc) as m1:
                cat = m1.sb("cat0", [P, DC, COLS0])
                keys = m1.sb("keys0", [P, NT, P])
                vals = m1.sb("vals0", [P, NT, P])
                g = m1.sb("g0", [P, DC, D])
                weights0(nc, c, a, cat)
                project0(nc, c, xnt, cat, values, source_scores, target, keys, vals)
                linear_attention0(nc, c, a, keys, vals, g)
                bo = m1.sb("bo0", [1, D])
                load(nc, (bo[:], row_of(a["L0_mix_b_out"])))
                add_product(nc, "mix0_", xnt, g, bo, c, x)
            with Mem(nc) as m1:
                scores = m1.sb("scores0", [P, K2, G, H0])
                acc = m1.sb("acc_0", [P, NT + 1, D + H0 + 1])
                edge_scores(nc, "es0_", c, e, e.value_row, source_scores, H0, target, True, scores)
                segment_softmax(nc, "sm0_", c, e, H0, H0, scores)
                aggregate(nc, "ag0_", c, e, e.value_row, values, H0, scores, H0 + 1, acc)
                finish_attention0(nc, acc, x, degree)
        with Mem(nc) as m0:
            wr = m0.sb("wr0", [P, DC, NX])
            logits = m0.sb("logits", [P, NT, NX])
            one = m0.sb("one", [P, 2, NT, NX])
            best = m0.sb("best", [P, 2, NT])
            slots = m0.sb("slots", [P, 2, NT], I32)
            expert = m0.sb("expert", [P, NG], I32)
            load(nc, (wr[:], a["L0_ffn_Wr"].rearrange("(k p) e -> p k e", p=P)))
            with Mem(nc) as m1:
                xn = m1.sb("xn0", [P, NT, D])
                layer_norm(nc, "ln1_", c, x, xnt, xn)
                project(nc, "rt_", c, xnt, wr, NX, logits)
                route(nc, c, logits, one, best)
                place_tokens(nc, c, one, slots, expert)
                mlp(nc, "ff0_", c, xnt, x, ACT.Gelu, 1024, tuple(a["L0_ffn_" + n] for n in ("W1s", "b1s", "W2s", "b2s")),
                    scatter=(xn, slots, expert_in))
            run_experts(nc, c, expert_in, expert_out, expert, *(a["L0_ffn_" + n] for n in ("W1p", "b1p", "W2p", "b2p")), 1024)
            gather_experts(nc, x, slots, best, expert_out)
        with Mem(nc) as m0:
            h = m0.sb("h1", [P, NT, D])
            dinv = m0.sb("dinv", [P, NT])
            with Mem(nc) as m1:
                xn = m1.sb("xn1", [P, NT, D])
                layer_norm(nc, "ln2_", c, x, xnt, xn)
                with Mem(nc) as m2:
                    w1 = m2.sb("gw1", [P, DC, D])
                    load(nc, (w1[:], a["L1_gnn_W1"].rearrange("(k p) d -> p k d", p=P)))
                    project(nc, "p1_", c, xnt, w1, D, h)
                    source_table1(nc, h, degree, dinv, rows1)
                with Mem(nc) as m2:
                    wqkv = m2.sb("wqkv1", [P, DC, 3 * D])
                    bkv = m2.sb("bkv1", [1, 2 * D])
                    bq = m2.sb("bq1", [P, DC])
                    kv = m2.sb("kv1", [P, NT, 2 * D])
                    g = m2.sb("g1", [P, DC, D])
                    gb = m2.sb("gb1", [1, D])
                    load(nc, (wqkv[:], a["L1_mix_w_qkv"].rearrange("(k p) j -> p k j", p=P)),
                         (bkv[:], row_of(a["L1_mix_b_qkv"][D:3 * D])), (bq[:], columns_of(a["L1_mix_b_qkv"][0:D])))
                    project(nc, "kv_", c, xnt, wqkv[:, :, D:3 * D], 2 * D, kv, bkv, D)
                    channel_attention1(nc, c, kv, wqkv[:, :, 0:D], bq, g, gb)
                    add_product(nc, "mix1_", xnt, g, gb, c, xn)
                add(nc, x, xn)
                gain = m1.sb("gain1", [P, DC])
                shift = m1.sb("shift1", [P, DC])
                load(nc, (gain[:], columns_of(a["L1_mix_norm_g"])), (shift[:], columns_of(a["L1_mix_norm_b"])))
                layer_norm(nc, "ln3_", c, xn, xnt, None, gain, shift)
            mlp(nc, "ff1_", c, xnt, x, ACT.Gelu, 768, tuple(a["L1_mix_" + n] for n in ("w_fc1", "b_fc1", "w_fc2", "b_fc2")))
            with Mem(nc) as m1:
                acc = m1.sb("acc_1", [P, NT + 1, D])
                bias1 = m1.sb("bias1", [P, D])
                load(nc, (bias1[:], row_of(a["L1_gnn_b1"]).broadcast_to([P, D])))
                aggregate(nc, "ag1_", c, e, e.src, rows1, 0, None, 0, acc)
                finish_gcn(nc, acc, h, dinv, bias1)
                turn_tokens(nc, "tt_", c, h, xnt)
            with Mem(nc) as m1:
                w2 = m1.sb("gw2", [P, DC, D])
                att = m1.sb("att2", [P, 2, D])
                bias2 = m1.sb("bias2", [P, D])
                target = m1.sb("target2", [P, NT + 1, 2])
                scores = m1.sb("scores2", [P, K2, G, 2])
                acc = m1.sb("acc_2", [P, NT + 1, D + 2])
                load(nc, (w2[:], a["L1_gnn_W2"].rearrange("(k p) d -> p k d", p=P)),
                     (att[:, 0, :], row_of(a["L1_gnn_att_src"]).broadcast_to([P, D])),
                     (att[:, 1, :], row_of(a["L1_gnn_att_dst"]).broadcast_to([P, D])),
                     (bias2[:], row_of(a["L1_gnn_b2"]).broadcast_to([P, D])))
                project(nc, "p2_", c, xnt, w2, D, h)
                tables2(nc, h, att, acc, target, source_scores2, rows2)
                edge_scores(nc, "es2_", c, e, e.src, source_scores2, 1, target, False, scores)
                segment_softmax(nc, "sm2_", c, e, 1, 2, scores)
                aggregate(nc, "ag2_", c, e, e.src, rows2, 1, scores, 2, acc)
                finish_gat(nc, acc, h, degree, bias2, x)
        with Mem(nc) as m0:
            xn = m0.sb("xn2", [P, NT, D])
            wr = m0.sb("wr2", [P, DC, 1])
            br = m0.sb("br2", [1, 1])
            w = m0.sb("w2", [P, NT, 1])
            gate = m0.sb("gate2", [P, NT, 1])
            load(nc, (wr[:], a["L1_ffn_wr"].rearrange("(k p) e -> p k e", p=P)), (br[:], row_of(a["L1_ffn_br"])))
            layer_norm(nc, "ln4_", c, x, xnt, xn)
            project(nc, "pw_", c, xnt, wr, 1, w, br)
            select_top(nc, c, w[:, :, 0], weights_row, gate)
            add(nc, x, xn)
            mlp(nc, "ff2_", c, xnt, x, ACT.Gelu_apprx_tanh, 1024, tuple(a["L1_ffn_" + n] for n in ("w1", "b1", "w2", "b2")), gate)
        store(nc, x, out)


INPUTS = ["x", "src", "dst", "edge_type_8"] + ["L0_gnn_" + n for n in ("W", "attn_src", "attn_dst")] + [
    "L0_mix_" + n for n in ("W_qkv", "W_out", "b_out")] + [
    "L0_ffn_" + n for n in ("Wr", "W1s", "b1s", "W2s", "b2s", "W1p", "b1p", "W2p", "b2p")] + [
    "L1_gnn_" + n for n in ("W1", "b1", "W2", "att_src", "att_dst", "b2")] + [
    "L1_mix_" + n for n in ("w_qkv", "b_qkv", "norm_g", "norm_b", "w_fc1", "b_fc1", "w_fc2", "b_fc2")] + [
    "L1_ffn_" + n for n in ("wr", "br", "w1", "b1", "w2", "b2")]


def kernel(**inputs):
    import numpy as _np
    import concourse.bacc as _bacc
    from concourse import mybir as _mybir
    from concourse.bass_utils import run_bass_kernel_spmd as _run

    nc = _bacc.Bacc("TRN2", target_bir_lowering=False, num_devices=1)
    arrays, args = {}, {}
    for name in INPUTS:
        a = _np.ascontiguousarray(inputs[name])
        arrays[f"in_{name}"] = a
        args[name] = nc.dram_tensor(f"in_{name}", a.shape, _mybir.dt.from_np(a.dtype), kind="ExternalInput").ap()
    out = nc.dram_tensor("out_dram", (N, D), _mybir.dt.float32, kind="ExternalOutput").ap()
    program(nc, args, out)
    r = _run(nc, [arrays], core_ids=[0])
    return r.results[0]["out_dram"]
```

```python
import itertools
from contextlib import ExitStack, contextmanager

import concourse.bass as bass
from concourse import mybir

ALU = mybir.AluOpType
ACT = mybir.ActivationFunctionType
AX = mybir.AxisListType
F32 = mybir.dt.float32
I32 = mybir.dt.int32
BF16 = mybir.dt.bfloat16

P = 128
N = 3125
D = 256
DC = D // P
NT = (N + P - 1) // P
NP = NT * P
TAIL = N - (NT - 1) * P
U = 5
assert NT % U == 0
CREDIT = 5
NEG = -1.0e30
R0, H0, D0 = 8, 8, 32
EPS = 1e-5
STAGES = itertools.count()


def before(u, slots, unroll=U):
    d = 1
    while ((u - d) % unroll) % slots != u % slots:
        d += 1
    return d


def earlier(i, u, slots, unroll=U):
    mine = [v for v in range(unroll) if v % slots == u % slots]
    return i * len(mine) + mine.index(u)


@contextmanager
def stage(nc, *names):
    here = next(STAGES)
    sems = [nc.alloc_semaphore(f"{n}_{here}") for n in names]
    with nc.Block() as block:
        yield (block, *sems)
    nc.clear_and_free_semaphores(sems)
    nc.all_engine_barrier()


class Mem:

    def __init__(self, nc):
        self.nc, self.ctx = nc, ExitStack()

    def __enter__(self):
        return self

    def __exit__(self, *a):
        return self.ctx.__exit__(*a)

    def sb(self, name, shape, dt=F32):
        return self.ctx.enter_context(self.nc.sbuf_tensor(name, shape, dt))

    def ps(self, name, shape, dt=F32):
        return self.ctx.enter_context(self.nc.psum_tensor(name, shape, dt))


def constants(nc, c, x, x_in):
    with Mem(nc) as m, stage(nc, "x_zeroed", "x_loaded", "iotas", "chain") as (block, x_zeroed, x_loaded, iotas, chain):
        part = c.part

        @block.gpsimd
        def _(pool):
            pool.iota(c.iota[:], [[1, P]], 0, 0, allow_small_or_imprecise_dtypes=True)
            pool.iota(part[:], [[0, 1]], 0, 1, allow_small_or_imprecise_dtypes=True)
            pool.iota(c.head[:], [[P, DC], [-D0, H0]], 0, 1, allow_small_or_imprecise_dtypes=True)
            pool.iota(c.token[:], [[P, NT]], 0, 1, allow_small_or_imprecise_dtypes=True).then_inc(iotas, 1)

        @block.sync
        def _(sp):
            full = (NT - 1) * P
            sp.dma_start(x[:, 0:NT - 1, :], x_in[0:full].rearrange("(t p) d -> p t d", p=P)).then_inc(x_loaded, 16)
            sp.wait_ge(x_zeroed, 1)
            sp.dma_start(x[0:TAIL, NT - 1, :], x_in[full:N]).then_inc(x_loaded, 16)
            sp.wait_ge(x_loaded, 32)

        @block.vector
        def _(dve):
            dve.memset(x[:, NT - 1, :], 0.0).then_inc(x_zeroed, 1)
            dve.memset(c.ones[:], 1.0)
            dve.wait_ge(iotas, 1)
            dve.tensor_scalar(c.ident[:], c.iota[:], part[:, 0:1], None, ALU.is_equal)
            dve.tensor_scalar(c.valid[:], c.token[:], float(N), None, ALU.is_lt).then_inc(chain, 1)
            dve.tensor_scalar(c.headge[:], c.head[:], 0.0, None, ALU.is_ge).then_inc(chain, 1)
            dve.wait_ge(chain, 2)
            dve.tensor_scalar(c.mask[:], c.valid[:], -1.0, -NEG, ALU.add, ALU.mult)
            dve.scalar_tensor_tensor(out=c.head32[:], in0=c.head[:], scalar=float(D0), in1=c.headge[:],
                                     op0=ALU.is_lt, op1=ALU.mult)


class Consts:
    def __init__(self, m):
        self.part = m.sb("part", [P, 1])
        self.iota = m.sb("iota", [P, P])
        self.head = m.sb("head", [P, DC, H0])
        self.headge = m.sb("headge", [P, DC, H0])
        self.head32 = m.sb("head32", [P, DC, H0])
        self.token = m.sb("token", [P, NT])
        self.valid = m.sb("valid", [P, NT])
        self.mask = m.sb("mask", [P, NT])
        self.ones = m.sb("ones", [P, P])
        self.ident = m.sb("ident", [P, P])


def layer_norm(nc, tag, c, x, xnt, xn=None, gain=None, bias=None):
    with Mem(nc) as m, stage(nc, *(tag + n for n in (
            "stats", "moments", "std", "rstd", "normed", "turned", "kept", "evacuated"))) as (
            block, stats, moments, std, rstd, normed, turned, kept, evacuated):
        st = m.sb(tag + "st", [P, NT, 6])
        mean2, mean, gap, gap2, m2, var, vareps, sd, r0, r1, r2, r3, rs = (
            m.sb(tag + n, [P, NT]) for n in ("mean2", "mean", "gap", "gap2", "m2", "var", "vareps", "sd", "r0", "r1", "r2", "r3", "rs"))
        slot = m.sb(tag + "slot", [P, U, D])
        turn = m.ps(tag + "turn", [P, U, 512])

        @block.vector
        def _(dve):
            with dve.Fori(0, NT // U) as i:
                for u in range(U):
                    dve.bn_stats(st[:, i * U + u, :], x[:, i * U + u, :]).then_inc(stats, 1)
            dve.wait_ge(stats, NT)
            dve.tensor_tensor(mean2[:], st[:, :, 1], st[:, :, 4], ALU.add).then_inc(moments, 1)
            dve.tensor_tensor(gap[:], st[:, :, 1], st[:, :, 4], ALU.subtract).then_inc(moments, 1)
            dve.tensor_tensor(m2[:], st[:, :, 2], st[:, :, 5], ALU.add).then_inc(moments, 1)
            dve.wait_ge(moments, 3)
            dve.tensor_scalar(mean[:], mean2[:], 0.5, None, ALU.mult).then_inc(moments, 1)
            dve.scalar_tensor_tensor(out=gap2[:], in0=gap[:], scalar=D / 4.0, in1=gap[:],
                                     op0=ALU.mult, op1=ALU.mult).then_inc(moments, 1)
            dve.wait_ge(moments, 5)
            dve.tensor_tensor(var[:], gap2[:], m2[:], ALU.add).then_inc(moments, 1)
            dve.wait_ge(moments, 6)
            dve.tensor_scalar(vareps[:], var[:], 1.0 / D, EPS, ALU.mult, ALU.add).then_inc(moments, 1)
            dve.wait_ge(std, 1)
            dve.reciprocal(r0[:], sd[:]).then_inc(moments, 1)
            dve.wait_ge(moments, 8)
            dve.tensor_tensor(r1[:], r0[:], r0[:], ALU.mult).then_inc(moments, 1)
            dve.wait_ge(moments, 9)
            dve.tensor_tensor(r2[:], r1[:], vareps[:], ALU.mult).then_inc(moments, 1)
            dve.wait_ge(moments, 10)
            dve.tensor_scalar(r3[:], r2[:], -0.5, 1.5, ALU.mult, ALU.add).then_inc(moments, 1)
            dve.wait_ge(moments, 11)
            dve.tensor_tensor(rs[:], r0[:], r3[:], ALU.mult).then_inc(rstd, 1)
            dve.wait_ge(rstd, 1)
            with dve.Fori(0, NT // U) as i:
                for u in range(U):
                    t = i * U + u
                    dve.wait_ge(turned, t - U + 1 + CREDIT)
                    if xn is not None:
                        dve.wait_ge(kept, t - U + 1 + CREDIT)
                    dve.tensor_scalar(slot[:, u, :], x[:, t, :], mean[:, bass.ts(t, 1)], rs[:, bass.ts(t, 1)],
                                      ALU.subtract, ALU.mult).then_inc(normed, 1)

        @block.gpsimd
        def _(pool):
            if xn is None:
                return
            pool.sem_inc(kept, CREDIT)
            with pool.Fori(0, NT // U) as i:
                for u in range(U):
                    t = i * U + u
                    pool.wait_ge(normed, t + 1)
                    pool.tensor_copy(xn[:, t, :], slot[:, u, :]).then_inc(kept, 1)

        @block.tensor
        def _(pe):
            pe.sem_inc(turned, CREDIT)
            with pe.Fori(0, NT // U) as i:
                for u in range(U):
                    t = i * U + u
                    pe.wait_ge(normed, t + 1)
                    pe.wait_ge(evacuated, t - U + 1 + CREDIT)
                    for k in range(DC):
                        last = pe.transpose(turn[:, u, k * P:(k + 1) * P], slot[:, u, k * P:(k + 1) * P], c.ident[:])
                    last.then_inc(turned, 1)

        @block.scalar
        def _(act):
            act.wait_ge(moments, 7)
            act.activation(sd[:], vareps[:], ACT.Sqrt).then_inc(std, 1)
            act.sem_inc(evacuated, CREDIT)
            with act.Fori(0, NT // U) as i:
                for u in range(U):
                    t = i * U + u
                    act.wait_ge(turned, t + 1 + CREDIT)
                    for k in range(DC):
                        dst = xnt[:, k, bass.ts(t, P)]
                        src = turn[:, u, k * P:(k + 1) * P]
                        if gain is None:
                            last = act.copy(dst, src)
                        else:
                            last = act.activation(dst, src, ACT.Identity, scale=gain[:, k:k + 1], bias=bias[:, k:k + 1])
                    last.then_inc(evacuated, 1)


HV = R0 * D
CK, CV, CS = HV, HV + P, HV + 2 * P
COLS0 = CS
CT, CEND = CS + R0 * H0, CS + 2 * R0 * H0
CHUNKS0 = [(lo, min(lo + 512, COLS0)) for lo in range(0, COLS0, 512)]


def weights0(nc, c, a, cat):
    with Mem(nc) as m, stage(nc, "w_loaded", "av_loaded", "kv_loaded", "blocked", "turned", "kept", "scored") as (
            block, w_loaded, av_loaded, kv_loaded, blocked, turned, kept, scored):
        w = m.sb("w0", [P, R0 * DC, D])
        av = m.sb("av0", [P, 2, DC])
        heads = m.sb("heads0", [P, DC, 2, H0])
        turn = m.ps("turn0", [P, 2, 512])
        score = m.ps("score0", [P, DC, R0, 2 * H0])

        @block.sync
        def _(sp):
            sp.dma_start(w[:], a["L0_gnn_W"].rearrange("r o f -> (r o) f").rearrange("(q p) f -> p q f", p=P)).then_inc(w_loaded, 16)
            for s, n in enumerate(("attn_src", "attn_dst")):
                sp.dma_start(av[:, s, :], a["L0_gnn_" + n].rearrange("h d -> (h d)").rearrange("(k p) -> p k", p=P),
                             allow_slow_non_contiguous=True).then_inc(av_loaded, 16)
            sp.dma_start(cat[:, :, CK:CS], a["L0_mix_W_qkv"].rearrange("(k p) j -> p k j", p=P)[:, :, P:3 * P]).then_inc(kv_loaded, 16)
            sp.wait_ge(kv_loaded, 16)

        @block.vector
        def _(dve):
            dve.wait_ge(av_loaded, 32)
            for k in range(DC):
                for s in range(2):
                    dve.tensor_scalar(heads[:, k, s, :], c.head32[:, k, :], av[:, s, k:k + 1], None,
                                      ALU.mult).then_inc(blocked, 1)
            dve.wait_ge(scored, 1)
            for k in range(DC):
                for s in range(2):
                    dst = cat[:, k, CS + s * R0 * H0:CS + (s + 1) * R0 * H0].rearrange("p (r h) -> p r h", h=H0)
                    dve.tensor_copy(dst, score[:, k, :, s * H0:(s + 1) * H0])

        @block.tensor
        def _(pe):
            pe.wait_ge(w_loaded, 16)
            for r in range(R0):
                if r >= 2:
                    pe.wait_ge(kept, r - 1)
                for k in range(DC):
                    for o in range(DC):
                        last = pe.transpose(turn[:, r % 2, (k * DC + o) * P:(k * DC + o + 1) * P],
                                            w[:, r * DC + o, k * P:(k + 1) * P], c.ident[:])
                last.then_inc(turned, 1)
            pe.wait_ge(blocked, 2 * DC)
            for r in range(R0):
                for k in range(DC):
                    for o in range(DC):
                        last = pe.matmul(score[:, k, r, :], w[:, r * DC + o, k * P:(k + 1) * P],
                                         heads[:, o, :, :].rearrange("p s h -> p (s h)"), start=(o == 0), stop=(o == DC - 1))
            last.then_inc(scored, 1)

        @block.scalar
        def _(act):
            for r in range(R0):
                act.wait_ge(turned, r + 1)
                act.copy(cat[:, :, r * D:(r + 1) * D], turn[:, r % 2, :].rearrange("p (k o) -> p k o", k=DC)).then_inc(kept, 1)


def linear_attention0(nc, c, a, keys, vals, g):
    scale = 32 ** -0.5
    with Mem(nc) as m, stage(nc, "loaded", "dve_did", "pe_did", "act_did", "exped") as (
            block, loaded, dve_did, pe_did, act_did, exped):
        wq = m.sb("wq0", [P, DC, P])
        wqt = m.sb("wqt0", [P, DC, P])
        wo = m.sb("wo0", [P, D])
        part_max = m.sb("pmax0", [P, P])
        col_max = m.sb("cmax0", [P, 1])
        diag = m.sb("diag0", [P, P])
        max_row = m.sb("maxrow0", [P, P])
        inv = m.sb("inv0", [P, P])
        ctx = m.sb("ctx0", [P, P])
        ctx2 = m.sb("ctxs0", [P, P])
        mo = m.sb("mo0", [P, D])
        turn = m.ps("mt0", [P, 512])
        rows = m.ps("mr0", [P, 512])
        ctx_ps = m.ps("mc0", [P, 512])
        sum_ps = m.ps("ms0", [P, 512])
        mo_ps = m.ps("mm0", [P, 512])
        g_ps = m.ps("mg0", [P, DC, D])

        @block.sync
        def _(sp):
            sp.dma_start(wq[:], a["L0_mix_W_qkv"].rearrange("(k p) j -> p k j", p=P)[:, :, 0:P]).then_inc(loaded, 16)
            sp.dma_start(wo[:], a["L0_mix_W_out"]).then_inc(loaded, 16)

        @block.vector
        def _(dve):
            dve.tensor_reduce(part_max[:], keys[:].rearrange("p t d -> p d t"), AX.X, ALU.max).then_inc(dve_did, 1)
            dve.wait_ge(pe_did, 1)
            dve.tensor_reduce(col_max[:], turn[:, 0:P], AX.X, ALU.max).then_inc(dve_did, 1)
            dve.wait_ge(dve_did, 2)
            dve.tensor_scalar(diag[:], c.ident[:], col_max[:, 0:1], None, ALU.mult).then_inc(dve_did, 1)
            dve.wait_ge(pe_did, 2)
            dve.tensor_copy(max_row[:], rows[:, 0:P]).then_inc(dve_did, 1)
            dve.wait_ge(dve_did, 4)
            dve.tensor_tensor(keys[:], keys[:], max_row[:].unsqueeze(1).broadcast_to([P, NT, P]), ALU.subtract).then_inc(dve_did, 1)
            dve.wait_ge(pe_did, 4)
            dve.reciprocal(inv[:], sum_ps[:, 0:P]).then_inc(dve_did, 1)
            dve.wait_ge(dve_did, 6)
            dve.scalar_tensor_tensor(out=ctx[:], in0=ctx_ps[:, 0:P], scalar=scale, in1=inv[:], op0=ALU.mult, op1=ALU.mult).then_inc(dve_did, 1)
            dve.wait_ge(dve_did, 7)
            dve.tensor_tensor(ctx2[:].rearrange("p (h d) -> p h d", d=32), ctx[:].rearrange("p (h d) -> p h d", d=32),
                              c.head32[:, 0, 0:4].unsqueeze(2).broadcast_to([P, 4, 32]), ALU.mult).then_inc(dve_did, 1)
            dve.wait_ge(pe_did, 5)
            dve.tensor_copy(mo[:], mo_ps[:, 0:D]).then_inc(dve_did, 1)
            dve.wait_ge(pe_did, 6)
            dve.tensor_copy(g[:], g_ps[:])

        @block.scalar
        def _(act):
            act.wait_ge(pe_did, 3)
            act.copy(wqt[:], turn[:, P:P + DC * P].rearrange("p (k f) -> p k f", k=DC)).then_inc(act_did, 1)
            act.wait_ge(dve_did, 5)
            act.activation(keys[:], keys[:], ACT.Exp).then_inc(exped, 1)

        @block.tensor
        def _(pe):
            pe.wait_ge(dve_did, 1)
            pe.transpose(turn[:, 0:P], part_max[:], c.ident[:]).then_inc(pe_did, 1)
            pe.wait_ge(dve_did, 3)
            pe.matmul(rows[:, 0:P], c.ones[:], diag[:], start=True, stop=True).then_inc(pe_did, 1)
            pe.wait_ge(loaded, 32)
            for k in range(DC):
                last = pe.transpose(turn[:, (k + 1) * P:(k + 2) * P], wq[:, k, :], c.ident[:])
            last.then_inc(pe_did, 1)
            pe.wait_ge(exped, 1)
            for t in range(NT):
                pe.matmul(sum_ps[:, 0:P], c.ones[:], keys[:, t, :], start=(t == 0), stop=(t == NT - 1))
                last = pe.matmul(ctx_ps[:, 0:P], vals[:, t, :], keys[:, t, :], start=(t == 0), stop=(t == NT - 1))
            last.then_inc(pe_did, 1)
            pe.wait_ge(dve_did, 8)
            pe.matmul(mo_ps[:, 0:D], ctx2[:], wo[:], start=True, stop=True).then_inc(pe_did, 1)
            pe.wait_ge(dve_did, 9)
            pe.wait_ge(act_did, 1)
            for k in range(DC):
                last = pe.matmul(g_ps[:, k, :], wqt[:, k, :], mo[:], start=True, stop=True)
            last.then_inc(pe_did, 1)


def add_product(nc, tag, xnt, g, bias, c, x, score=None):
    with Mem(nc) as m, stage(nc, "staged", "multiplied", "added", *ScoreSteps.NAMES) as (block, staged, multiplied, added, *sems):
        slot = m.sb(tag + "slot", [P, 2, DC, P])
        acc = m.ps(tag + "acc", [P, 2, 512])
        steps = None
        if score is not None:
            steps = ScoreSteps(m, sems, tag, *score[2], first=score[0], per=score[1], **score[3])

        def batches(u):
            return () if steps is None else range(u * steps.per // U, (u + 1) * steps.per // U)

        @block.sync
        def _(sp):
            if steps is not None:
                with sp.Fori(0, NT // U) as i:
                    for v in range(steps.per):
                        steps.load_rows(sp, i, v)

        @block.scalar
        def _(act):
            if steps is not None:
                with act.Fori(0, NT // U) as i:
                    for v in range(steps.per):
                        steps.indices(act, i, v)

        @block.gpsimd
        def _(pool):
            with pool.Fori(0, NT // U) as i:
                for u in range(U):
                    t = i * U + u
                    pool.wait_ge(multiplied, t - before(u, 2) + 1 + CREDIT)
                    pool.tensor_copy(slot[:, u % 2], xnt[:, :, bass.ts(t, P)]).then_inc(staged, 1)
                    for v in batches(u):
                        steps.gather(pool, i, v)

        @block.tensor
        def _(pe):
            pe.sem_inc(multiplied, CREDIT)
            if steps is not None:
                steps.start_pe(pe)
            with pe.Fori(0, NT // U) as i:
                for u in range(U):
                    t = i * U + u
                    pe.wait_ge(staged, t + 1)
                    pe.wait_ge(added, t - before(u, 2) + 1 + CREDIT)
                    for k in range(DC):
                        pe.matmul(acc[:, u % 2, 0:D], slot[:, u % 2, k, :], g[:, k, :], start=(k == 0), stop=False)
                    pe.matmul(acc[:, u % 2, 0:D], c.ones[0:1, :], bias[:], start=False, stop=True).then_inc(multiplied, 1)
                    for v in batches(u):
                        steps.match(pe, i, v)

        @block.vector
        def _(dve):
            dve.sem_inc(added, CREDIT)
            if steps is not None:
                steps.start_dve(dve)
            with dve.Fori(0, NT // U) as i:
                for u in range(U):
                    t = i * U + u
                    for v in batches(u):
                        steps.one_hot(dve, i, v)
                    dve.wait_ge(multiplied, t + 1 + CREDIT)
                    dve.tensor_tensor(x[:, t, :], x[:, t, :], acc[:, u % 2, 0:D], ALU.add).then_inc(added, 1)
                    for v in batches(u):
                        steps.score(dve, i, v)


E = 50000
BLK = 256
NB = (E + BLK - 1) // BLK
G = NB + NT - 1
K2 = BLK // P
HALF = G // 2
assert G == 2 * HALF and HALF % U == 0 and HALF <= P
FAR = 4095
LOW = 24
BH = NB // 2


class Edges:

    def __init__(self, m):
        self.src = m.sb("e_src", [P, K2, G], I32)
        self.value_row = m.sb("e_row", [P, K2, G], I32)
        self.local = m.sb("e_local", [P, K2, G])
        self.rel = m.sb("e_rel", [P, K2, G])
        self.step = m.sb("e_step", [HALF, 2, BLK])
        self.back = m.sb("e_back", [HALF, 2, BLK])
        self.first = m.sb("e_first", [HALF, 2, BLK])
        self.last = m.sb("e_last", [HALF, 2, BLK])
        self.cont = m.sb("e_cont", [H0, G])
        self.over_prev = m.sb("e_over_prev", [H0, G])
        self.over_this = m.sb("e_over_this", [H0, G])
        self.tile = m.sb("e_tile", [1, G], I32)


def find_groups(nc, c, a, e, packed, tiles, local_row, low_row):
    with Mem(nc) as m, stage(nc, "zeroed", "loaded", "iotas", "packed", "stored", "counted", "chain",
                             "fetched", "tiles_out", "tiles_in", "turned", "kept", "brows", "rows_out") as (
            block, zeroed, loaded, iotas, packed_up, stored, counted, chain, fetched, tiles_out, tiles_in, turned, kept,
            brows, rows_out):
        raw = m.sb("g_raw", [BH, 3, 2, BLK], I32)
        sh = m.sb("g_sh", [BH, 2, 2, BLK], I32)
        pk = m.sb("g_pk", [BH, 2, BLK], I32)
        dstf = m.sb("g_dstf", [BH, 2, BLK])
        junk = m.sb("g_junk", [BH, 2, BLK])
        cnt = m.sb("g_cnt", [BH, NT + 1])
        off = m.sb("g_off", [P, NT + 1])
        offm = m.sb("g_offm", [P, 2, NT])
        offi = m.sb("g_offi", [P, 2, NT], I32)
        blki = m.sb("g_blki", [P, 2, NT], I32)
        blk = m.sb("g_blk", [P, 2, NT])
        some = m.sb("g_some", [P, NT])
        span = m.sb("g_span", [P, NT])
        num = m.sb("g_num", [P, NT])
        cum = m.sb("g_cum", [P, NT])
        base = m.sb("g_base", [P, NT])
        base2 = m.sb("g_base2", [P, NT])
        gid = m.sb("g_gid", [P, 2])
        tid = m.sb("g_tid", [P, NT])
        cmp = m.sb("g_cmp", [P, 2, NT])
        cmp2 = m.sb("g_cmp2", [P, 2, NT])
        cmp3 = m.sb("g_cmp3", [P, 2, NT])
        tile = m.sb("g_tile", [P, 2])
        rowf = m.sb("g_rowf", [P, 2])
        rowf2 = m.sb("g_rowf2", [P, 2])
        row = m.sb("g_row", [P, 2], I32)
        tilei = m.sb("g_tilei", [P, 2], I32)
        got = m.sb("g_got", [HALF, 2, BLK], I32)
        bits = m.sb("g_bits", [HALF, 3, 2, BLK], I32)
        f = m.sb("g_f", [HALF, 3, 2, BLK])
        lowi = m.sb("g_lowi", [HALF, 2, BLK], I32)
        brow = m.sb("g_brow", [HALF, 2, 2, BLK], BF16)
        vrow = m.sb("g_vrow", [HALF, 2, BLK])
        loc = m.sb("g_loc", [HALF, 2, BLK])
        ok0 = m.sb("g_ok0", [HALF, 2, BLK])
        ok = m.sb("g_ok", [HALF, 2, BLK])
        key0 = m.sb("g_key0", [HALF, 2, BLK])
        key = m.sb("g_key", [HALF, 2, BLK])
        tile128 = m.sb("g_t128", [P, 2])
        edge = m.sb("g_edge", [HALF, 2, BLK])
        runs = m.sb("g_runs", [HALF, 2])
        rep = m.sb("g_rep", [HALF, 2, 3, H0])
        rows = m.sb("g_rows", [H0, 3, G])
        same = m.sb("g_same", [H0, G])
        prev = m.sb("g_prev", [H0, G])
        this = m.sb("g_this", [H0, G])
        total = m.ps("g_total", [P, 512])
        turn = m.ps("g_turn", [P, 4, 512])
        trow = m.ps("g_trow", [P, 3, 512])

        @block.sync
        def _(sp):
            sp.wait_ge(zeroed, 1)
            cut = BH * BLK
            for n, name in enumerate(("src", "dst", "edge_type_8")):
                v = a[name]
                sp.dma_start(raw[:, n, 0, :], v[0:cut].rearrange("(b e) -> b e", e=BLK)).then_inc(loaded, 16)
                sp.dma_start(raw[0:BH - 1, n, 1, :], v[cut:(NB - 1) * BLK].rearrange("(b e) -> b e", e=BLK)).then_inc(loaded, 16)
                sp.dma_start(raw[BH - 1:BH, n, 1, 0:E - (NB - 1) * BLK],
                             v[(NB - 1) * BLK:E].rearrange("(b e) -> b e", b=1)).then_inc(loaded, 16)
            sp.wait_ge(packed_up, 1)
            for h in range(2):
                sp.dma_start(packed[h * BH:(h + 1) * BH], pk[:, h, :]).then_inc(stored, 16)
            sp.wait_ge(chain, 18)
            for h in range(2):
                sp.dma_start(tiles[0, h * HALF:(h + 1) * HALF].rearrange("(g a) -> g a", a=1), tilei[0:HALF, h:h + 1],
                             allow_slow_non_contiguous=True).then_inc(tiles_out, 16)
            sp.wait_ge(tiles_out, 32)
            sp.dma_start(e.tile[:], tiles).then_inc(tiles_in, 16)
            sp.wait_ge(tiles_in, 16)
            sp.wait_ge(brows, 2)
            for h in range(2):
                sp.dma_start(low_row[h * HALF:(h + 1) * HALF], brow[:, 0, h, :]).then_inc(rows_out, 16)
                sp.dma_start(local_row[h * HALF:(h + 1) * HALF], brow[:, 1, h, :]).then_inc(rows_out, 16)
            sp.wait_ge(rows_out, 64)

        @block.gpsimd
        def _(pool):
            pool.iota(gid[:], [[HALF, 2]], 0, 1, allow_small_or_imprecise_dtypes=True)
            pool.iota(tid[:], [[1, NT]], 0, 0, allow_small_or_imprecise_dtypes=True).then_inc(iotas, 1)
            pool.wait_ge(stored, 32)
            pool.wait_ge(chain, 17)
            for h in range(2):
                pool.indirect_dma_start(got[:, h, :], None, packed, bass.IndirectOffsetOnAxis(row[0:HALF, h:h + 1], 0)).then_inc(fetched, 16)

        @block.tensor
        def _(pe):
            pe.wait_ge(counted, NT + 1)
            pe.matmul(total[:, 0:NT + 1], c.ones[0:BH, :], cnt[:], start=True, stop=True).then_inc(turned, 1)
            for q, (n, src) in enumerate(((22, f[:, 0]), (23, vrow), (24, loc), (22, f[:, 2]))):
                pe.wait_ge(chain, n)
                for h in range(2):
                    for k in range(K2):
                        last = pe.transpose(turn[:, q, (h * K2 + k) * P:(h * K2 + k) * P + HALF],
                                            src[:, h, k * P:(k + 1) * P], c.ident[0:HALF, 0:HALF])
                last.then_inc(turned, 1)
            pe.wait_ge(chain, 35)
            for q in range(3):
                for h in range(2):
                    last = pe.transpose(trow[0:H0, q, h * HALF:(h + 1) * HALF], rep[:, h, q, :], c.ident[0:HALF, 0:HALF])
            last.then_inc(turned, 1)

        @block.scalar
        def _(act):
            def spread(q):
                return turn[:, q, :].rearrange("p (h k g) -> p h k g", h=2, k=K2)[:, :, :, 0:HALF]
            for q, dst in enumerate((e.src, e.value_row, e.local, e.rel)):
                act.wait_ge(turned, q + 2)
                act.copy(dst[:].rearrange("p k (h g) -> p h k g", h=2), spread(q))
            act.wait_ge(turned, 6)
            act.copy(rows[:], trow[0:H0, :, 0:G]).then_inc(kept, 1)

        @block.vector
        def _(dve):
            done = [0]

            def link(ins):
                done[0] += 1
                ins.then_inc(chain, 1)
                dve.wait_ge(chain, done[0])

            dve.memset(raw[:, 1, 1, :], FAR)
            dve.memset(raw[:, 0, 1, :], 0)
            dve.memset(raw[:, 2, 1, :], 0).then_inc(zeroed, 1)
            dve.wait_ge(loaded, 16 * 9)
            link(dve.tensor_scalar(sh[:, 0], raw[:, 1], 12, None, ALU.logical_shift_left))
            link(dve.tensor_scalar(sh[:, 1], raw[:, 2], 24, None, ALU.logical_shift_left))
            link(dve.tensor_tensor(pk[:], sh[:, 0], raw[:, 0], ALU.bitwise_or))
            dve.tensor_tensor(pk[:], pk[:], sh[:, 1], ALU.bitwise_or).then_inc(packed_up, 1)
            link(dve.tensor_copy(dstf[:], raw[:, 1]))
            for t in range(NT + 1):
                if t:
                    dve.wait_ge(counted, t)
                dve.tensor_scalar(junk[:], dstf[:], float(t * P), 0.0, ALU.is_lt, ALU.add,
                                  accum_out=cnt[:, t:t + 1]).then_inc(counted, 1)
            dve.wait_ge(turned, 1)
            link(dve.tensor_copy(off[:], total[:, 0:NT + 1]))
            link(dve.tensor_copy(offm[:, 0], off[:, 0:NT]))
            link(dve.tensor_scalar(offm[:, 1], off[:, 1:NT + 1], -1.0, None, ALU.add))
            link(dve.tensor_copy(offi[:], offm[:]))
            link(dve.tensor_scalar(blki[:], offi[:], 8, None, ALU.arith_shift_right))
            link(dve.tensor_copy(blk[:], blki[:]))
            link(dve.tensor_tensor(some[:], off[:, 1:NT + 1], off[:, 0:NT], ALU.is_gt))
            dve.wait_ge(iotas, 1)
            link(dve.tensor_tensor(span[:], blk[:, 1], blk[:, 0], ALU.subtract))
            link(dve.scalar_tensor_tensor(out=num[:], in0=span[:], scalar=1.0, in1=some[:], op0=ALU.add, op1=ALU.mult))
            link(dve.tensor_tensor_scan(cum[:], c.ones[:, 0:NT], num[:], 0.0, ALU.mult, ALU.add))
            link(dve.tensor_tensor(base[:], blk[:, 0], cum[:], ALU.subtract))
            dve.tensor_tensor(base2[:], base[:], num[:], ALU.add).then_inc(counted, 1)
            dve.tensor_tensor(cmp[:], cum[:].unsqueeze(1).broadcast_to([P, 2, NT]),
                              gid[:].unsqueeze(2).broadcast_to([P, 2, NT]), ALU.is_le).then_inc(counted, 1)
            dve.wait_ge(counted, NT + 3)
            dve.tensor_reduce(tile[:], cmp[:], AX.X, ALU.add).then_inc(counted, 1)
            dve.wait_ge(counted, NT + 4)
            dve.tensor_tensor(cmp2[:], tid[:].unsqueeze(1).broadcast_to([P, 2, NT]),
                              tile[:].unsqueeze(2).broadcast_to([P, 2, NT]), ALU.is_equal).then_inc(counted, 1)
            dve.wait_ge(counted, NT + 5)
            dve.tensor_tensor(cmp3[:], cmp2[:], base2[:].unsqueeze(1).broadcast_to([P, 2, NT]), ALU.mult).then_inc(counted, 1)
            dve.wait_ge(counted, NT + 6)
            dve.tensor_reduce(rowf[:], cmp3[:], AX.X, ALU.add).then_inc(counted, 1)
            dve.wait_ge(counted, NT + 7)
            link(dve.tensor_tensor(rowf2[:], rowf[:], gid[:], ALU.add))
            link(dve.tensor_scalar(row[:], rowf2[:], float(NB - 1), None, ALU.min))
            link(dve.tensor_copy(tilei[:], tile[:]))
            dve.wait_ge(fetched, 32)
            link(dve.tensor_scalar(bits[:, 0], got[:], FAR, None, ALU.bitwise_and))
            link(dve.tensor_scalar(bits[:, 1], got[:], 12, FAR, ALU.logical_shift_right, ALU.bitwise_and))
            link(dve.tensor_scalar(bits[:, 2], got[:], 24, None, ALU.logical_shift_right))
            link(dve.tensor_copy(f[:], bits[:]))
            link(dve.scalar_tensor_tensor(out=vrow[:], in0=f[:, 2], scalar=float(NP), in1=f[:, 0], op0=ALU.mult, op1=ALU.add))
            dve.tensor_scalar(tile128[:], tile[:], float(-P), None, ALU.mult).then_inc(counted, 1)
            dve.wait_ge(counted, NT + 8)
            for h in range(2):
                ins = dve.tensor_scalar(loc[:, h], f[:, 1, h], tile128[0:HALF, h:h + 1], None, ALU.add)
                if h == 0:
                    ins.then_inc(counted, 1)
            link(ins)
            dve.wait_ge(counted, NT + 9)
            dve.tensor_copy(brow[:, 1], loc[:]).then_inc(brows, 1)
            dve.tensor_scalar(lowi[:], got[:], P - 1, None, ALU.bitwise_and).then_inc(counted, 1)
            dve.wait_ge(counted, NT + 10)
            dve.tensor_copy(brow[:, 0], lowi[:]).then_inc(brows, 1)
            link(dve.tensor_scalar(ok0[:], loc[:], 0.0, None, ALU.is_ge))
            link(dve.scalar_tensor_tensor(out=ok[:], in0=loc[:], scalar=float(P), in1=ok0[:], op0=ALU.is_lt, op1=ALU.mult))
            link(dve.scalar_tensor_tensor(out=key0[:], in0=f[:, 1], scalar=1.0, in1=ok[:], op0=ALU.add, op1=ALU.mult))
            link(dve.tensor_scalar(key[:], key0[:], -1.0, None, ALU.add))
            link(dve.memset(edge[:, :, 0:1], 0.0))
            link(dve.tensor_tensor(edge[:, :, 1:BLK], key[:, :, 1:BLK], key[:, :, 0:BLK - 1], ALU.not_equal))
            link(dve.tensor_reduce(runs[:], edge[:], AX.X, ALU.add))
            link(dve.tensor_scalar(edge[:], edge[:], NEG, None, ALU.mult))
            link(dve.tensor_copy(rep[:, :, 0, :], key[:, :, 0:1].broadcast_to([HALF, 2, H0])))
            link(dve.tensor_copy(rep[:, :, 1, :], key[:, :, BLK - 1:BLK].broadcast_to([HALF, 2, H0])))
            link(dve.tensor_scalar(rep[:, :, 2, :], runs[:].unsqueeze(2).broadcast_to([HALF, 2, H0]), 0.0, None, ALU.is_equal))
            link(dve.tensor_copy(e.step[:], edge[:]))
            link(dve.memset(e.step[:, :, 0:1], NEG))
            link(dve.tensor_copy(e.back[:, :, 0:BLK - 1], edge[:, :, 1:BLK]))
            link(dve.memset(e.back[:, :, BLK - 1:BLK], NEG))
            link(dve.memset(e.last[:, :, BLK - 1:BLK], 0.0))
            for h in range(2):
                link(dve.tensor_tensor_scan(e.first[:, h], edge[:, h], edge[:, h], 0.0, ALU.min, ALU.min))
                link(dve.tensor_tensor_scan(e.last[:, h, 0:BLK - 1][:, ::-1], edge[:, h, 1:BLK][:, ::-1],
                                            edge[:, h, 1:BLK][:, ::-1], 0.0, ALU.min, ALU.min))
            dve.wait_ge(kept, 1)
            link(dve.memset(same[:], 0.0))
            link(dve.memset(prev[:], 0.0))
            link(dve.tensor_tensor(same[:, 1:G], rows[:, 0, 1:G], rows[:, 1, 0:G - 1], ALU.is_equal))
            link(dve.tensor_tensor(prev[:, 1:G], same[:, 1:G], rows[:, 2, 0:G - 1], ALU.mult))
            link(dve.tensor_tensor(this[:], same[:], rows[:, 2, :], ALU.mult))
            link(dve.tensor_scalar(e.cont[:], same[:], -1.0, -NEG, ALU.add, ALU.mult))
            link(dve.tensor_scalar(e.over_prev[:], prev[:], -1.0, -NEG, ALU.add, ALU.mult))
            link(dve.tensor_scalar(e.over_this[:], this[:], -1.0, -NEG, ALU.add, ALU.mult))


SLOPE = 0.2


PARTS = 3
BT = U * K2


def split(dve, chain, base, src, parts, rest):
    dve.tensor_copy(parts(0), src).then_inc(chain, 1)
    for i in range(1, PARTS):
        dve.wait_ge(chain, base + 2 * i - 1)
        dve.tensor_tensor(rest, src if i == 1 else rest, parts(i - 1), ALU.subtract).then_inc(chain, 1)
        dve.wait_ge(chain, base + 2 * i)
        dve.tensor_copy(parts(i), rest).then_inc(chain, 1)
    dve.wait_ge(chain, base + 2 * PARTS - 1)


class ScoreSteps:

    NAMES = ("hot", "matched", "scored", "indexed", "begun", "low_hot", "s_chain",
             *(f"{name}{v}" for name in ("row", "low", "gathered") for v in range(U)))

    def __init__(self, m, sems, tag, c, e, heads, target, scores, local_row, first, per, index=None, table=None,
                 low_row=None, own=None, high=None):
        self.hot, self.matched, self.scored, self.indexed, self.begun, self.low_hot, self.chain, *slotted = sems
        self.row, self.low, self.gathered = slotted[0:U], slotted[U:2 * U], slotted[2 * U:3 * U]
        self.c, self.e, self.heads, self.target, self.scores, self.local_row = c, e, heads, target, scores, local_row
        self.first, self.per, self.index, self.table, self.low_row, self.own, self.high = first, per, index, table, low_row, own, high
        self.width = R0 * heads if heads > 1 else 2 * PARTS
        self.brow = m.sb(tag + "brow", [P, per, BT * P], BF16)
        self.onet = m.sb(tag + "onet", [P, per, BT * P], BF16)
        self.tot = m.sb(tag + "tot", [P, K2, U, heads])
        if heads > 1:
            self.idx = m.sb(tag + "idx", [P, per, K2, U], I32)
            self.rows = m.sb(tag + "rows", [P, per, K2, U, heads])
            self.pick = m.sb(tag + "pick", [P, K2, U, self.width])
            self.red = m.sb(tag + "red", [P, K2, U, heads])
            self.rid = m.sb(tag + "rid", [P, R0, heads])
            self.hit = m.ps(tag + "hit", [P, K2, 512])
        else:
            self.lrow = m.sb(tag + "lrow", [P, per, BT * P], BF16)
            self.lonet = m.sb(tag + "lonet", [P, per, BT * P], BF16)
            self.mask = m.sb(tag + "mask", [P, K2, U, NT])
            self.mask2 = m.sb(tag + "mask2", [P, K2, U, NT])
            self.red = m.sb(tag + "red", [P, K2, U, 1])
            self.red2 = m.sb(tag + "red2", [P, K2, U, 2])
            self.hit = m.ps(tag + "hit", [P, 2, 512])
            self.own_hit = m.ps(tag + "own_hit", [P, 2, 512])

    def hits(self, v):
        if self.heads > 1:
            return self.hit[:, :, 0:U * self.width].rearrange("p k (g w) -> p k g w", g=U)
        return self.hit[:, v % 2, 0:BT * self.width].rearrange("p (k g w) -> p k g w", k=K2, g=U)

    def own_hits(self, v):
        return self.own_hit[:, v % 2, 0:BT * NT].rearrange("p (k g w) -> p k g w", k=K2, g=U)

    def load_rows(self, sp, i, v):
        n = i * self.per + v
        sp.wait_ge(self.hot, n + 1)
        rows = self.local_row.rearrange("(b g) e -> b (g e)", g=U)
        sp.dma_start(self.brow[:, v, :], rows[bass.ds(n + self.first, 1)].broadcast_to([P, BT * P])).then_inc(self.row[v], 16)

    def load_low_rows(self, act, i, v):
        n = i * self.per + v
        act.wait_ge(self.low_hot, n + 1)
        rows = self.low_row.rearrange("(b g) e -> b (g e)", g=U)
        act.dma_start(self.lrow[:, v, :], rows[bass.ds(n + self.first, 1)].broadcast_to([P, BT * P])).then_inc(self.low[v], 16)

    def indices(self, act, i, v):
        n = i * self.per + v
        act.wait_ge(self.scored, n + 1)
        act.copy(self.idx[:, v], self.index[:, :, bass.ds((n + self.first) * U, U)]).then_inc(self.indexed, 1)

    def gather(self, pool, i, v):
        n = i * self.per + v
        pool.wait_ge(self.indexed, n + 1)
        pool.sem_inc(self.begun, 1)
        for k in range(K2):
            for g in range(U):
                pool.indirect_dma_start(self.rows[:, v, k, g, :], None, self.table,
                                        bass.IndirectOffsetOnAxis(self.idx[:, v, k, g:g + 1], 0)).then_inc(self.gathered[v], 16)

    def start_dve(self, dve):
        if self.heads > 1:
            for r in range(R0):
                last = dve.memset(self.rid[:, r, :], float(r))
            last.then_inc(self.chain, 1)
            dve.wait_ge(self.chain, 1)
        dve.sem_inc(self.scored, self.per)
        dve.sem_inc(self.hot, self.per)
        dve.sem_inc(self.low_hot, self.per)

    def one_hot(self, dve, i, v):
        n = i * self.per + v
        dve.wait_ge(self.matched, n + 1)
        dve.wait_ge(self.row[v], (i + 1) * 16)
        dve.tensor_scalar(self.onet[:, v, :], self.brow[:, v, :], self.c.part[:, 0:1], None, ALU.is_equal).then_inc(self.hot, 1)
        if self.heads == 1:
            dve.wait_ge(self.low[v], (i + 1) * 16)
            dve.tensor_scalar(self.lonet[:, v, :], self.lrow[:, v, :], self.c.part[:, 0:1], None, ALU.is_equal).then_inc(self.low_hot, 1)

    def score(self, dve, i, v):
        n = i * self.per + v
        at = bass.ds((n + self.first) * U, U)
        if self.heads > 1:
            dve.wait_ge(self.matched, n + 1 + self.per)
            for k in range(K2):
                for g in range(U):
                    last = dve.scalar_tensor_tensor(
                        out=self.pick[:, k, g, :], in0=self.rid[:].rearrange("p r h -> p (r h)"),
                        scalar=self.e.rel[:, k, bass.ds((n + self.first) * U + g, 1)],
                        in1=self.hits(v)[:, k, g, :], op0=ALU.is_equal, op1=ALU.mult)
            last.then_inc(self.chain, 1)
            dve.wait_ge(self.chain, n * 3 + 2)
            for k in range(K2):
                last = dve.tensor_reduce(self.red[:, k], self.pick[:, k].rearrange("p g (r h) -> p g h r", h=self.heads), AX.X, ALU.add)
            last.then_inc(self.chain, 1)
            dve.wait_ge(self.chain, n * 3 + 3)
            dve.wait_ge(self.gathered[v], (i + 1) * 16 * BT)
            dve.tensor_tensor(self.tot[:], self.red[:], self.rows[:, v], ALU.add).then_inc(self.chain, 1)
            dve.wait_ge(self.chain, n * 3 + 4)
        else:
            dve.tensor_tensor(self.mask[:], self.c.iota[:, 0:NT].unsqueeze(1).unsqueeze(1).broadcast_to([P, K2, U, NT]),
                              self.high[:, :, at].unsqueeze(3).broadcast_to([P, K2, U, NT]), ALU.is_equal).then_inc(self.chain, 1)
            dve.wait_ge(self.matched, n + 1 + self.per)
            dve.wait_ge(self.chain, n * 4 + 1)
            dve.tensor_tensor(self.mask2[:], self.mask[:], self.own_hits(v), ALU.mult)
            dve.tensor_reduce(self.red2[:], self.hits(v).rearrange("p k g (s w) -> p k g w s", w=2), AX.X, ALU.add).then_inc(self.chain, 1)
            dve.wait_ge(self.chain, n * 4 + 2)
            dve.tensor_reduce(self.red[:], self.mask2[:], AX.X, ALU.add).then_inc(self.chain, 1)
            dve.wait_ge(self.chain, n * 4 + 3)
            dve.tensor_copy(self.scores[:, :, at, 1:2], self.red2[:, :, :, 1:2])
            dve.tensor_tensor(self.tot[:], self.red[:], self.red2[:, :, :, 0:1], ALU.add).then_inc(self.chain, 1)
            dve.wait_ge(self.chain, n * 4 + 4)
        dve.scalar_tensor_tensor(out=self.scores[:, :, at, 0:self.heads].rearrange("p k g h -> p k (g h)") if self.heads > 1
                                 else self.scores[:, :, at, 0], in0=self.tot[:].rearrange("p k g h -> p k (g h)"), scalar=SLOPE,
                                 in1=self.tot[:].rearrange("p k g h -> p k (g h)"), op0=ALU.mult, op1=ALU.max).then_inc(self.scored, 1)

    def start_pe(self, pe):
        pe.sem_inc(self.matched, self.per)

    def match(self, pe, i, v):
        n = i * self.per + v
        pe.wait_ge(self.hot, n + 1 + self.per)
        if self.heads == 1:
            pe.wait_ge(self.low_hot, n + 1 + self.per)
        pe.wait_ge(self.scored, n - (1 if self.heads > 1 else before(v, 2, self.per)) + 1 + self.per)
        for g in range(U):
            tile = pe.value_load(self.e.tile[0:1, bass.ds((n + self.first) * U + g, 1)], min_val=0, max_val=NT)
            for k in range(K2):
                hot = slice((g * K2 + k) * P, (g * K2 + k + 1) * P)
                if self.heads > 1:
                    for s in range(PARTS):
                        last = pe.matmul(self.hits(v)[:, k, g, :], self.onet[:, v, hot], self.target[:, tile, s, :],
                                         start=(s == 0), stop=(s == PARTS - 1))
                else:
                    pe.matmul(self.hits(v)[:, k, g, :], self.onet[:, v, hot],
                              self.target[:, tile].rearrange("p s w -> p (s w)"), start=True, stop=True)
                    for s in range(PARTS):
                        last = pe.matmul(self.own_hits(v)[:, k, g, :], self.lonet[:, v, hot], self.own[:, s, :],
                                         start=(s == 0), stop=(s == PARTS - 1))
        last.then_inc(self.matched, 1)


def edge_scores(nc, tag, first, count, per, *args, **kw):
    with Mem(nc) as m, stage(nc, *ScoreSteps.NAMES) as (block, *sems):
        steps = ScoreSteps(m, sems, tag, *args, first=first, per=per, **kw)

        @block.sync
        def _(sp):
            with sp.Fori(0, count // per) as i:
                for v in range(per):
                    steps.load_rows(sp, i, v)

        @block.gpsimd
        def _(pool):
            if steps.heads > 1:
                with pool.Fori(0, count // per) as i:
                    for v in range(per):
                        steps.gather(pool, i, v)

        @block.scalar
        def _(act):
            with act.Fori(0, count // per) as i:
                for v in range(per):
                    if steps.heads > 1:
                        steps.indices(act, i, v)
                    else:
                        steps.load_low_rows(act, i, v)

        @block.tensor
        def _(pe):
            steps.start_pe(pe)
            with pe.Fori(0, count // per) as i:
                for v in range(per):
                    steps.match(pe, i, v)

        @block.vector
        def _(dve):
            steps.start_dve(dve)
            with dve.Fori(0, count // per) as i:
                steps.one_hot(dve, i, 0)
                for v in range(per):
                    if v + 1 < per:
                        steps.one_hot(dve, i, v + 1)
                    steps.score(dve, i, v)


def project0(nc, c, xnt, cat, values, keys, vals, *args, **kw):
    nb = len(CHUNKS0)
    with Mem(nc) as m, stage(nc, "staged", "used", "multiplied", "by_act", "by_dve", "stored0", "stored1", *ScoreSteps.NAMES) as (
            block, staged, used, multiplied, by_act, by_dve, stored0, stored1, *sems):
        steps = ScoreSteps(m, sems, "es0_", *args, first=0, per=U, **kw)
        stored = (stored0, stored1)
        slot = m.sb("xslot0", [P, 2, DC, P])
        hv = m.sb("hv0", [P, 2, HV])
        acc = m.ps("acc0", [P, nb, 512])
        vrows = values.rearrange("(r t p) d -> t p r d", r=R0, p=P)

        @block.gpsimd
        def _(pool):
            with pool.Fori(0, NT // U) as i:
                for u in range(U):
                    t = i * U + u
                    pool.wait_ge(used, t - before(u, 2) + 1 + CREDIT)
                    pool.tensor_copy(slot[:, u % 2], xnt[:, :, bass.ts(t, P)]).then_inc(staged, 1)
                    steps.gather(pool, i, u)

        @block.tensor
        def _(pe):
            pe.sem_inc(used, CREDIT)
            steps.start_pe(pe)
            with pe.Fori(0, NT // U) as i:
                for u in range(U):
                    t = i * U + u
                    pe.wait_ge(staged, t + 1)
                    pe.wait_ge(by_act, t + CREDIT)
                    pe.wait_ge(by_dve, t + CREDIT)
                    for b, (lo, hi) in enumerate(CHUNKS0):
                        for k in range(DC):
                            last = pe.matmul(acc[:, b, 0:hi - lo], slot[:, u % 2, k, :], cat[:, k, lo:hi],
                                             start=(k == 0), stop=(k == DC - 1))
                        if b < nb - 1:
                            last.then_inc(multiplied, 1)
                    last.then_inc(used, 1)
                    steps.match(pe, i, u)

        @block.scalar
        def _(act):
            act.sem_inc(by_act, CREDIT)
            with act.Fori(0, NT // U) as i:
                for u in range(U):
                    t = i * U + u
                    steps.indices(act, i, u)
                    act.wait_ge(stored[u % 2], earlier(i, u, 2) * 16 + 16)
                    for b in range(2):
                        act.wait_ge(multiplied, t * (nb - 1) + b + 1)
                        last = act.copy(hv[:, u % 2, b * 512:(b + 1) * 512], acc[:, b, :])
                    last.then_inc(by_act, 1)

        @block.vector
        def _(dve):
            dve.sem_inc(by_dve, CREDIT)
            steps.start_dve(dve)
            with dve.Fori(0, NT // U) as i:
                for u in range(U):
                    t = i * U + u
                    steps.one_hot(dve, i, u)
                    dve.wait_ge(stored[u % 2], earlier(i, u, 2) * 16 + 16)
                    for b in range(2, 4):
                        dve.wait_ge(multiplied, t * (nb - 1) + b + 1)
                        dve.tensor_copy(hv[:, u % 2, b * 512:(b + 1) * 512], acc[:, b, :])
                    dve.wait_ge(used, t + 1 + CREDIT)
                    dve.tensor_scalar(keys[:, t, :], acc[:, 4, CK - HV:CV - HV], c.mask[:, bass.ts(t, 1)], None, ALU.add)
                    dve.tensor_copy(vals[:, t, :], acc[:, 4, CV - HV:COLS0 - HV]).then_inc(by_dve, 1)
                    steps.score(dve, i, u)

        @block.sync
        def _(sp):
            for q in stored:
                sp.sem_inc(q, 16)
            with sp.Fori(0, NT // U) as i:
                for u in range(U):
                    t = i * U + u
                    steps.load_rows(sp, i, u)
                    sp.wait_ge(by_act, t + 1 + CREDIT)
                    sp.wait_ge(by_dve, t + 1 + CREDIT)
                    sp.dma_start(vrows[t], hv[:, u % 2, :].rearrange("p (r d) -> p r d", r=R0)).then_inc(stored[u % 2], 16)
            for n, q in enumerate(stored):
                sp.wait_ge(q, 16 + 16 * (NT // U) * len(range(n, U, 2)))


def score_tables0(nc, sc, source_scores, target):
    with Mem(nc) as m, stage(nc, "zeroed", "chain", "stored") as (block, zeroed, chain, stored):
        rest = m.sb("st_rest", [P, NT, R0 * H0])

        @block.sync
        def _(sp):
            for r in range(R0):
                sp.dma_start(source_scores[r * NP:(r + 1) * NP].rearrange("(t p) h -> p t h", p=P),
                             sc[:, :, r * H0:(r + 1) * H0]).then_inc(stored, 16)
            sp.wait_ge(stored, 16 * R0)

        @block.vector
        def _(dve):
            dve.memset(target[:, NT], 0.0)
            split(dve, chain, 0, sc[:, :, R0 * H0:], lambda s: target[:, 0:NT, s, :], rest[:])


def segment_softmax(nc, tag, c, e, heads, channels, scores):
    step = 512 // BLK
    pairs = [(h, q) for h in range(2) for q in range(0, channels, step)]
    with Mem(nc) as m, stage(nc, "turned", "kept", "scanned", "ends", "ends_turned", "rows", "carried", "carry_turned",
                             "carry_kept", "spread", "shifted", "exped", "back_turned", "back_kept") as (
            block, turned, kept, scanned, ends, ends_turned, rows_kept, carried, carry_turned,
            carry_kept, spread, shifted, exped, back_turned, back_kept):
        s = m.sb(tag + "s", [HALF, 2, channels, BLK])
        fwd = m.sb(tag + "fwd", [HALF, 2, heads, BLK])
        top = m.sb(tag + "top", [HALF, 2, heads, BLK])
        tip = m.sb(tag + "tip", [HALF, 2, 2, heads])
        tips = m.sb(tag + "tips", [heads, 2, G])
        inc = m.sb(tag + "inc", [heads, 2, G])
        car = m.sb(tag + "car", [heads, 2, G])
        carg = m.sb(tag + "carg", [HALF, 2, 2, heads])
        turn = m.ps(tag + "turn", [P, 4, 512])
        small = m.ps(tag + "small", [P, 512])
        small2 = m.ps(tag + "small2", [P, 512])

        @block.tensor
        def _(pe):
            for n, (h, q) in enumerate(pairs):
                if n >= 4:
                    pe.wait_ge(kept, n - 3)
                for j in range(step):
                    for k in range(K2):
                        last = pe.transpose(turn[0:HALF, n % 4, j * BLK + k * P:j * BLK + (k + 1) * P],
                                            scores[:, k, h * HALF:(h + 1) * HALF, q + j], c.ident[:])
                last.then_inc(turned, 1)
            pe.wait_ge(ends, 1)
            for d in range(2):
                for h in range(2):
                    last = pe.transpose(small[0:heads, d * G + h * HALF:d * G + (h + 1) * HALF], tip[:, h, d, :],
                                        c.ident[0:HALF, 0:HALF])
            last.then_inc(ends_turned, 1)
            pe.wait_ge(carried, 2)
            for h in range(2):
                for d in range(2):
                    last = pe.transpose(small2[0:HALF, (h * 2 + d) * heads:(h * 2 + d + 1) * heads],
                                        car[:, d, h * HALF:(h + 1) * HALF], c.ident[0:heads, 0:heads])
            last.then_inc(carry_turned, 1)
            pe.wait_ge(kept, len(pairs))
            for n, (h, q) in enumerate(pairs):
                pe.wait_ge(exped, h + 1)
                if n >= 4:
                    pe.wait_ge(back_kept, n - 3)
                for j in range(step):
                    for k in range(K2):
                        last = pe.transpose(turn[:, n % 4, (j * K2 + k) * P:(j * K2 + k) * P + HALF],
                                            s[:, h, q + j, k * P:(k + 1) * P], c.ident[0:HALF, 0:HALF])
                last.then_inc(back_turned, 1)

        @block.scalar
        def _(act):
            for n, (h, q) in enumerate(pairs):
                act.wait_ge(turned, n + 1)
                act.copy(s[:, h, q:q + step, :], turn[0:HALF, n % 4, :].rearrange("p (j e) -> p j e", j=step)).then_inc(kept, 1)
            for h in range(2):
                act.wait_ge(shifted, h + 1)
                act.activation(s[:, h], s[:, h], ACT.Exp, scale=-1.0).then_inc(exped, 1)
            for n, (h, q) in enumerate(pairs):
                act.wait_ge(back_turned, n + 1)
                src = turn[:, n % 4, :].rearrange("p (j k g) -> p j k g", j=step, k=K2)
                for j in range(step):
                    last = act.copy(scores[:, :, h * HALF:(h + 1) * HALF, q + j], src[:, j, :, 0:HALF])
                last.then_inc(back_kept, 1)

        @block.vector
        def _(dve):
            per = len(pairs) // 2
            for h in range(2):
                for q in range(heads):
                    dve.wait_ge(kept, h * per + q // step + 1)
                    dve.tensor_tensor_scan(fwd[:, h, q, :], e.step[:, h, :], s[:, h, q, :], 0.0, ALU.add, ALU.max).then_inc(scanned, 1)
            for h in range(2):
                for q in range(heads):
                    dve.wait_ge(scanned, h * heads + q + 1)
                    dve.tensor_tensor_scan(top[:, h, q, ::-1], e.back[:, h, ::-1], fwd[:, h, q, ::-1], 0.0,
                                           ALU.add, ALU.max).then_inc(scanned, 1)
            dve.wait_ge(scanned, 4 * heads)
            for h in range(2):
                dve.tensor_copy(tip[:, h, 0, :], fwd[:, h, :, BLK - 1])
                last = dve.tensor_copy(tip[:, h, 1, :], top[:, h, :, 0])
            last.then_inc(ends, 1)
            dve.wait_ge(ends_turned, 1)
            dve.tensor_copy(tips[:], small[0:heads, 0:2 * G].rearrange("p (d g) -> p d g", d=2)).then_inc(rows_kept, 1)
            dve.wait_ge(rows_kept, 1)
            dve.tensor_tensor(inc[:, 0, 1:G], tips[:, 0, 0:G - 1], e.cont[0:heads, 1:G], ALU.add)
            dve.tensor_tensor(inc[:, 1, 1:G], tips[:, 1, 1:G], e.cont[0:heads, 1:G], ALU.add)
            dve.memset(car[:, 0, 0:1], NEG)
            dve.memset(car[:, 1, G - 1:G], NEG).then_inc(rows_kept, 1)
            dve.wait_ge(rows_kept, 2)
            dve.tensor_tensor_scan(car[:, 0, 1:G], e.over_prev[0:heads, 1:G], inc[:, 0, 1:G], NEG, ALU.add, ALU.max).then_inc(carried, 1)
            dve.tensor_tensor_scan(car[:, 1, 0:G - 1][:, ::-1], e.over_this[0:heads, 1:G][:, ::-1], inc[:, 1, 1:G][:, ::-1],
                                   NEG, ALU.add, ALU.max).then_inc(carried, 1)
            dve.wait_ge(carry_turned, 1)
            dve.tensor_copy(carg[:], small2[0:HALF, 0:4 * heads].rearrange("p (h d q) -> p h d q", h=2, d=2)).then_inc(carry_kept, 1)
            dve.wait_ge(carry_kept, 1)
            for h in range(2):
                for q in range(heads):
                    dve.scalar_tensor_tensor(out=fwd[:, h, q, :], in0=e.first[:, h, :], scalar=carg[:, h, 0, q:q + 1],
                                             in1=top[:, h, q, :], op0=ALU.add, op1=ALU.max).then_inc(spread, 1)
                for q in range(heads):
                    dve.wait_ge(spread, 2 * heads * h + q + 1)
                    dve.scalar_tensor_tensor(out=top[:, h, q, :], in0=e.last[:, h, :], scalar=carg[:, h, 1, q:q + 1],
                                             in1=fwd[:, h, q, :], op0=ALU.add, op1=ALU.max).then_inc(spread, 1)
                dve.wait_ge(spread, 2 * heads * (h + 1))
                if heads == channels:
                    dve.scalar_tensor_tensor(out=s[:, h].rearrange("p q e -> p (q e)"), in0=top[:, h].rearrange("p q e -> p (q e)"),
                                             scalar=0.0, in1=s[:, h].rearrange("p q e -> p (q e)"),
                                             op0=ALU.max, op1=ALU.subtract).then_inc(shifted, 1)
                else:
                    dve.tensor_tensor(fwd[:, h, 0, :], top[:, h, 0, :], s[:, h, 1, :], ALU.max).then_inc(carry_kept, 1)
                    dve.wait_ge(carry_kept, h + 2)
                    dve.tensor_tensor(s[:, h], fwd[:, h, 0:1, :].broadcast_to([HALF, 2, BLK]), s[:, h], ALU.subtract).then_inc(shifted, 1)


def aggregate(nc, tag, c, e, index, table, heads, weights, extra, acc):
    wide = D + extra
    with Mem(nc) as m, stage(nc, "indexed", "hot", "weighted", "ones", "multiplied", "added", "zeroed", "begun",
                             *(f"gathered{u}" for u in range(U))) as (
            block, indexed, hot, weighted, ones_set, multiplied, added, zeroed, begun, *gathered):
        idx = m.sb(tag + "idx", [P, U, K2], I32)
        rows = m.sb(tag + "rows", [P, U, K2, D])
        one = m.sb(tag + "one", [P, 2, K2, P])
        msg = m.sb(tag + "msg", [P, 2, K2, wide]) if weights is not None else None
        part = m.ps(tag + "part", [P, 2, 512])

        @block.gpsimd
        def _(pool):
            with pool.Fori(0, G // U) as i:
                for u in range(U):
                    pool.wait_ge(indexed, i * U + u + 1)
                    pool.sem_inc(begun, 1)
                    for k in range(K2):
                        pool.indirect_dma_start(rows[:, u, k, :], None, table,
                                                bass.IndirectOffsetOnAxis(idx[:, u, k:k + 1], 0)).then_inc(gathered[u], 16)

        @block.scalar
        def _(act):
            act.wait_ge(zeroed, 1)
            with act.Fori(0, G // U) as i:
                for u in range(U):
                    g = i * U + u
                    act.wait_ge(added, g - U + 1 + CREDIT)
                    act.copy(idx[:, u, :], index[:, :, bass.ts(g, 1)].squeeze(2)).then_inc(indexed, 1)

        @block.tensor
        def _(pe):
            pe.sem_inc(multiplied, CREDIT)
            with pe.Fori(0, G // U) as i:
                for u in range(U):
                    g = i * U + u
                    pe.wait_ge(hot, g + 1)
                    if weights is None:
                        pe.wait_ge(gathered[u], (i + 1) * 16 * K2)
                    else:
                        pe.wait_ge(weighted, g + 1)
                    pe.wait_ge(added, g - before(u, 2) + 1 + CREDIT)
                    for k in range(K2):
                        rhs = rows[:, u, k, :] if weights is None else msg[:, u % 2, k, :]
                        last = pe.matmul(part[:, u % 2, 0:wide], one[:, u % 2, k, :], rhs, start=(k == 0), stop=(k == K2 - 1))
                    last.then_inc(multiplied, 1)

        @block.vector
        def _(dve):
            if weights is not None:
                dve.memset(msg[:], 1.0)
            dve.memset(acc[:], 0.0).then_inc(zeroed, 1)
            dve.wait_ge(zeroed, 1)
            dve.sem_inc(added, CREDIT)

            def prepare(i, u):
                g = i * U + u
                dve.wait_ge(multiplied, g - before(u, 2) + 1 + CREDIT)
                for k in range(K2):
                    last = dve.tensor_scalar(one[:, u % 2, k, :], c.iota[:], e.local[:, k, bass.ts(g, 1)], None, ALU.is_equal)
                last.then_inc(hot, 1)
                if weights is None:
                    return
                dve.wait_ge(gathered[u], (i + 1) * 16 * K2)
                n = weights.shape[3]
                dve.tensor_copy(msg[:, u % 2, :, D:D + n], weights[:, :, g, :])
                for k in range(K2):
                    if heads == 1:
                        last = dve.tensor_scalar(msg[:, u % 2, k, 0:D], rows[:, u, k, :], weights[:, k, g, 0:1], None, ALU.mult)
                    else:
                        last = dve.tensor_tensor(
                            msg[:, u % 2, k, 0:D].rearrange("p (h d) -> p h d", h=heads),
                            rows[:, u, k, :].rearrange("p (h d) -> p h d", h=heads),
                            weights[:, k, g, :].unsqueeze(2).broadcast_to([P, heads, D // heads]), ALU.mult)
                last.then_inc(weighted, 1)

            with dve.Fori(0, G // U) as i:
                for u in range(U):
                    g = i * U + u
                    if u == 0:
                        prepare(i, 0)
                    if u + 1 < U:
                        prepare(i, u + 1)
                    tile = dve.value_load(e.tile[0:1, bass.ts(g, 1)], min_val=0, max_val=NT)
                    dve.wait_ge(multiplied, g + 1 + CREDIT)
                    dve.wait_ge(added, g + CREDIT)
                    dve.tensor_tensor(acc[:, tile, :], acc[:, tile, :], part[:, u % 2, 0:wide], ALU.add).then_inc(added, 1)


def finish_attention0(nc, acc, x, degree):
    with Mem(nc) as m, stage(nc, "chain") as (block, chain):
        den = m.sb("f0_den", [P, NT, H0])
        inv = m.sb("f0_inv", [P, NT, H0])

        @block.vector
        def _(dve):
            dve.tensor_copy(degree[:], acc[:, 0:NT, D + H0])
            dve.tensor_scalar(den[:], acc[:, 0:NT, D:D + H0], 1e-12, None, ALU.add).then_inc(chain, 1)
            dve.wait_ge(chain, 1)
            dve.reciprocal(inv[:], den[:]).then_inc(chain, 1)
            dve.wait_ge(chain, 2)
            v = acc[:, 0:NT, 0:D].rearrange("p t (h d) -> p t h d", h=H0)
            dve.tensor_tensor(v, v, inv[:].unsqueeze(3).broadcast_to([P, NT, H0, D0]), ALU.mult).then_inc(chain, 1)
            dve.wait_ge(chain, 3)
            dve.tensor_tensor(x[:], x[:], acc[:, 0:NT, 0:D], ALU.add)


def project(nc, tag, c, xnt, w, width, out, bias=None, masked=0):
    with Mem(nc) as m, stage(nc, "staged", "multiplied", "kept", "biased") as (block, staged, multiplied, kept, biased):
        slot = m.sb(tag + "slot", [P, 2, DC, P])
        acc = m.ps(tag + "acc", [P, 2, 512])

        @block.gpsimd
        def _(pool):
            with pool.Fori(0, NT // U) as i:
                for u in range(U):
                    t = i * U + u
                    pool.wait_ge(multiplied, t - before(u, 2) + 1 + CREDIT)
                    pool.tensor_copy(slot[:, u % 2], xnt[:, :, bass.ts(t, P)]).then_inc(staged, 1)

        @block.tensor
        def _(pe):
            pe.sem_inc(multiplied, CREDIT)
            with pe.Fori(0, NT // U) as i:
                for u in range(U):
                    t = i * U + u
                    pe.wait_ge(staged, t + 1)
                    pe.wait_ge(kept, t - before(u, 2) + 1 + CREDIT)
                    for k in range(DC):
                        last = pe.matmul(acc[:, u % 2, 0:width], slot[:, u % 2, k, :], w[:, k, :], start=(k == 0),
                                         stop=(k == DC - 1 and bias is None))
                    if bias is not None:
                        last = pe.matmul(acc[:, u % 2, 0:width], c.ones[0:1, :], bias[:], start=False, stop=True)
                    last.then_inc(multiplied, 1)

        @block.vector
        def _(dve):
            dve.sem_inc(kept, CREDIT)
            with dve.Fori(0, NT // U) as i:
                for u in range(U):
                    t = i * U + u
                    dve.wait_ge(multiplied, t + 1 + CREDIT)
                    if masked:
                        last = dve.tensor_scalar(out[:, t, 0:masked], acc[:, u % 2, 0:masked], c.valid[:, bass.ts(t, 1)], None, ALU.mult)
                    if masked < width:
                        last = dve.tensor_copy(out[:, t, masked:width], acc[:, u % 2, masked:width])
                    last.then_inc(kept, 1)


NX = 8
TOP_BIG = 1.0e6


def route(nc, c, logits, one, best):
    with Mem(nc) as m, stage(nc, "chain", "exped") as (block, chain, exped):
        top = m.sb("r_top", [P, NT])
        total = m.sb("r_total", [P, NT])
        inv = m.sb("r_inv", [P, NT])
        rw = m.sb("r_rw", [P, NT, NX])
        same = m.sb("r_same", [P, NT, NX])
        place = m.sb("r_place", [P, NT, NX])
        first = m.sb("r_first", [P, NT])

        def wide(v):
            return v.unsqueeze(2).broadcast_to([P, NT, NX])

        numbers = c.iota[:, 0:NX].unsqueeze(1).broadcast_to([P, NT, NX])

        @block.scalar
        def _(act):
            act.wait_ge(chain, 2)
            act.activation(logits[:], logits[:], ACT.Exp).then_inc(exped, 1)

        @block.vector
        def _(dve):
            done = [0]

            def link(ins):
                done[0] += 1
                ins.then_inc(chain, 1)
                dve.wait_ge(chain, done[0])

            link(dve.tensor_reduce(top[:], logits[:], AX.X, ALU.max))
            link(dve.tensor_tensor(logits[:], logits[:], wide(top[:]), ALU.subtract))
            dve.wait_ge(exped, 1)
            link(dve.tensor_reduce(total[:], logits[:], AX.X, ALU.add))
            link(dve.reciprocal(inv[:], total[:]))
            link(dve.tensor_tensor(rw[:], logits[:], wide(inv[:]), ALU.mult))
            for n in range(2):
                link(dve.tensor_reduce(best[:, n], rw[:], AX.X, ALU.max))
                link(dve.tensor_tensor(same[:], rw[:], wide(best[:, n]), ALU.is_equal))
                link(dve.scalar_tensor_tensor(out=place[:], in0=same[:], scalar=-TOP_BIG, in1=numbers, op0=ALU.mult, op1=ALU.add))
                link(dve.tensor_reduce(first[:], place[:], AX.X, ALU.min))
                link(dve.tensor_scalar(first[:], first[:], TOP_BIG, None, ALU.add))
                link(dve.tensor_tensor(one[:, n], wide(first[:]), numbers, ALU.is_equal))
                if n == 0:
                    link(dve.scalar_tensor_tensor(out=rw[:], in0=one[:, 0], scalar=-4.0, in1=rw[:], op0=ALU.mult, op1=ALU.add))
            link(dve.tensor_tensor(total[:], best[:, 0], best[:, 1], ALU.add))
            link(dve.reciprocal(inv[:], total[:]))
            dve.tensor_tensor(best[:], best[:], inv[:].unsqueeze(1).broadcast_to([P, 2, NT]), ALU.mult)


GM = 256
NG = 2 * N // GM + NX
NSLOT = NG * GM
assert NG % 2 == 0


def place_tokens(nc, c, one, slots, expert):
    with Mem(nc) as m, stage(nc, "chain", "summed") as (block, chain, summed):
        tri = m.sb("pl_tri", [P, P])
        cnt = m.sb("pl_cnt", [P, NT, NX])
        keep = m.sb("pl_keep", [P, NX, NT])
        tot = m.sb("pl_tot", [P, NX, NT])
        cum = m.sb("pl_cum", [P, NX, NT])
        ng1, ng2, cumg, base, gid = (m.sb("pl_" + n, [P, NG]) for n in ("ng1", "ng2", "cumg", "base", "gid"))
        ngi = m.sb("pl_ngi", [P, NX], I32)
        pos = m.sb("pl_pos", [P, NX, NT])
        mine = m.sb("pl_mine", [P, 2, NT, NX])
        row = m.sb("pl_row", [P, 2, NT])
        spare = m.sb("pl_spare", [P, 2, NT])
        less = m.sb("pl_less", [P, NG, NX])
        ps = m.ps("pl_ps", [P, 2, 512])

        @block.tensor
        def _(pe):
            pe.wait_ge(chain, 3)
            flat = cnt[:].rearrange("p t e -> p (t e)")
            pe.matmul(ps[:, 0, 0:NT * NX], tri[:], flat, start=True, stop=True)
            pe.matmul(ps[:, 1, 0:NT * NX], c.ones[:], flat, start=True, stop=True).then_inc(summed, 1)

        @block.vector
        def _(dve):
            done = [0]

            def link(ins):
                done[0] += 1
                ins.then_inc(chain, 1)
                dve.wait_ge(chain, done[0])

            link(dve.tensor_scalar(tri[:], c.iota[:], c.part[:, 0:1], None, ALU.is_gt))
            link(dve.tensor_tensor(cnt[:], one[:, 0], one[:, 1], ALU.add))
            link(dve.tensor_tensor(cnt[:], cnt[:], c.valid[:].unsqueeze(2).broadcast_to([P, NT, NX]), ALU.mult))
            link(dve.memset(keep[:], 1.0))
            link(dve.memset(keep[:, :, 0:1], 0.0))
            dve.wait_ge(summed, 1)
            link(dve.tensor_copy(tot[:], ps[:, 1, 0:NT * NX].rearrange("p (t e) -> p e t", e=NX)))
            link(dve.tensor_tensor_scan(cum[:].rearrange("p e t -> p (e t)"), keep[:].rearrange("p e t -> p (e t)"),
                                        tot[:].rearrange("p e t -> p (e t)"), 0.0, ALU.mult, ALU.add))
            link(dve.tensor_scalar(ng1[:, 0:NX], cum[:, :, NT - 1], float(GM - 1), None, ALU.add))
            link(dve.tensor_copy(ngi[:], ng1[:, 0:NX]))
            link(dve.tensor_scalar(ngi[:], ngi[:], GM.bit_length() - 1, None, ALU.arith_shift_right))
            link(dve.tensor_copy(ng2[:, 0:NX], ngi[:]))
            link(dve.tensor_tensor_scan(cumg[:, 0:NX], c.ones[:, 0:NX], ng2[:, 0:NX], 0.0, ALU.mult, ALU.add))
            link(dve.tensor_tensor(base[:, 0:NX], cumg[:, 0:NX], ng2[:, 0:NX], ALU.subtract))
            link(dve.tensor_scalar(base[:, 0:NX], base[:, 0:NX], float(GM), None, ALU.mult))
            link(dve.tensor_tensor(pos[:], cum[:], tot[:], ALU.subtract))
            link(dve.tensor_tensor(pos[:], pos[:], base[:, 0:NX].unsqueeze(2).broadcast_to([P, NX, NT]), ALU.add))
            link(dve.tensor_tensor(pos[:], pos[:], ps[:, 0, 0:NT * NX].rearrange("p (t e) -> p e t", e=NX), ALU.add))
            for n in range(2):
                link(dve.tensor_tensor(mine[:, n], one[:, n], pos[:].rearrange("p e t -> p t e"), ALU.mult))
            link(dve.tensor_reduce(row[:], mine[:], AX.X, ALU.add))
            for n in range(2):
                link(dve.tensor_scalar(spare[:, n], c.token[:], float(NSLOT - N + n * P), None, ALU.add))
                link(dve.tensor_tensor(row[:, n], row[:, n], spare[:, n], ALU.subtract))
                link(dve.tensor_tensor(row[:, n], row[:, n], c.valid[:], ALU.mult))
                link(dve.tensor_tensor(row[:, n], row[:, n], spare[:, n], ALU.add))
            link(dve.tensor_copy(slots[:], row[:]))
            link(dve.tensor_tensor(less[:], cumg[:, 0:NX].unsqueeze(1).broadcast_to([P, NG, NX]),
                                   c.iota[:, 0:NG].unsqueeze(2).broadcast_to([P, NG, NX]), ALU.is_le))
            link(dve.tensor_reduce(gid[:], less[:], AX.X, ALU.add))
            dve.tensor_scalar(expert[:], gid[:], float(NX - 1), None, ALU.min)


def zero_rows(nc, rows, out_rows):
    with Mem(nc) as m, stage(nc, "zeroed", "stored") as (block, zeroed, stored):
        z = m.sb("z_z", [P, 8, D])

        @block.vector
        def _(dve):
            dve.memset(z[:], 0.0).then_inc(zeroed, 1)

        @block.sync
        def _(sp):
            sp.wait_ge(zeroed, 1)
            for q in range(NSLOT // (8 * P)):
                sp.dma_start(rows[q * 8 * P:(q + 1) * 8 * P].rearrange("(k p) d -> p k d", p=P), z[:]).then_inc(stored, 16)
            sp.dma_start(out_rows[NSLOT:].rearrange("(k p) d -> p k d", p=P), z[:, 0:2]).then_inc(stored, 16)
            sp.wait_ge(stored, 16 * (NSLOT // (8 * P) + 1))


def scatter_tokens(pool, xn, slots, rows, scattered):
    for n in range(2):
        for t in range(NT):
            pool.indirect_dma_start(rows, bass.IndirectOffsetOnAxis(slots[:, n, t:t + 1], 0), xn[:, t, :], None).then_inc(scattered, 16)
    pool.wait_ge(scattered, 16 * 2 * NT)


def run_experts(nc, c, rows, out_rows, expert, w1p, b1p, w2p, b2p, hidden):
    fb = hidden // P
    gt = GM // P
    with Mem(nc) as m, stage(nc, "loaded0", "loaded1", "turned", "kept", "up", "shaped", "down", "out0", "out1",
                             "stored0", "stored1") as (
            block, loaded0, loaded1, turned, kept, up, shaped, down, out0, out1, stored0, stored1):
        loaded, out_made, stored = (loaded0, loaded1), (out0, out1), (stored0, stored1)
        w1 = m.sb("x_w1", [P, 2, DC, hidden])
        w2 = m.sb("x_w2", [P, 2, fb, D])
        b1 = m.sb("x_b1", [P, 2, fb])
        b2 = m.sb("x_b2", [P, 2, D])
        xr = m.sb("x_xr", [P, 2, gt, D])
        xt = m.sb("x_xt", [P, DC, GM])
        hid = m.sb("x_hid", [P, fb, GM])
        y = m.sb("x_y", [P, 2, gt, D])
        turn = m.ps("x_turn", [P, DC, GM])
        up_ps = m.ps("x_up", [P, 3, 512])
        down_ps = m.ps("x_down", [P, gt, 512])

        @block.sync
        def _(sp):
            def load(b, g):
                e = sp.value_load(expert[0:1, bass.ds(g, 1)], min_val=0, max_val=NX - 1)
                sp.dma_start(xr[:, b], rows[bass.ds(g * GM, GM)].rearrange("(k p) d -> p k d", p=P)).then_inc(loaded[b], 16)
                sp.dma_start(w1[:, b], w1p[e].rearrange("(k p) f -> p k f", p=P)).then_inc(loaded[b], 16)
                sp.dma_start(b1[:, b], b1p[e].rearrange("(k p) -> p k", p=P), allow_slow_non_contiguous=True).then_inc(loaded[b], 16)
                sp.dma_start(w2[:, b], w2p[e].rearrange("(k p) f -> p k f", p=P)).then_inc(loaded[b], 16)
                sp.dma_start(b2[:, b], b2p[e].rearrange("(a d) -> a d", a=1).broadcast_to([P, D])).then_inc(loaded[b], 16)

            def save(b, g, i):
                sp.wait_ge(out_made[b], i + 1 + b)
                sp.dma_start(out_rows[bass.ds(g * GM, GM)].rearrange("(k p) d -> p k d", p=P), y[:, b]).then_inc(stored[b], 16)

            for b in range(2):
                sp.sem_inc(stored[b], 16)
                load(b, b)
            with sp.Fori(0, NG // 2 - 1) as i:
                for b in range(2):
                    save(b, i * 2 + b, i)
                    load(b, i * 2 + 2 + b)
            for b in range(2):
                save(b, NG - 2 + b, NG // 2 - 1)
            for b in range(2):
                sp.wait_ge(stored[b], 16 * (NG // 2 + 1))

        @block.tensor
        def _(pe):
            with pe.Fori(0, NG // 2) as i:
                for b in range(2):
                    g = i * 2 + b
                    pe.wait_ge(loaded[b], (i + 1) * 80)
                    pe.wait_ge(kept, g + 1)
                    for k in range(DC):
                        for j in range(gt):
                            last = pe.transpose(turn[:, k, j * P:(j + 1) * P], xr[:, b, j, k * P:(k + 1) * P], c.ident[:])
                    last.then_inc(turned, 1)
                    pe.wait_ge(kept, g + 2)
                    for f in range(fb):
                        pe.wait_ge(shaped, g * fb + f + 1 - before(f, 3, fb) + CREDIT)
                        for k in range(DC):
                            last = pe.matmul(up_ps[:, f % 3, 0:GM], w1[:, b, k, f * P:(f + 1) * P], xt[:, k, :], start=(k == 0), stop=(k == DC - 1))
                        last.then_inc(up, 1)
                    pe.wait_ge(shaped, (g + 1) * fb + CREDIT)
                    for j in range(gt):
                        pe.wait_ge(out_made[1 - b], i + 1)
                        for f in range(fb):
                            last = pe.matmul(down_ps[:, j, 0:D], hid[:, f, j * P:(j + 1) * P], w2[:, b, f, :], start=(f == 0), stop=(f == fb - 1))
                        last.then_inc(down, 1)

        @block.scalar
        def _(act):
            act.sem_inc(kept, 1)
            act.sem_inc(shaped, CREDIT)
            with act.Fori(0, NG // 2) as i:
                for b in range(2):
                    g = i * 2 + b
                    act.wait_ge(turned, g + 1)
                    act.copy(xt[:], turn[:]).then_inc(kept, 1)
                    for f in range(fb):
                        act.wait_ge(up, g * fb + f + 1)
                        act.activation(hid[:, f, :], up_ps[:, f % 3, 0:GM], ACT.Gelu, bias=b1[:, b, f:f + 1]).then_inc(shaped, 1)

        @block.vector
        def _(dve):
            dve.sem_inc(out_made[1], 1)
            with dve.Fori(0, NG // 2) as i:
                for b in range(2):
                    g = i * 2 + b
                    dve.wait_ge(stored[b], (i + 1) * 16)
                    for j in range(gt):
                        dve.wait_ge(down, g * gt + j + 1)
                        last = dve.tensor_tensor(y[:, b, j, :], down_ps[:, j, 0:D], b2[:, b, :], ALU.add)
                    last.then_inc(out_made[b], 1)


def gather_experts(nc, x, slots, best, out_rows):
    depth = 4
    with Mem(nc) as m, stage(nc, "added", *(f"got{s}" for s in range(depth))) as (block, added, *got):
        y = m.sb("y_y", [P, depth, 2, D])

        @block.gpsimd
        def _(pool):
            for t in range(NT):
                if t >= depth:
                    pool.wait_ge(added, 2 * (t - depth + 1))
                for n in range(2):
                    pool.indirect_dma_start(y[:, t % depth, n, :], None, out_rows,
                                            bass.IndirectOffsetOnAxis(slots[:, n, t:t + 1], 0)).then_inc(got[t % depth], 16)

        @block.vector
        def _(dve):
            for t in range(NT):
                dve.wait_ge(got[t % depth], 32 * (t // depth + 1))
                for n in range(2):
                    if n:
                        dve.wait_ge(added, 2 * t + 1)
                    dve.scalar_tensor_tensor(out=x[:, t, :], in0=y[:, t % depth, n, :], scalar=best[:, n, t:t + 1],
                                             in1=x[:, t, :], op0=ALU.mult, op1=ALU.add).then_inc(added, 1)


def mlp(nc, tag, c, xnt, x, act_func, hidden, weights, gate=None, scatter=None):
    fb = hidden // P
    chunk = U * P
    half = chunk // 2
    with Mem(nc) as m, stage(nc, "loaded", "up", "shaped", "down", "added", "biased", "scattered") as (
            block, loaded, up, shaped, down, added, biased, scattered):
        w1 = m.sb(tag + "w1", [P, DC, hidden])
        w2 = m.sb(tag + "w2", [P, fb, D])
        b1 = m.sb(tag + "b1", [P, fb])
        b2 = m.sb(tag + "b2", [P, D])
        hid = m.sb(tag + "hid", [P, fb, chunk])
        up_ps = m.ps(tag + "up", [P, 2, 2, 512])
        down_ps = m.ps(tag + "down", [P, 2, 512])

        @block.gpsimd
        def _(pool):
            if scatter is not None:
                scatter_tokens(pool, *scatter, scattered)

        @block.sync
        def _(sp):
            a1, c1, a2, c2 = weights
            sp.dma_start(w1[:], a1.rearrange("(k p) f -> p k f", p=P)).then_inc(loaded, 16)
            sp.dma_start(b1[:], columns_of(c1), allow_slow_non_contiguous=True).then_inc(loaded, 16)
            sp.dma_start(w2[:], a2.rearrange("(k p) f -> p k f", p=P)).then_inc(loaded, 16)
            sp.dma_start(b2[:], row_of(c2).broadcast_to([P, D])).then_inc(loaded, 16)

        @block.tensor
        def _(pe):
            pe.wait_ge(loaded, 64)
            with pe.Fori(0, NT // U) as j:
                for f in range(fb):
                    pe.wait_ge(shaped, j * fb + f - 2 + 1 + CREDIT)
                    for n in range(2):
                        for k in range(DC):
                            last = pe.matmul(up_ps[:, f % 2, n, 0:half], w1[:, k, f * P:(f + 1) * P],
                                             xnt[:, k, bass.ds(j * chunk + n * half, half)], start=(k == 0), stop=(k == DC - 1))
                    last.then_inc(up, 1)
                pe.wait_ge(shaped, (j + 1) * fb + CREDIT)
                for u in range(U):
                    pe.wait_ge(added, j * U + u - before(u, 2) + 1 + CREDIT)
                    for f in range(fb):
                        last = pe.matmul(down_ps[:, u % 2, 0:D], hid[:, f, u * P:(u + 1) * P], w2[:, f, :],
                                         start=(f == 0), stop=(f == fb - 1))
                    last.then_inc(down, 1)

        @block.scalar
        def _(act):
            act.sem_inc(shaped, CREDIT)
            with act.Fori(0, NT // U) as j:
                for f in range(fb):
                    act.wait_ge(up, j * fb + f + 1)
                    act.activation(hid[:, f, :].rearrange("p (n t) -> p n t", n=2), up_ps[:, f % 2, :, 0:half],
                                   act_func, bias=b1[:, f:f + 1]).then_inc(shaped, 1)

        @block.vector
        def _(dve):
            dve.sem_inc(added, CREDIT)
            dve.wait_ge(loaded, 64)
            with dve.Fori(0, NT // U) as j:
                for u in range(U):
                    t = j * U + u
                    weight = 1.0 if gate is None else gate[:, t, 0:1]
                    dve.scalar_tensor_tensor(out=x[:, t, :], in0=b2[:], scalar=weight,
                                             in1=x[:, t, :], op0=ALU.mult, op1=ALU.add).then_inc(biased, 1)
                    dve.wait_ge(biased, t + 1)
                    dve.wait_ge(down, t + 1)
                    dve.scalar_tensor_tensor(out=x[:, t, :], in0=down_ps[:, u % 2, 0:D], scalar=weight,
                                             in1=x[:, t, :], op0=ALU.mult, op1=ALU.add).then_inc(added, 1)


def load(nc, *pairs):
    with stage(nc, "loaded") as (block, loaded):
        @block.sync
        def _(sp):
            for dst, src in pairs:
                sp.dma_start(dst, src, allow_slow_non_contiguous=True).then_inc(loaded, 16)
            sp.wait_ge(loaded, 16 * len(pairs))


def row_of(v):
    return v.rearrange("(a d) -> a d", a=1)


def columns_of(v):
    return v.rearrange("(k p) -> p k", p=P)


def turn_tokens(nc, tag, c, x, xt):
    with Mem(nc) as m, stage(nc, "staged", "turned", "kept") as (block, staged, turned, kept):
        slot = m.sb(tag + "slot", [P, 2, D])
        turn = m.ps(tag + "turn", [P, 2, 512])

        @block.vector
        def _(dve):
            with dve.Fori(0, NT // U) as i:
                for u in range(U):
                    t = i * U + u
                    dve.wait_ge(turned, t - before(u, 2) + 1 + CREDIT)
                    dve.tensor_copy(slot[:, u % 2, :], x[:, t, :]).then_inc(staged, 1)

        @block.tensor
        def _(pe):
            pe.sem_inc(turned, CREDIT)
            with pe.Fori(0, NT // U) as i:
                for u in range(U):
                    t = i * U + u
                    pe.wait_ge(staged, t + 1)
                    pe.wait_ge(kept, t - before(u, 2) + 1 + CREDIT)
                    for k in range(DC):
                        last = pe.transpose(turn[:, u % 2, k * P:(k + 1) * P], slot[:, u % 2, k * P:(k + 1) * P], c.ident[:])
                    last.then_inc(turned, 1)

        @block.scalar
        def _(act):
            act.sem_inc(kept, CREDIT)
            with act.Fori(0, NT // U) as i:
                for u in range(U):
                    t = i * U + u
                    act.wait_ge(turned, t + 1 + CREDIT)
                    act.copy(xt[:, :, bass.ts(t, P)], turn[:, u % 2, 0:D].rearrange("p (k t) -> p k t", k=DC)).then_inc(kept, 1)


def source_table1(nc, h, degree, dinv, table):
    with Mem(nc) as m, stage(nc, "chain", "rooted", "stored") as (block, chain, rooted, stored):
        deg, root, r0, r1, r2, r3 = (m.sb("d_" + n, [P, NT]) for n in ("deg", "root", "r0", "r1", "r2", "r3"))

        @block.scalar
        def _(act):
            act.wait_ge(chain, 1)
            act.activation(root[:], deg[:], ACT.Sqrt).then_inc(rooted, 1)

        @block.vector
        def _(dve):
            dve.tensor_scalar(deg[:], degree[:], 1.0, None, ALU.add).then_inc(chain, 1)
            dve.wait_ge(rooted, 1)
            dve.reciprocal(r0[:], root[:]).then_inc(chain, 1)
            dve.wait_ge(chain, 2)
            dve.tensor_tensor(r1[:], r0[:], r0[:], ALU.mult).then_inc(chain, 1)
            dve.wait_ge(chain, 3)
            dve.tensor_tensor(r2[:], r1[:], deg[:], ALU.mult).then_inc(chain, 1)
            dve.wait_ge(chain, 4)
            dve.tensor_scalar(r3[:], r2[:], -0.5, 1.5, ALU.mult, ALU.add).then_inc(chain, 1)
            dve.wait_ge(chain, 5)
            dve.tensor_tensor(dinv[:], r0[:], r3[:], ALU.mult).then_inc(chain, 1)
            dve.wait_ge(chain, 6)
            dve.tensor_tensor(h[:], h[:], dinv[:].unsqueeze(2).broadcast_to([P, NT, D]), ALU.mult).then_inc(chain, 1)

        @block.sync
        def _(sp):
            sp.wait_ge(chain, 7)
            sp.dma_start(table.rearrange("(t p) d -> p t d", p=P), h[:]).then_inc(stored, 16)
            sp.wait_ge(stored, 16)


def finish_gcn(nc, acc, h, dinv, bias):
    with stage(nc, "chain") as (block, chain):
        @block.vector
        def _(dve):
            dve.tensor_tensor(h[:], h[:], acc[:, 0:NT, :], ALU.add).then_inc(chain, 1)
            dve.wait_ge(chain, 1)
            dve.tensor_tensor(h[:], h[:], dinv[:].unsqueeze(2).broadcast_to([P, NT, D]), ALU.mult).then_inc(chain, 1)
            dve.wait_ge(chain, 2)
            dve.tensor_tensor(h[:], h[:], bias[:].unsqueeze(1).broadcast_to([P, NT, D]), ALU.add).then_inc(chain, 1)
            dve.wait_ge(chain, 3)
            dve.tensor_scalar(h[:], h[:], 0.0, None, ALU.max)


def tables2(nc, e, h, att, tmp, own, high, target, table):
    with Mem(nc) as m, stage(nc, "chain", "stored", "split_up") as (block, chain, stored, split_up):
        sc = m.sb("t2_sc", [P, 2, NT])
        tgt = m.sb("t2_tgt", [P, NT, 2])
        rest = m.sb("t2_rest", [P, NT])
        rest2 = m.sb("t2_rest2", [P, NT, 2])
        highi = m.sb("t2_highi", [P, K2, G], I32)
        both = m.sb("t2_both", [P, NT])

        @block.vector
        def _(dve):
            dve.memset(target[:, NT], 0.0)
            for s in range(2):
                if s:
                    dve.wait_ge(chain, 2)
                dve.tensor_tensor(tmp[:, 0:NT, 0:D], h[:], att[:, s, :].unsqueeze(1).broadcast_to([P, NT, D]), ALU.mult).then_inc(chain, 1)
                dve.wait_ge(chain, 2 * s + 1)
                dve.tensor_reduce(sc[:, s, :], tmp[:, 0:NT, 0:D], AX.X, ALU.add).then_inc(chain, 1)
            dve.wait_ge(chain, 4)
            dve.tensor_copy(tgt[:, :, 0], sc[:, 1, :])
            dve.tensor_tensor(both[:], sc[:, 0, :], sc[:, 1, :], ALU.add).then_inc(chain, 1)
            dve.wait_ge(chain, 5)
            dve.scalar_tensor_tensor(out=tgt[:, :, 1], in0=both[:], scalar=SLOPE, in1=both[:], op0=ALU.mult, op1=ALU.max).then_inc(chain, 1)
            dve.tensor_scalar(highi[:], e.src[:], P.bit_length() - 1, None, ALU.arith_shift_right).then_inc(chain, 1)
            dve.wait_ge(chain, 7)
            dve.tensor_copy(high[:], highi[:])
            split(dve, split_up, 0, sc[:, 0, :], lambda s: own[:, s, :], rest[:])
            split(dve, split_up, 2 * PARTS - 1, tgt[:], lambda s: target[:, 0:NT, s, :], rest2[:])

        @block.sync
        def _(sp):
            sp.dma_start(table.rearrange("(t p) d -> p t d", p=P), h[:]).then_inc(stored, 16)
            sp.wait_ge(stored, 16)


def finish_gat(nc, acc, h, degree, bias, x):
    with Mem(nc) as m, stage(nc, "chain") as (block, chain):
        some, n, inv_n, own, own2, own3, own4, den, den2, inv = (
            m.sb("fg_" + k, [P, NT]) for k in ("some", "n", "inv_n", "own", "own2", "own3", "own4", "den", "den2", "inv"))

        @block.vector
        def _(dve):
            done = [0]

            def link(ins):
                done[0] += 1
                ins.then_inc(chain, 1)
                dve.wait_ge(chain, done[0])

            def wide(v):
                return v[:].unsqueeze(2).broadcast_to([P, NT, D])

            link(dve.tensor_scalar(some[:], degree[:], 1.0, None, ALU.is_lt))
            link(dve.tensor_scalar(n[:], degree[:], 1.0, None, ALU.max))
            link(dve.reciprocal(inv_n[:], n[:]))
            link(dve.tensor_tensor(own[:], acc[:, 0:NT, D + 1], inv_n[:], ALU.mult))
            link(dve.tensor_tensor(own2[:], own[:], some[:], ALU.add))
            link(dve.tensor_tensor(den[:], acc[:, 0:NT, D], own2[:], ALU.add))
            link(dve.tensor_scalar(den2[:], den[:], 1e-16, None, ALU.add))
            link(dve.reciprocal(inv[:], den2[:]))
            link(dve.tensor_tensor(h[:], h[:], wide(own2), ALU.mult))
            link(dve.tensor_tensor(h[:], h[:], acc[:, 0:NT, 0:D], ALU.add))
            link(dve.tensor_tensor(h[:], h[:], wide(inv), ALU.mult))
            link(dve.tensor_tensor(h[:], h[:], bias[:].unsqueeze(1).broadcast_to([P, NT, D]), ALU.add))
            link(dve.scalar_tensor_tensor(out=x[:].rearrange("p t d -> p (t d)"), in0=h[:].rearrange("p t d -> p (t d)"), scalar=0.0,
                                          in1=x[:].rearrange("p t d -> p (t d)"), op0=ALU.max, op1=ALU.add))


H1, D1 = 4, 64


def channel_attention1(nc, c, kv, wq, bq, g, bias):
    with Mem(nc) as m, stage(nc, "dve_did", "pe_did", "exped") as (block, dve_did, pe_did, exped):
        wqt = m.sb("c_wqt", [P, DC, D])
        high = m.sb("c_high", [P, 1])
        highs = m.sb("c_highs", [P, P])
        own = m.sb("c_own", [P, P])
        off = m.sb("c_off", [P, P])
        att = m.sb("c_att", [P, DC, P])
        att2 = m.sb("c_att2", [P, DC, P])
        top = m.sb("c_top", [P, DC])
        total = m.sb("c_total", [P, DC])
        inv = m.sb("c_inv", [P, DC])
        attt = m.sb("c_attt", [P, DC, P])
        acc = m.ps("c_acc", [P, DC, 512])
        turn = m.ps("c_turn", [P, 512])
        turn2 = m.ps("c_turn2", [P, 512])
        gps = m.ps("c_g", [P, DC, D])
        bps = m.ps("c_b", [1, 512])

        @block.tensor
        def _(pe):
            for q in range(DC):
                for k in range(DC):
                    last = pe.transpose(turn[:, (q * DC + k) * P:(q * DC + k + 1) * P], wq[:, k, q * P:(q + 1) * P], c.ident[:])
            last.then_inc(pe_did, 1)
            for q in range(DC):
                for t in range(NT):
                    last = pe.matmul(acc[:, q, 0:P], kv[:, t, q * P:(q + 1) * P], kv[:, t, D + q * P:D + (q + 1) * P],
                                     start=(t == 0), stop=(t == NT - 1))
            last.then_inc(pe_did, 1)
            pe.wait_ge(dve_did, 6)
            for q in range(DC):
                last = pe.transpose(turn2[:, q * P:(q + 1) * P], att2[:, q, :], c.ident[:])
            last.then_inc(pe_did, 1)
            pe.wait_ge(dve_did, 7)
            for k in range(DC):
                for q in range(DC):
                    pe.matmul(gps[:, k, q * P:(q + 1) * P], wqt[:, q, k * P:(k + 1) * P], attt[:, q, :], start=True, stop=True)
            for q in range(DC):
                last = pe.matmul(bps[:, q * P:(q + 1) * P], bq[:, q:q + 1], attt[:, q, :], start=True, stop=True)
            last.then_inc(pe_did, 1)

        @block.scalar
        def _(act):
            act.wait_ge(dve_did, 4)
            act.activation(att[:], att[:], ACT.Exp).then_inc(exped, 1)

        @block.vector
        def _(dve):
            dve.tensor_scalar(high[:], c.part[:], float(D1), None, ALU.is_ge)
            dve.tensor_scalar(highs[:], c.iota[:], float(D1), None, ALU.is_ge).then_inc(dve_did, 1)
            dve.wait_ge(dve_did, 1)
            dve.tensor_scalar(own[:], highs[:], high[:, 0:1], None, ALU.is_equal).then_inc(dve_did, 1)
            dve.wait_ge(dve_did, 2)
            dve.tensor_scalar(off[:], own[:], -1.0, -NEG, ALU.add, ALU.mult)
            dve.wait_ge(pe_did, 1)
            dve.tensor_copy(wqt[:], turn[:].rearrange("p (q f) -> p q f", q=DC)).then_inc(dve_did, 1)
            dve.wait_ge(pe_did, 2)
            dve.wait_ge(dve_did, 3)
            for q in range(DC):
                last = dve.scalar_tensor_tensor(out=att[:, q, :], in0=acc[:, q, 0:P], scalar=D1 ** -0.5, in1=off[:], op0=ALU.mult, op1=ALU.add)
            last.then_inc(exped, 1)
            dve.wait_ge(exped, 1)
            dve.tensor_reduce(top[:], att[:], AX.X, ALU.max).then_inc(exped, 1)
            dve.wait_ge(exped, 2)
            dve.tensor_tensor(att[:], att[:], top[:].unsqueeze(2).broadcast_to([P, DC, P]), ALU.subtract).then_inc(dve_did, 1)
            dve.wait_ge(exped, 3)
            dve.tensor_reduce(total[:], att[:], AX.X, ALU.add).then_inc(exped, 1)
            dve.wait_ge(exped, 4)
            dve.reciprocal(inv[:], total[:]).then_inc(dve_did, 1)
            dve.wait_ge(dve_did, 5)
            dve.tensor_tensor(att2[:], att[:], inv[:].unsqueeze(2).broadcast_to([P, DC, P]), ALU.mult).then_inc(dve_did, 1)
            dve.wait_ge(pe_did, 3)
            dve.tensor_copy(attt[:], turn2[:, 0:DC * P].rearrange("p (q d) -> p q d", q=DC)).then_inc(dve_did, 1)
            dve.wait_ge(pe_did, 4)
            dve.tensor_copy(g[:], gps[:])
            dve.tensor_copy(bias[:], bps[:, 0:D])


TAKEN = max(1, N // 2) - 1


def select_top(nc, c, w, weights_row, gate):
    with Mem(nc) as m, stage(nc, "chain", "stored", "loaded", "counted", "turned") as (
            block, chain, stored, loaded, counted, turned):
        wide = m.sb("k_wide", [P, NP])
        above = m.sb("k_above", [P, NP])
        clean, cnt, low, cand, ind, scan, excl, pos, pos2, early, less, tie, sel = (
            m.sb("k_" + n, [P, NT]) for n in ("clean", "cnt", "low", "cand", "ind", "scan", "excl", "pos", "pos2", "early", "less", "tie", "sel"))
        best = m.sb("k_best", [P, 1])
        edge1 = m.sb("k_edge1", [1, 1])
        edge = m.sb("k_edge", [P, 1])
        quota = m.sb("k_quota", [P, 1])
        tri = m.sb("k_tri", [P, P])
        tp = m.ps("k_tp", [P, 512])
        bp = m.ps("k_bp", [P, 512])
        pp = m.ps("k_pp", [P, 2, 512])

        @block.sync
        def _(sp):
            sp.wait_ge(chain, 2)
            sp.dma_start(weights_row.rearrange("a (t p) -> p (a t)", p=P), clean[:], allow_slow_non_contiguous=True).then_inc(stored, 16)
            sp.wait_ge(stored, 16)
            sp.dma_start(wide[:], weights_row.broadcast_to([P, NP])).then_inc(loaded, 16)

        @block.tensor
        def _(pe):
            pe.wait_ge(chain, 5)
            pe.transpose(tp[0:1, 0:P], best[:], c.ident[:]).then_inc(turned, 1)
            pe.wait_ge(chain, 6)
            pe.matmul(bp[:, 0:1], c.ones[0:1, :], edge1[:], start=True, stop=True).then_inc(turned, 1)
            pe.wait_ge(chain, 10)
            pe.matmul(pp[:, 0, 0:NT], tri[:], ind[:], start=True, stop=True)
            pe.matmul(pp[:, 1, 0:NT], c.ones[:], ind[:], start=True, stop=True).then_inc(turned, 1)

        @block.vector
        def _(dve):
            done = [0]

            def link(ins):
                done[0] += 1
                ins.then_inc(chain, 1)
                dve.wait_ge(chain, done[0])

            link(dve.tensor_tensor(low[:], w, c.valid[:], ALU.mult))
            link(dve.tensor_tensor(clean[:], low[:], c.mask[:], ALU.add))
            dve.wait_ge(loaded, 16)
            with dve.Fori(0, NT // U) as i:
                for u in range(U):
                    t = i * U + u
                    dve.wait_ge(counted, t + 1)
                    dve.tensor_scalar(above[:], wide[:], clean[:, bass.ts(t, 1)], 0.0, ALU.is_gt, ALU.add,
                                      accum_out=cnt[:, bass.ts(t, 1)]).then_inc(counted, 1)
            dve.wait_ge(counted, NT + 1)
            link(dve.tensor_scalar(low[:], cnt[:], float(TAKEN), None, ALU.is_lt))
            link(dve.scalar_tensor_tensor(out=cand[:], in0=cnt[:], scalar=1.0, in1=low[:], op0=ALU.add, op1=ALU.mult))
            link(dve.tensor_reduce(best[:], cand[:], AX.X, ALU.max))
            dve.wait_ge(turned, 1)
            link(dve.tensor_reduce(edge1[:], tp[0:1, 0:P], AX.X, ALU.max))
            dve.wait_ge(turned, 2)
            link(dve.tensor_scalar(edge[:], bp[:, 0:1], -1.0, None, ALU.add))
            link(dve.tensor_scalar(quota[:], edge[:], -1.0, float(TAKEN), ALU.mult, ALU.add))
            link(dve.tensor_scalar(ind[:], cnt[:], edge[:, 0:1], None, ALU.is_equal))
            link(dve.tensor_scalar(tri[:], c.iota[:], c.part[:, 0:1], None, ALU.is_gt))
            dve.wait_ge(turned, 3)
            link(dve.tensor_tensor_scan(scan[:], c.ones[:, 0:NT], pp[:, 1, 0:NT], 0.0, ALU.mult, ALU.add))
            link(dve.tensor_tensor(excl[:], scan[:], pp[:, 1, 0:NT], ALU.subtract))
            link(dve.tensor_tensor(pos[:], excl[:], pp[:, 0, 0:NT], ALU.add))
            link(dve.tensor_scalar(early[:], pos[:], quota[:, 0:1], None, ALU.is_lt))
            link(dve.tensor_scalar(less[:], cnt[:], edge[:, 0:1], None, ALU.is_lt))
            link(dve.tensor_tensor(tie[:], early[:], ind[:], ALU.mult))
            link(dve.tensor_tensor(sel[:], tie[:], less[:], ALU.add))
            link(dve.tensor_tensor(gate[:], sel[:].unsqueeze(2), w.unsqueeze(2), ALU.mult))

        @block.scalar
        def _(act):
            act.sem_inc(counted, 1)


def add(nc, x, y):
    with stage(nc, "added") as (block, added):
        @block.vector
        def _(dve):
            dve.tensor_tensor(x[:], x[:], y[:], ALU.add)


def store(nc, x, out):
    with stage(nc, "stored") as (block, stored):
        @block.sync
        def _(sp):
            full = (NT - 1) * P
            sp.dma_start(out[0:full].rearrange("(t p) d -> p t d", p=P), x[:, 0:NT - 1, :]).then_inc(stored, 16)
            sp.dma_start(out[full:N], x[0:TAIL, NT - 1, :]).then_inc(stored, 16)
            sp.wait_ge(stored, 32)


def program(nc, a, out):
    packed = nc.dram_tensor("packed", [NB, BLK], I32).ap()
    local_row = nc.dram_tensor("local_row", [G, BLK], BF16).ap()
    low_row = nc.dram_tensor("low_row", [G, BLK], BF16).ap()
    tiles = nc.dram_tensor("tiles", [1, G], I32).ap()
    expert_in = nc.dram_tensor("expert_in", [NSLOT + 2 * P, D], F32).ap()
    expert_out = nc.dram_tensor("expert_out", [NSLOT + 2 * P, D], F32).ap()
    rows1 = nc.dram_tensor("rows1", [NP, D], F32).ap()
    rows2 = nc.dram_tensor("rows2", [NP, D], F32).ap()
    weights_row = nc.dram_tensor("weights_row", [1, NP], F32).ap()
    values = nc.dram_tensor("values0", [R0 * NP, D], F32).ap()
    source_scores = nc.dram_tensor("source_scores0", [R0 * NP, H0], F32).ap()
    with Mem(nc) as m:
        c = Consts(m)
        x = m.sb("x", [P, NT, D])
        xnt = m.sb("xnt", [P, DC, NP])
        e = Edges(m)
        degree = m.sb("degree", [P, NT])
        constants(nc, c, x, a["x"])
        zero_rows(nc, expert_in, expert_out)
        find_groups(nc, c, a, e, packed, tiles, local_row, low_row)
        layer_norm(nc, "ln0_", c, x, xnt)
        with Mem(nc) as m0:
            scores = m0.sb("scores0", [P, K2, G, H0])
            with Mem(nc) as m1:
                target = m1.sb("target0", [P, NT + 1, PARTS, R0 * H0], BF16)
                cat = m1.sb("cat0", [P, DC, CEND])
                g = m1.sb("g0", [P, DC, D])
                bo = m1.sb("bo0", [1, D])
                weights0(nc, c, a, cat)
                load(nc, (bo[:], row_of(a["L0_mix_b_out"])))
                with Mem(nc) as m2:
                    sc = m2.sb("sc0", [P, NT, 2 * R0 * H0])
                    project(nc, "ps_", c, xnt, cat[:, :, CS:CEND], 2 * R0 * H0, sc)
                    score_tables0(nc, sc, source_scores, target)
                args = (c, e, H0, target, scores, local_row)
                kw = dict(index=e.value_row, table=source_scores)
                with Mem(nc) as m2:
                    keys = m2.sb("keys0", [P, NT, P])
                    vals = m2.sb("vals0", [P, NT, P])
                    project0(nc, c, xnt, cat, values, keys, vals, *args, **kw)
                    linear_attention0(nc, c, a, keys, vals, g)
                add_product(nc, "mix0_", xnt, g, bo, c, x, (NT, 2, args, kw))
                done = NT + 2 * (NT // U)
                edge_scores(nc, "es0b_", done, G // U - done, 3, *args, **kw)
            with Mem(nc) as m1:
                acc = m1.sb("acc_0", [P, NT + 1, D + H0 + 1])
                segment_softmax(nc, "sm0_", c, e, H0, H0, scores)
                aggregate(nc, "ag0_", c, e, e.value_row, values, H0, scores, H0 + 1, acc)
                finish_attention0(nc, acc, x, degree)
        with Mem(nc) as m0:
            wr = m0.sb("wr0", [P, DC, NX])
            logits = m0.sb("logits", [P, NT, NX])
            one = m0.sb("one", [P, 2, NT, NX])
            best = m0.sb("best", [P, 2, NT])
            slots = m0.sb("slots", [P, 2, NT], I32)
            expert = m0.sb("expert", [P, NG], I32)
            load(nc, (wr[:], a["L0_ffn_Wr"].rearrange("(k p) e -> p k e", p=P)))
            with Mem(nc) as m1:
                xn = m1.sb("xn0", [P, NT, D])
                layer_norm(nc, "ln1_", c, x, xnt, xn)
                project(nc, "rt_", c, xnt, wr, NX, logits)
                route(nc, c, logits, one, best)
                place_tokens(nc, c, one, slots, expert)
                mlp(nc, "ff0_", c, xnt, x, ACT.Gelu, 1024, tuple(a["L0_ffn_" + n] for n in ("W1s", "b1s", "W2s", "b2s")),
                    scatter=(xn, slots, expert_in))
            run_experts(nc, c, expert_in, expert_out, expert, *(a["L0_ffn_" + n] for n in ("W1p", "b1p", "W2p", "b2p")), 1024)
            gather_experts(nc, x, slots, best, expert_out)
        with Mem(nc) as m0:
            h = m0.sb("h1", [P, NT, D])
            dinv = m0.sb("dinv", [P, NT])
            with Mem(nc) as m1:
                xn = m1.sb("xn1", [P, NT, D])
                layer_norm(nc, "ln2_", c, x, xnt, xn)
                with Mem(nc) as m2:
                    w1 = m2.sb("gw1", [P, DC, D])
                    load(nc, (w1[:], a["L1_gnn_W1"].rearrange("(k p) d -> p k d", p=P)))
                    project(nc, "p1_", c, xnt, w1, D, h)
                    source_table1(nc, h, degree, dinv, rows1)
                with Mem(nc) as m2:
                    wqkv = m2.sb("wqkv1", [P, DC, 3 * D])
                    bkv = m2.sb("bkv1", [1, 2 * D])
                    bq = m2.sb("bq1", [P, DC])
                    kv = m2.sb("kv1", [P, NT, 2 * D])
                    g = m2.sb("g1", [P, DC, D])
                    gb = m2.sb("gb1", [1, D])
                    load(nc, (wqkv[:], a["L1_mix_w_qkv"].rearrange("(k p) j -> p k j", p=P)),
                         (bkv[:], row_of(a["L1_mix_b_qkv"][D:3 * D])), (bq[:], columns_of(a["L1_mix_b_qkv"][0:D])))
                    project(nc, "kv_", c, xnt, wqkv[:, :, D:3 * D], 2 * D, kv, bkv, D)
                    channel_attention1(nc, c, kv, wqkv[:, :, 0:D], bq, g, gb)
                    add_product(nc, "mix1_", xnt, g, gb, c, xn)
                add(nc, x, xn)
                gain = m1.sb("gain1", [P, DC])
                shift = m1.sb("shift1", [P, DC])
                load(nc, (gain[:], columns_of(a["L1_mix_norm_g"])), (shift[:], columns_of(a["L1_mix_norm_b"])))
                layer_norm(nc, "ln3_", c, xn, xnt, None, gain, shift)
            mlp(nc, "ff1_", c, xnt, x, ACT.Gelu, 768, tuple(a["L1_mix_" + n] for n in ("w_fc1", "b_fc1", "w_fc2", "b_fc2")))
            with Mem(nc) as m1:
                acc = m1.sb("acc_1", [P, NT + 1, D])
                bias1 = m1.sb("bias1", [P, D])
                load(nc, (bias1[:], row_of(a["L1_gnn_b1"]).broadcast_to([P, D])))
                aggregate(nc, "ag1_", c, e, e.src, rows1, 0, None, 0, acc)
                finish_gcn(nc, acc, h, dinv, bias1)
                turn_tokens(nc, "tt_", c, h, xnt)
            with Mem(nc) as m1:
                w2 = m1.sb("gw2", [P, DC, D])
                att = m1.sb("att2", [P, 2, D])
                bias2 = m1.sb("bias2", [P, D])
                target = m1.sb("target2", [P, NT + 1, PARTS, 2], BF16)
                own = m1.sb("own2", [P, PARTS, NT], BF16)
                high = m1.sb("high2", [P, K2, G])
                scores = m1.sb("scores2", [P, K2, G, 2])
                acc = m1.sb("acc_2", [P, NT + 1, D + 2])
                load(nc, (w2[:], a["L1_gnn_W2"].rearrange("(k p) d -> p k d", p=P)),
                     (att[:, 0, :], row_of(a["L1_gnn_att_src"]).broadcast_to([P, D])),
                     (att[:, 1, :], row_of(a["L1_gnn_att_dst"]).broadcast_to([P, D])),
                     (bias2[:], row_of(a["L1_gnn_b2"]).broadcast_to([P, D])))
                project(nc, "p2_", c, xnt, w2, D, h)
                tables2(nc, e, h, att, acc, own, high, target, rows2)
                edge_scores(nc, "es2_", 0, G // U, 4, c, e, 1, target, scores, local_row, low_row=low_row, own=own, high=high)
                segment_softmax(nc, "sm2_", c, e, 1, 2, scores)
                aggregate(nc, "ag2_", c, e, e.src, rows2, 1, scores, 2, acc)
                finish_gat(nc, acc, h, degree, bias2, x)
        with Mem(nc) as m0:
            xn = m0.sb("xn2", [P, NT, D])
            wr = m0.sb("wr2", [P, DC, 1])
            br = m0.sb("br2", [1, 1])
            w = m0.sb("w2", [P, NT, 1])
            gate = m0.sb("gate2", [P, NT, 1])
            load(nc, (wr[:], a["L1_ffn_wr"].rearrange("(k p) e -> p k e", p=P)), (br[:], row_of(a["L1_ffn_br"])))
            layer_norm(nc, "ln4_", c, x, xnt, xn)
            project(nc, "pw_", c, xnt, wr, 1, w, br)
            select_top(nc, c, w[:, :, 0], weights_row, gate)
            add(nc, x, xn)
            mlp(nc, "ff2_", c, xnt, x, ACT.Gelu_apprx_tanh, 1024, tuple(a["L1_ffn_" + n] for n in ("w1", "b1", "w2", "b2")), gate)
        store(nc, x, out)


INPUTS = ["x", "src", "dst", "edge_type_8"] + ["L0_gnn_" + n for n in ("W", "attn_src", "attn_dst")] + [
    "L0_mix_" + n for n in ("W_qkv", "W_out", "b_out")] + [
    "L0_ffn_" + n for n in ("Wr", "W1s", "b1s", "W2s", "b2s", "W1p", "b1p", "W2p", "b2p")] + [
    "L1_gnn_" + n for n in ("W1", "b1", "W2", "att_src", "att_dst", "b2")] + [
    "L1_mix_" + n for n in ("w_qkv", "b_qkv", "norm_g", "norm_b", "w_fc1", "b_fc1", "w_fc2", "b_fc2")] + [
    "L1_ffn_" + n for n in ("wr", "br", "w1", "b1", "w2", "b2")]


def kernel(**inputs):
    import numpy as _np
    import concourse.bacc as _bacc
    from concourse import mybir as _mybir
    from concourse.bass_utils import run_bass_kernel_spmd as _run

    nc = _bacc.Bacc("TRN2", target_bir_lowering=False, num_devices=1)
    arrays, args = {}, {}
    for name in INPUTS:
        a = _np.ascontiguousarray(inputs[name])
        arrays[f"in_{name}"] = a
        args[name] = nc.dram_tensor(f"in_{name}", a.shape, _mybir.dt.from_np(a.dtype), kind="ExternalInput").ap()
    out = nc.dram_tensor("out_dram", (N, D), _mybir.dt.float32, kind="ExternalOutput").ap()
    program(nc, args, out)
    r = _run(nc, [arrays], core_ids=[0])
    return r.results[0]["out_dram"]
```

```python
import itertools
from contextlib import ExitStack, contextmanager

import concourse.bass as bass
from concourse import mybir

ALU = mybir.AluOpType
ACT = mybir.ActivationFunctionType
AX = mybir.AxisListType
F32 = mybir.dt.float32
I32 = mybir.dt.int32
BF16 = mybir.dt.bfloat16

P = 128
N = 3125
D = 256
DC = D // P
NT = (N + P - 1) // P
NP = NT * P
TAIL = N - (NT - 1) * P
U = 5
assert NT % U == 0
CREDIT = 5
NEG = -1.0e30
R0, H0, D0 = 8, 8, 32
EPS = 1e-5
STAGES = itertools.count()


def before(u, slots, unroll=U):
    d = 1
    while ((u - d) % unroll) % slots != u % slots:
        d += 1
    return d


def earlier(i, u, slots, unroll=U):
    mine = [v for v in range(unroll) if v % slots == u % slots]
    return i * len(mine) + mine.index(u)


TOGETHER = []


@contextmanager
def together(nc):
    with ExitStack() as memories:
        sems = []
        with nc.Block() as block:
            TOGETHER.append((block, sems, memories))
            yield
            TOGETHER.pop()
        nc.clear_and_free_semaphores(sems)
        nc.all_engine_barrier()


@contextmanager
def stage(nc, *names):
    here = next(STAGES)
    sems = [nc.alloc_semaphore(f"{n}_{here}") for n in names]
    if TOGETHER:
        TOGETHER[-1][1].extend(sems)
        yield (TOGETHER[-1][0], *sems)
        return
    with nc.Block() as block:
        yield (block, *sems)
    nc.clear_and_free_semaphores(sems)
    nc.all_engine_barrier()


class Mem:

    def __init__(self, nc):
        self.nc, self.ctx = nc, ExitStack()

    def __enter__(self):
        return self

    def __exit__(self, *a):
        if TOGETHER:
            TOGETHER[-1][2].enter_context(self.ctx.pop_all())
            return None
        return self.ctx.__exit__(*a)

    def sb(self, name, shape, dt=F32):
        return self.ctx.enter_context(self.nc.sbuf_tensor(name, shape, dt))

    def ps(self, name, shape, dt=F32):
        return self.ctx.enter_context(self.nc.psum_tensor(name, shape, dt))


def constants(nc, c, x, x_in):
    with Mem(nc) as m, stage(nc, "x_zeroed", "x_loaded", "iotas", "chain") as (block, x_zeroed, x_loaded, iotas, chain):
        part = c.part

        @block.gpsimd
        def _(pool):
            pool.iota(c.iota[:], [[1, P]], 0, 0, allow_small_or_imprecise_dtypes=True)
            pool.iota(part[:], [[0, 1]], 0, 1, allow_small_or_imprecise_dtypes=True)
            pool.iota(c.head[:], [[P, DC], [-D0, H0]], 0, 1, allow_small_or_imprecise_dtypes=True)
            pool.iota(c.token[:], [[P, NT]], 0, 1, allow_small_or_imprecise_dtypes=True).then_inc(iotas, 1)

        @block.sync
        def _(sp):
            full = (NT - 1) * P
            sp.dma_start(x[:, 0:NT - 1, :], x_in[0:full].rearrange("(t p) d -> p t d", p=P)).then_inc(x_loaded, 16)
            sp.wait_ge(x_zeroed, 1)
            sp.dma_start(x[0:TAIL, NT - 1, :], x_in[full:N]).then_inc(x_loaded, 16)
            sp.wait_ge(x_loaded, 32)

        @block.vector
        def _(dve):
            dve.memset(x[:, NT - 1, :], 0.0).then_inc(x_zeroed, 1)
            dve.memset(c.ones[:], 1.0)
            dve.wait_ge(iotas, 1)
            dve.tensor_scalar(c.ident[:], c.iota[:], part[:, 0:1], None, ALU.is_equal)
            dve.tensor_scalar(c.valid[:], c.token[:], float(N), None, ALU.is_lt).then_inc(chain, 1)
            dve.tensor_scalar(c.headge[:], c.head[:], 0.0, None, ALU.is_ge).then_inc(chain, 1)
            dve.wait_ge(chain, 2)
            dve.tensor_scalar(c.mask[:], c.valid[:], -1.0, -NEG, ALU.add, ALU.mult)
            dve.scalar_tensor_tensor(out=c.head32[:], in0=c.head[:], scalar=float(D0), in1=c.headge[:],
                                     op0=ALU.is_lt, op1=ALU.mult)


class Consts:
    def __init__(self, m):
        self.part = m.sb("part", [P, 1])
        self.iota = m.sb("iota", [P, P])
        self.head = m.sb("head", [P, DC, H0])
        self.headge = m.sb("headge", [P, DC, H0])
        self.head32 = m.sb("head32", [P, DC, H0])
        self.token = m.sb("token", [P, NT])
        self.valid = m.sb("valid", [P, NT])
        self.mask = m.sb("mask", [P, NT])
        self.ones = m.sb("ones", [P, P])
        self.ident = m.sb("ident", [P, P])


def layer_norm(nc, tag, c, x, xnt, xn=None, gain=None, bias=None):
    with Mem(nc) as m, stage(nc, *(tag + n for n in (
            "stats", "moments", "std", "rstd", "normed", "turned", "kept", "evacuated"))) as (
            block, stats, moments, std, rstd, normed, turned, kept, evacuated):
        st = m.sb(tag + "st", [P, NT, 6])
        mean2, mean, gap, gap2, m2, var, vareps, sd, r0, r1, r2, r3, rs = (
            m.sb(tag + n, [P, NT]) for n in ("mean2", "mean", "gap", "gap2", "m2", "var", "vareps", "sd", "r0", "r1", "r2", "r3", "rs"))
        slot = m.sb(tag + "slot", [P, U, D])
        turn = m.ps(tag + "turn", [P, U, 512])

        @block.vector
        def _(dve):
            with dve.Fori(0, NT // U) as i:
                for u in range(U):
                    dve.bn_stats(st[:, i * U + u, :], x[:, i * U + u, :]).then_inc(stats, 1)
            dve.wait_ge(stats, NT)
            dve.tensor_tensor(mean2[:], st[:, :, 1], st[:, :, 4], ALU.add).then_inc(moments, 1)
            dve.tensor_tensor(gap[:], st[:, :, 1], st[:, :, 4], ALU.subtract).then_inc(moments, 1)
            dve.tensor_tensor(m2[:], st[:, :, 2], st[:, :, 5], ALU.add).then_inc(moments, 1)
            dve.wait_ge(moments, 3)
            dve.tensor_scalar(mean[:], mean2[:], 0.5, None, ALU.mult).then_inc(moments, 1)
            dve.scalar_tensor_tensor(out=gap2[:], in0=gap[:], scalar=D / 4.0, in1=gap[:],
                                     op0=ALU.mult, op1=ALU.mult).then_inc(moments, 1)
            dve.wait_ge(moments, 5)
            dve.tensor_tensor(var[:], gap2[:], m2[:], ALU.add).then_inc(moments, 1)
            dve.wait_ge(moments, 6)
            dve.tensor_scalar(vareps[:], var[:], 1.0 / D, EPS, ALU.mult, ALU.add).then_inc(moments, 1)
            dve.wait_ge(std, 1)
            dve.reciprocal(r0[:], sd[:]).then_inc(moments, 1)
            dve.wait_ge(moments, 8)
            dve.tensor_tensor(r1[:], r0[:], r0[:], ALU.mult).then_inc(moments, 1)
            dve.wait_ge(moments, 9)
            dve.tensor_tensor(r2[:], r1[:], vareps[:], ALU.mult).then_inc(moments, 1)
            dve.wait_ge(moments, 10)
            dve.tensor_scalar(r3[:], r2[:], -0.5, 1.5, ALU.mult, ALU.add).then_inc(moments, 1)
            dve.wait_ge(moments, 11)
            dve.tensor_tensor(rs[:], r0[:], r3[:], ALU.mult).then_inc(rstd, 1)
            dve.wait_ge(rstd, 1)
            with dve.Fori(0, NT // U) as i:
                for u in range(U):
                    t = i * U + u
                    dve.wait_ge(turned, t - U + 1 + CREDIT)
                    if xn is not None:
                        dve.wait_ge(kept, t - U + 1 + CREDIT)
                    dve.tensor_scalar(slot[:, u, :], x[:, t, :], mean[:, bass.ts(t, 1)], rs[:, bass.ts(t, 1)],
                                      ALU.subtract, ALU.mult).then_inc(normed, 1)

        @block.tensor
        def _(pe):
            pe.sem_inc(turned, CREDIT)
            with pe.Fori(0, NT // U) as i:
                for u in range(U):
                    t = i * U + u
                    pe.wait_ge(normed, t + 1)
                    pe.wait_ge(evacuated, t - U + 1 + CREDIT)
                    for k in range(DC):
                        last = pe.transpose(turn[:, u, k * P:(k + 1) * P], slot[:, u, k * P:(k + 1) * P], c.ident[:])
                    last.then_inc(turned, 1)

        @block.scalar
        def _(act):
            act.wait_ge(moments, 7)
            act.activation(sd[:], vareps[:], ACT.Sqrt).then_inc(std, 1)
            act.sem_inc(evacuated, CREDIT)
            if xn is not None:
                act.sem_inc(kept, CREDIT)
            with act.Fori(0, NT // U) as i:
                for u in range(U):
                    t = i * U + u
                    if xn is not None:
                        act.wait_ge(normed, t + 1)
                        act.copy(xn[:, t, :], slot[:, u, :]).then_inc(kept, 1)
                    act.wait_ge(turned, t + 1 + CREDIT)
                    for k in range(DC):
                        dst = xnt[:, k, bass.ts(t, P)]
                        src = turn[:, u, k * P:(k + 1) * P]
                        if gain is None:
                            last = act.copy(dst, src)
                        else:
                            last = act.activation(dst, src, ACT.Identity, scale=gain[:, k:k + 1], bias=bias[:, k:k + 1])
                    last.then_inc(evacuated, 1)


HV = R0 * D
CK, CV, CS = HV, HV + P, HV + 2 * P
COLS0 = CS
CT, CEND = CS + R0 * H0, CS + 2 * R0 * H0
CHUNKS0 = [(lo, min(lo + 512, COLS0)) for lo in range(0, COLS0, 512)]


def weights0(nc, c, a, cat):
    with Mem(nc) as m, stage(nc, "w_loaded", "av_loaded", "kv_loaded", "blocked", "turned", "kept", "scored") as (
            block, w_loaded, av_loaded, kv_loaded, blocked, turned, kept, scored):
        w = m.sb("w0", [P, R0 * DC, D])
        av = m.sb("av0", [P, 2, DC])
        heads = m.sb("heads0", [P, DC, 2, H0])
        turn = m.ps("turn0", [P, 2, 512])
        score = m.ps("score0", [P, DC, R0, 2 * H0])

        @block.sync
        def _(sp):
            sp.dma_start(w[:], a["L0_gnn_W"].rearrange("r o f -> (r o) f").rearrange("(q p) f -> p q f", p=P)).then_inc(w_loaded, 16)
            for s, n in enumerate(("attn_src", "attn_dst")):
                sp.dma_start(av[:, s, :], a["L0_gnn_" + n].rearrange("h d -> (h d)").rearrange("(k p) -> p k", p=P),
                             allow_slow_non_contiguous=True).then_inc(av_loaded, 16)
            sp.dma_start(cat[:, :, CK:CS], a["L0_mix_W_qkv"].rearrange("(k p) j -> p k j", p=P)[:, :, P:3 * P]).then_inc(kv_loaded, 16)
            sp.wait_ge(kv_loaded, 16)

        @block.vector
        def _(dve):
            dve.wait_ge(av_loaded, 32)
            for k in range(DC):
                for s in range(2):
                    dve.tensor_scalar(heads[:, k, s, :], c.head32[:, k, :], av[:, s, k:k + 1], None,
                                      ALU.mult).then_inc(blocked, 1)
            dve.wait_ge(scored, 1)
            for k in range(DC):
                for s in range(2):
                    dst = cat[:, k, CS + s * R0 * H0:CS + (s + 1) * R0 * H0].rearrange("p (r h) -> p r h", h=H0)
                    dve.tensor_copy(dst, score[:, k, :, s * H0:(s + 1) * H0])

        @block.tensor
        def _(pe):
            pe.wait_ge(w_loaded, 16)
            for r in range(R0):
                if r >= 2:
                    pe.wait_ge(kept, r - 1)
                for k in range(DC):
                    for o in range(DC):
                        last = pe.transpose(turn[:, r % 2, (k * DC + o) * P:(k * DC + o + 1) * P],
                                            w[:, r * DC + o, k * P:(k + 1) * P], c.ident[:])
                last.then_inc(turned, 1)
            pe.wait_ge(blocked, 2 * DC)
            for r in range(R0):
                for k in range(DC):
                    for o in range(DC):
                        last = pe.matmul(score[:, k, r, :], w[:, r * DC + o, k * P:(k + 1) * P],
                                         heads[:, o, :, :].rearrange("p s h -> p (s h)"), start=(o == 0), stop=(o == DC - 1))
            last.then_inc(scored, 1)

        @block.scalar
        def _(act):
            for r in range(R0):
                act.wait_ge(turned, r + 1)
                act.copy(cat[:, :, r * D:(r + 1) * D], turn[:, r % 2, :].rearrange("p (k o) -> p k o", k=DC)).then_inc(kept, 1)


def linear_attention0(nc, c, a, keys, vals, g):
    scale = 32 ** -0.5
    with Mem(nc) as m, stage(nc, "loaded", "dve_did", "pe_did", "act_did", "exped") as (
            block, loaded, dve_did, pe_did, act_did, exped):
        wq = m.sb("wq0", [P, DC, P])
        wqt = m.sb("wqt0", [P, DC, P])
        wo = m.sb("wo0", [P, D])
        part_max = m.sb("pmax0", [P, P])
        col_max = m.sb("cmax0", [P, 1])
        diag = m.sb("diag0", [P, P])
        max_row = m.sb("maxrow0", [P, P])
        inv = m.sb("inv0", [P, P])
        ctx = m.sb("ctx0", [P, P])
        ctx2 = m.sb("ctxs0", [P, P])
        mo = m.sb("mo0", [P, D])
        turn = m.ps("mt0", [P, 512])
        rows = m.ps("mr0", [P, 512])
        ctx_ps = m.ps("mc0", [P, 512])
        sum_ps = m.ps("ms0", [P, 512])
        mo_ps = m.ps("mm0", [P, 512])
        g_ps = m.ps("mg0", [P, DC, D])

        @block.sync
        def _(sp):
            sp.dma_start(wq[:], a["L0_mix_W_qkv"].rearrange("(k p) j -> p k j", p=P)[:, :, 0:P]).then_inc(loaded, 16)
            sp.dma_start(wo[:], a["L0_mix_W_out"]).then_inc(loaded, 16)

        @block.vector
        def _(dve):
            dve.tensor_reduce(part_max[:], keys[:].rearrange("p t d -> p d t"), AX.X, ALU.max).then_inc(dve_did, 1)
            dve.wait_ge(pe_did, 1)
            dve.tensor_reduce(col_max[:], turn[:, 0:P], AX.X, ALU.max).then_inc(dve_did, 1)
            dve.wait_ge(dve_did, 2)
            dve.tensor_scalar(diag[:], c.ident[:], col_max[:, 0:1], None, ALU.mult).then_inc(dve_did, 1)
            dve.wait_ge(pe_did, 2)
            dve.tensor_copy(max_row[:], rows[:, 0:P]).then_inc(dve_did, 1)
            dve.wait_ge(dve_did, 4)
            dve.tensor_tensor(keys[:], keys[:], max_row[:].unsqueeze(1).broadcast_to([P, NT, P]), ALU.subtract).then_inc(dve_did, 1)
            dve.wait_ge(pe_did, 4)
            dve.reciprocal(inv[:], sum_ps[:, 0:P]).then_inc(dve_did, 1)
            dve.wait_ge(dve_did, 6)
            dve.scalar_tensor_tensor(out=ctx[:], in0=ctx_ps[:, 0:P], scalar=scale, in1=inv[:], op0=ALU.mult, op1=ALU.mult).then_inc(dve_did, 1)
            dve.wait_ge(dve_did, 7)
            dve.tensor_tensor(ctx2[:].rearrange("p (h d) -> p h d", d=32), ctx[:].rearrange("p (h d) -> p h d", d=32),
                              c.head32[:, 0, 0:4].unsqueeze(2).broadcast_to([P, 4, 32]), ALU.mult).then_inc(dve_did, 1)
            dve.wait_ge(pe_did, 5)
            dve.tensor_copy(mo[:], mo_ps[:, 0:D]).then_inc(dve_did, 1)
            dve.wait_ge(pe_did, 6)
            dve.tensor_copy(g[:], g_ps[:])

        @block.scalar
        def _(act):
            act.wait_ge(pe_did, 3)
            act.copy(wqt[:], turn[:, P:P + DC * P].rearrange("p (k f) -> p k f", k=DC)).then_inc(act_did, 1)
            act.wait_ge(dve_did, 5)
            act.activation(keys[:], keys[:], ACT.Exp).then_inc(exped, 1)

        @block.tensor
        def _(pe):
            pe.wait_ge(dve_did, 1)
            pe.transpose(turn[:, 0:P], part_max[:], c.ident[:]).then_inc(pe_did, 1)
            pe.wait_ge(dve_did, 3)
            pe.matmul(rows[:, 0:P], c.ones[:], diag[:], start=True, stop=True).then_inc(pe_did, 1)
            pe.wait_ge(loaded, 32)
            for k in range(DC):
                last = pe.transpose(turn[:, (k + 1) * P:(k + 2) * P], wq[:, k, :], c.ident[:])
            last.then_inc(pe_did, 1)
            pe.wait_ge(exped, 1)
            for t in range(NT):
                pe.matmul(sum_ps[:, 0:P], c.ones[:], keys[:, t, :], start=(t == 0), stop=(t == NT - 1))
                last = pe.matmul(ctx_ps[:, 0:P], vals[:, t, :], keys[:, t, :], start=(t == 0), stop=(t == NT - 1))
            last.then_inc(pe_did, 1)
            pe.wait_ge(dve_did, 8)
            pe.matmul(mo_ps[:, 0:D], ctx2[:], wo[:], start=True, stop=True).then_inc(pe_did, 1)
            pe.wait_ge(dve_did, 9)
            pe.wait_ge(act_did, 1)
            for k in range(DC):
                last = pe.matmul(g_ps[:, k, :], wqt[:, k, :], mo[:], start=True, stop=True)
            last.then_inc(pe_did, 1)


def steps_beside(ride, m, sems, tag):
    return None if ride is None else ride[0](m, sems, tag, *ride[1], **ride[2])


def names_beside(ride):
    return () if ride is None else ride[0].NAMES


def beside(steps, point, points):
    return () if steps is None else range(point * steps.per // points, (point + 1) * steps.per // points)


def dve_beside(steps, dve, i, point, points):
    here = beside(steps, point, points)
    for v in here:
        if v == 0:
            steps.prepare(dve, i, v)
        if v + 1 < steps.per:
            steps.prepare(dve, i, v + 1)
        steps.finish(dve, i, v)


def add_product(nc, tag, xnt, g, bias, c, x, ride=None):
    with Mem(nc) as m, stage(nc, "staged", "multiplied", "added", *names_beside(ride)) as (block, staged, multiplied, added, *sems):
        slot = m.sb(tag + "slot", [P, U, DC, P])
        acc = m.ps(tag + "acc", [P, U, 512])
        steps = steps_beside(ride, m, sems, tag)

        @block.sync
        def _(sp):
            if steps is not None and steps.loads:
                with sp.Fori(0, NT // U) as i:
                    for v in range(steps.per):
                        steps.load_rows(sp, i, v)

        @block.gpsimd
        def _(pool):
            if steps is not None and steps.gathers:
                steps.start_pool(pool)
                with pool.Fori(0, NT // U) as i:
                    for v in range(steps.per):
                        steps.gather(pool, i, v)

        @block.scalar
        def _(act):
            with act.Fori(0, NT // U) as i:
                for u in range(U):
                    t = i * U + u
                    act.wait_ge(multiplied, t - U + 1 + CREDIT)
                    act.copy(slot[:, u], xnt[:, :, bass.ts(t, P)]).then_inc(staged, 1)

        @block.tensor
        def _(pe):
            pe.sem_inc(multiplied, CREDIT)
            if steps is not None:
                steps.start_pe(pe)
            with pe.Fori(0, NT // U) as i:
                for u in range(U):
                    t = i * U + u
                    pe.wait_ge(staged, t + 1)
                    pe.wait_ge(added, t - U + 1 + CREDIT)
                    for k in range(DC):
                        pe.matmul(acc[:, u, 0:D], slot[:, u, k, :], g[:, k, :], start=(k == 0), stop=False)
                    pe.matmul(acc[:, u, 0:D], c.ones[0:1, :], bias[:], start=False, stop=True).then_inc(multiplied, 1)
                    for v in beside(steps, u, U):
                        steps.match(pe, i, v)

        @block.vector
        def _(dve):
            dve.sem_inc(added, CREDIT)
            if steps is not None:
                steps.start_dve(dve)
            with dve.Fori(0, NT // U) as i:
                for u in range(U):
                    t = i * U + u
                    for v in beside(steps, u, U):
                        steps.prepare(dve, i, v)
                    dve.wait_ge(multiplied, t + 1 + CREDIT)
                    dve.tensor_tensor(x[:, t, :], x[:, t, :], acc[:, u, 0:D], ALU.add).then_inc(added, 1)
                    for v in beside(steps, u, U):
                        steps.finish(dve, i, v)


E = 50000
BLK = 256
NB = (E + BLK - 1) // BLK
G = NB + NT - 1
K2 = BLK // P
HALF = G // 2
assert G == 2 * HALF and HALF % U == 0 and HALF <= P
FAR = 4095
LOW = 24
BH = NB // 2


class Edges:

    def __init__(self, m):
        self.src = m.sb("e_src", [P, K2, G], I32)
        self.value_row = m.sb("e_row", [P, K2, G], I32)
        self.local = m.sb("e_local", [P, K2, G])
        self.rel = m.sb("e_rel", [P, K2, G])
        self.step = m.sb("e_step", [HALF, 2, BLK])
        self.back = m.sb("e_back", [HALF, 2, BLK])
        self.first = m.sb("e_first", [HALF, 2, BLK])
        self.last = m.sb("e_last", [HALF, 2, BLK])
        self.cont = m.sb("e_cont", [H0, G])
        self.over_prev = m.sb("e_over_prev", [H0, G])
        self.over_this = m.sb("e_over_this", [H0, G])
        self.tile = m.sb("e_tile", [1, G], I32)


def find_groups(nc, c, a, e, packed, tiles, local_row, low_row):
    with Mem(nc) as m, stage(nc, "zeroed", "loaded", "iotas", "packed", "stored", "counted", "chain",
                             "fetched", "tiles_out", "tiles_in", "turned", "kept", "brows", "rows_out") as (
            block, zeroed, loaded, iotas, packed_up, stored, counted, chain, fetched, tiles_out, tiles_in, turned, kept,
            brows, rows_out):
        raw = m.sb("g_raw", [BH, 3, 2, BLK], I32)
        sh = m.sb("g_sh", [BH, 2, 2, BLK], I32)
        pk = m.sb("g_pk", [BH, 2, BLK], I32)
        dstf = m.sb("g_dstf", [BH, 2, BLK])
        junk = m.sb("g_junk", [BH, 2, BLK])
        cnt = m.sb("g_cnt", [BH, NT + 1])
        off = m.sb("g_off", [P, NT + 1])
        offm = m.sb("g_offm", [P, 2, NT])
        offi = m.sb("g_offi", [P, 2, NT], I32)
        blki = m.sb("g_blki", [P, 2, NT], I32)
        blk = m.sb("g_blk", [P, 2, NT])
        some = m.sb("g_some", [P, NT])
        span = m.sb("g_span", [P, NT])
        num = m.sb("g_num", [P, NT])
        cum = m.sb("g_cum", [P, NT])
        base = m.sb("g_base", [P, NT])
        base2 = m.sb("g_base2", [P, NT])
        gid = m.sb("g_gid", [P, 2])
        tid = m.sb("g_tid", [P, NT])
        cmp = m.sb("g_cmp", [P, 2, NT])
        cmp2 = m.sb("g_cmp2", [P, 2, NT])
        cmp3 = m.sb("g_cmp3", [P, 2, NT])
        tile = m.sb("g_tile", [P, 2])
        rowf = m.sb("g_rowf", [P, 2])
        rowf2 = m.sb("g_rowf2", [P, 2])
        row = m.sb("g_row", [P, 2], I32)
        tilei = m.sb("g_tilei", [P, 2], I32)
        got = m.sb("g_got", [HALF, 2, BLK], I32)
        bits = m.sb("g_bits", [HALF, 3, 2, BLK], I32)
        f = m.sb("g_f", [HALF, 3, 2, BLK])
        lowi = m.sb("g_lowi", [HALF, 2, BLK], I32)
        brow = m.sb("g_brow", [HALF, 2, 2, BLK], BF16)
        vrow = m.sb("g_vrow", [HALF, 2, BLK])
        loc = m.sb("g_loc", [HALF, 2, BLK])
        ok0 = m.sb("g_ok0", [HALF, 2, BLK])
        ok = m.sb("g_ok", [HALF, 2, BLK])
        key0 = m.sb("g_key0", [HALF, 2, BLK])
        key = m.sb("g_key", [HALF, 2, BLK])
        tile128 = m.sb("g_t128", [P, 2])
        edge = m.sb("g_edge", [HALF, 2, BLK])
        runs = m.sb("g_runs", [HALF, 2])
        rep = m.sb("g_rep", [HALF, 2, 3, H0])
        rows = m.sb("g_rows", [H0, 3, G])
        same = m.sb("g_same", [H0, G])
        prev = m.sb("g_prev", [H0, G])
        this = m.sb("g_this", [H0, G])
        total = m.ps("g_total", [P, 512])
        turn = m.ps("g_turn", [P, 4, 512])
        trow = m.ps("g_trow", [P, 3, 512])

        @block.sync
        def _(sp):
            sp.wait_ge(zeroed, 1)
            cut = BH * BLK
            for n, name in enumerate(("src", "dst", "edge_type_8")):
                v = a[name]
                sp.dma_start(raw[:, n, 0, :], v[0:cut].rearrange("(b e) -> b e", e=BLK)).then_inc(loaded, 16)
                sp.dma_start(raw[0:BH - 1, n, 1, :], v[cut:(NB - 1) * BLK].rearrange("(b e) -> b e", e=BLK)).then_inc(loaded, 16)
                sp.dma_start(raw[BH - 1:BH, n, 1, 0:E - (NB - 1) * BLK],
                             v[(NB - 1) * BLK:E].rearrange("(b e) -> b e", b=1)).then_inc(loaded, 16)
            sp.wait_ge(packed_up, 1)
            for h in range(2):
                sp.dma_start(packed[h * BH:(h + 1) * BH], pk[:, h, :]).then_inc(stored, 16)
            sp.wait_ge(chain, 18)
            for h in range(2):
                sp.dma_start(tiles[0, h * HALF:(h + 1) * HALF].rearrange("(g a) -> g a", a=1), tilei[0:HALF, h:h + 1],
                             allow_slow_non_contiguous=True).then_inc(tiles_out, 16)
            sp.wait_ge(tiles_out, 32)
            sp.dma_start(e.tile[:], tiles).then_inc(tiles_in, 16)
            sp.wait_ge(tiles_in, 16)
            sp.wait_ge(brows, 2)
            for h in range(2):
                sp.dma_start(low_row[h * HALF:(h + 1) * HALF], brow[:, 0, h, :]).then_inc(rows_out, 16)
                sp.dma_start(local_row[h * HALF:(h + 1) * HALF], brow[:, 1, h, :]).then_inc(rows_out, 16)
            sp.wait_ge(rows_out, 64)

        @block.gpsimd
        def _(pool):
            pool.iota(gid[:], [[HALF, 2]], 0, 1, allow_small_or_imprecise_dtypes=True)
            pool.iota(tid[:], [[1, NT]], 0, 0, allow_small_or_imprecise_dtypes=True).then_inc(iotas, 1)
            pool.wait_ge(stored, 32)
            pool.wait_ge(chain, 17)
            for h in range(2):
                pool.indirect_dma_start(got[:, h, :], None, packed, bass.IndirectOffsetOnAxis(row[0:HALF, h:h + 1], 0)).then_inc(fetched, 16)

        @block.tensor
        def _(pe):
            pe.wait_ge(counted, NT + 1)
            pe.matmul(total[:, 0:NT + 1], c.ones[0:BH, :], cnt[:], start=True, stop=True).then_inc(turned, 1)
            for q, (n, src) in enumerate(((22, f[:, 0]), (23, vrow), (24, loc), (22, f[:, 2]))):
                pe.wait_ge(chain, n)
                for h in range(2):
                    for k in range(K2):
                        last = pe.transpose(turn[:, q, (h * K2 + k) * P:(h * K2 + k) * P + HALF],
                                            src[:, h, k * P:(k + 1) * P], c.ident[0:HALF, 0:HALF])
                last.then_inc(turned, 1)
            pe.wait_ge(chain, 35)
            for q in range(3):
                for h in range(2):
                    last = pe.transpose(trow[0:H0, q, h * HALF:(h + 1) * HALF], rep[:, h, q, :], c.ident[0:HALF, 0:HALF])
            last.then_inc(turned, 1)

        @block.scalar
        def _(act):
            def spread(q):
                return turn[:, q, :].rearrange("p (h k g) -> p h k g", h=2, k=K2)[:, :, :, 0:HALF]
            for q, dst in enumerate((e.src, e.value_row, e.local, e.rel)):
                act.wait_ge(turned, q + 2)
                act.copy(dst[:].rearrange("p k (h g) -> p h k g", h=2), spread(q))
            act.wait_ge(turned, 6)
            act.copy(rows[:], trow[0:H0, :, 0:G]).then_inc(kept, 1)

        @block.vector
        def _(dve):
            done = [0]

            def link(ins):
                done[0] += 1
                ins.then_inc(chain, 1)
                dve.wait_ge(chain, done[0])

            dve.memset(raw[:, 1, 1, :], FAR)
            dve.memset(raw[:, 0, 1, :], 0)
            dve.memset(raw[:, 2, 1, :], 0).then_inc(zeroed, 1)
            dve.wait_ge(loaded, 16 * 9)
            link(dve.tensor_scalar(sh[:, 0], raw[:, 1], 12, None, ALU.logical_shift_left))
            link(dve.tensor_scalar(sh[:, 1], raw[:, 2], 24, None, ALU.logical_shift_left))
            link(dve.tensor_tensor(pk[:], sh[:, 0], raw[:, 0], ALU.bitwise_or))
            dve.tensor_tensor(pk[:], pk[:], sh[:, 1], ALU.bitwise_or).then_inc(packed_up, 1)
            link(dve.tensor_copy(dstf[:], raw[:, 1]))
            for t in range(NT + 1):
                if t:
                    dve.wait_ge(counted, t)
                dve.tensor_scalar(junk[:], dstf[:], float(t * P), 0.0, ALU.is_lt, ALU.add,
                                  accum_out=cnt[:, t:t + 1]).then_inc(counted, 1)
            dve.wait_ge(turned, 1)
            link(dve.tensor_copy(off[:], total[:, 0:NT + 1]))
            link(dve.tensor_copy(offm[:, 0], off[:, 0:NT]))
            link(dve.tensor_scalar(offm[:, 1], off[:, 1:NT + 1], -1.0, None, ALU.add))
            link(dve.tensor_copy(offi[:], offm[:]))
            link(dve.tensor_scalar(blki[:], offi[:], 8, None, ALU.arith_shift_right))
            link(dve.tensor_copy(blk[:], blki[:]))
            link(dve.tensor_tensor(some[:], off[:, 1:NT + 1], off[:, 0:NT], ALU.is_gt))
            dve.wait_ge(iotas, 1)
            link(dve.tensor_tensor(span[:], blk[:, 1], blk[:, 0], ALU.subtract))
            link(dve.scalar_tensor_tensor(out=num[:], in0=span[:], scalar=1.0, in1=some[:], op0=ALU.add, op1=ALU.mult))
            link(dve.tensor_tensor_scan(cum[:], c.ones[:, 0:NT], num[:], 0.0, ALU.mult, ALU.add))
            link(dve.tensor_tensor(base[:], blk[:, 0], cum[:], ALU.subtract))
            dve.tensor_tensor(base2[:], base[:], num[:], ALU.add).then_inc(counted, 1)
            dve.tensor_tensor(cmp[:], cum[:].unsqueeze(1).broadcast_to([P, 2, NT]),
                              gid[:].unsqueeze(2).broadcast_to([P, 2, NT]), ALU.is_le).then_inc(counted, 1)
            dve.wait_ge(counted, NT + 3)
            dve.tensor_reduce(tile[:], cmp[:], AX.X, ALU.add).then_inc(counted, 1)
            dve.wait_ge(counted, NT + 4)
            dve.tensor_tensor(cmp2[:], tid[:].unsqueeze(1).broadcast_to([P, 2, NT]),
                              tile[:].unsqueeze(2).broadcast_to([P, 2, NT]), ALU.is_equal).then_inc(counted, 1)
            dve.wait_ge(counted, NT + 5)
            dve.tensor_tensor(cmp3[:], cmp2[:], base2[:].unsqueeze(1).broadcast_to([P, 2, NT]), ALU.mult).then_inc(counted, 1)
            dve.wait_ge(counted, NT + 6)
            dve.tensor_reduce(rowf[:], cmp3[:], AX.X, ALU.add).then_inc(counted, 1)
            dve.wait_ge(counted, NT + 7)
            link(dve.tensor_tensor(rowf2[:], rowf[:], gid[:], ALU.add))
            link(dve.tensor_scalar(row[:], rowf2[:], float(NB - 1), None, ALU.min))
            link(dve.tensor_copy(tilei[:], tile[:]))
            dve.wait_ge(fetched, 32)
            link(dve.tensor_scalar(bits[:, 0], got[:], FAR, None, ALU.bitwise_and))
            link(dve.tensor_scalar(bits[:, 1], got[:], 12, FAR, ALU.logical_shift_right, ALU.bitwise_and))
            link(dve.tensor_scalar(bits[:, 2], got[:], 24, None, ALU.logical_shift_right))
            link(dve.tensor_copy(f[:], bits[:]))
            link(dve.scalar_tensor_tensor(out=vrow[:], in0=f[:, 2], scalar=float(NP), in1=f[:, 0], op0=ALU.mult, op1=ALU.add))
            dve.tensor_scalar(tile128[:], tile[:], float(-P), None, ALU.mult).then_inc(counted, 1)
            dve.wait_ge(counted, NT + 8)
            for h in range(2):
                ins = dve.tensor_scalar(loc[:, h], f[:, 1, h], tile128[0:HALF, h:h + 1], None, ALU.add)
                if h == 0:
                    ins.then_inc(counted, 1)
            link(ins)
            dve.wait_ge(counted, NT + 9)
            dve.tensor_copy(brow[:, 1], loc[:]).then_inc(brows, 1)
            dve.tensor_scalar(lowi[:], got[:], P - 1, None, ALU.bitwise_and).then_inc(counted, 1)
            dve.wait_ge(counted, NT + 10)
            dve.tensor_copy(brow[:, 0], lowi[:]).then_inc(brows, 1)
            link(dve.tensor_scalar(ok0[:], loc[:], 0.0, None, ALU.is_ge))
            link(dve.scalar_tensor_tensor(out=ok[:], in0=loc[:], scalar=float(P), in1=ok0[:], op0=ALU.is_lt, op1=ALU.mult))
            link(dve.scalar_tensor_tensor(out=key0[:], in0=f[:, 1], scalar=1.0, in1=ok[:], op0=ALU.add, op1=ALU.mult))
            link(dve.tensor_scalar(key[:], key0[:], -1.0, None, ALU.add))
            link(dve.memset(edge[:, :, 0:1], 0.0))
            link(dve.tensor_tensor(edge[:, :, 1:BLK], key[:, :, 1:BLK], key[:, :, 0:BLK - 1], ALU.not_equal))
            link(dve.tensor_reduce(runs[:], edge[:], AX.X, ALU.add))
            link(dve.tensor_scalar(edge[:], edge[:], NEG, None, ALU.mult))
            link(dve.tensor_copy(rep[:, :, 0, :], key[:, :, 0:1].broadcast_to([HALF, 2, H0])))
            link(dve.tensor_copy(rep[:, :, 1, :], key[:, :, BLK - 1:BLK].broadcast_to([HALF, 2, H0])))
            link(dve.tensor_scalar(rep[:, :, 2, :], runs[:].unsqueeze(2).broadcast_to([HALF, 2, H0]), 0.0, None, ALU.is_equal))
            link(dve.tensor_copy(e.step[:], edge[:]))
            link(dve.memset(e.step[:, :, 0:1], NEG))
            link(dve.tensor_copy(e.back[:, :, 0:BLK - 1], edge[:, :, 1:BLK]))
            link(dve.memset(e.back[:, :, BLK - 1:BLK], NEG))
            link(dve.memset(e.last[:, :, BLK - 1:BLK], 0.0))
            for h in range(2):
                link(dve.tensor_tensor_scan(e.first[:, h], edge[:, h], edge[:, h], 0.0, ALU.min, ALU.min))
                link(dve.tensor_tensor_scan(e.last[:, h, 0:BLK - 1][:, ::-1], edge[:, h, 1:BLK][:, ::-1],
                                            edge[:, h, 1:BLK][:, ::-1], 0.0, ALU.min, ALU.min))
            dve.wait_ge(kept, 1)
            link(dve.memset(same[:], 0.0))
            link(dve.memset(prev[:], 0.0))
            link(dve.tensor_tensor(same[:, 1:G], rows[:, 0, 1:G], rows[:, 1, 0:G - 1], ALU.is_equal))
            link(dve.tensor_tensor(prev[:, 1:G], same[:, 1:G], rows[:, 2, 0:G - 1], ALU.mult))
            link(dve.tensor_tensor(this[:], same[:], rows[:, 2, :], ALU.mult))
            link(dve.tensor_scalar(e.cont[:], same[:], -1.0, -NEG, ALU.add, ALU.mult))
            link(dve.tensor_scalar(e.over_prev[:], prev[:], -1.0, -NEG, ALU.add, ALU.mult))
            link(dve.tensor_scalar(e.over_this[:], this[:], -1.0, -NEG, ALU.add, ALU.mult))


SLOPE = 0.2


PARTS = 3
BT = U * K2


def split(dve, chain, base, src, parts, rest):
    dve.tensor_copy(parts(0), src).then_inc(chain, 1)
    for i in range(1, PARTS):
        dve.wait_ge(chain, base + 2 * i - 1)
        dve.tensor_tensor(rest, src if i == 1 else rest, parts(i - 1), ALU.subtract).then_inc(chain, 1)
        dve.wait_ge(chain, base + 2 * i)
        dve.tensor_copy(parts(i), rest).then_inc(chain, 1)
    dve.wait_ge(chain, base + 2 * PARTS - 1)


class ScoreSteps:

    NAMES = ("hot", "matched", "scored", "indexed", "begun", "low_hot", "s_chain",
             *(f"{name}{v}" for name in ("row", "low", "gathered") for v in range(U)))

    def __init__(self, m, sems, tag, c, e, heads, target, scores, local_row, first, per, slots=None, index=None, table=None,
                 low_row=None, own=None, high=None):
        self.hot, self.matched, self.scored, self.indexed, self.begun, self.low_hot, self.chain, *slotted = sems
        self.row, self.low, self.gathered = slotted[0:U], slotted[U:2 * U], slotted[2 * U:3 * U]
        self.c, self.e, self.heads, self.target, self.scores, self.local_row = c, e, heads, target, scores, local_row
        self.first, self.per, self.index, self.table, self.low_row, self.own, self.high = first, per, index, table, low_row, own, high
        self.width = R0 * heads if heads > 1 else 2 * PARTS
        self.loads, self.gathers = True, heads > 1
        self.slots = slots or per
        assert per % self.slots == 0 and self.slots <= U
        self.brow = m.sb(tag + "brow", [P, self.slots, BT * P], BF16)
        self.onet = m.sb(tag + "onet", [P, self.slots, BT * P], BF16)
        self.tot = m.sb(tag + "tot", [P, K2, U, heads])
        if heads > 1:
            self.idx = m.sb(tag + "idx", [P, self.slots, K2, U], I32)
            self.rows = m.sb(tag + "rows", [P, self.slots, K2, U, heads])
            self.pick = m.sb(tag + "pick", [P, K2, U, self.width])
            self.red = m.sb(tag + "red", [P, K2, U, heads])
            self.rid = m.sb(tag + "rid", [P, R0, heads])
            self.hit = m.ps(tag + "hit", [P, K2, 512])
        else:
            self.lrow = m.sb(tag + "lrow", [P, self.slots, BT * P], BF16)
            self.lonet = m.sb(tag + "lonet", [P, self.slots, BT * P], BF16)
            self.mask = m.sb(tag + "mask", [P, K2, U, NT])
            self.mask2 = m.sb(tag + "mask2", [P, K2, U, NT])
            self.red = m.sb(tag + "red", [P, K2, U, 1])
            self.red2 = m.sb(tag + "red2", [P, K2, U, 2])
            self.hit = m.ps(tag + "hit", [P, 2, 512])

    def uses(self, i, v):
        return i * (self.per // self.slots) + v // self.slots + 1

    def hits(self, v):
        if self.heads > 1:
            return self.hit[:, :, 0:U * self.width].rearrange("p k (g w) -> p k g w", g=U)
        return self.hit[:, v % 2, 0:BT * self.width].rearrange("p (k g w) -> p k g w", k=K2, g=U)

    def own_hits(self, v):
        return self.hit[:, v % 2, 64:64 + BT * NT].rearrange("p (k g w) -> p k g w", k=K2, g=U)

    def load_rows(self, sp, i, v):
        n = i * self.per + v
        sp.wait_ge(self.hot, n + 1)
        rows = self.local_row.rearrange("(b g) e -> b (g e)", g=U)
        sp.dma_start(self.brow[:, v % self.slots, :], rows[bass.ds(n + self.first, 1)].broadcast_to([P, BT * P])).then_inc(self.row[v % self.slots], 16)
        if self.heads == 1:
            sp.wait_ge(self.low_hot, n + 1)
            rows = self.low_row.rearrange("(b g) e -> b (g e)", g=U)
            sp.dma_start(self.lrow[:, v % self.slots, :],
                         rows[bass.ds(n + self.first, 1)].broadcast_to([P, BT * P])).then_inc(self.low[v % self.slots], 16)


    def start_pool(self, pool):
        if self.gathers:
            pool.sem_inc(self.scored, self.slots)

    def gather(self, pool, i, v):
        n = i * self.per + v
        pool.wait_ge(self.scored, n + 1)
        pool.tensor_copy(self.idx[:, v % self.slots], self.index[:, :, bass.ds((n + self.first) * U, U)]).then_inc(self.indexed, 1)
        pool.wait_ge(self.indexed, n + 1)
        pool.sem_inc(self.begun, 1)
        for k in range(K2):
            for g in range(U):
                pool.indirect_dma_start(self.rows[:, v % self.slots, k, g, :], None, self.table,
                                        bass.IndirectOffsetOnAxis(self.idx[:, v % self.slots, k, g:g + 1], 0)).then_inc(self.gathered[v % self.slots], 16)

    def start_dve(self, dve):
        if self.heads > 1:
            for r in range(R0):
                last = dve.memset(self.rid[:, r, :], float(r))
            last.then_inc(self.chain, 1)
            dve.wait_ge(self.chain, 1)
        if not self.gathers:
            dve.sem_inc(self.scored, self.slots)
        dve.sem_inc(self.hot, self.slots)
        dve.sem_inc(self.low_hot, self.slots)

    def prepare(self, dve, i, v):
        n = i * self.per + v
        dve.wait_ge(self.matched, n + 1)
        dve.wait_ge(self.row[v % self.slots], self.uses(i, v) * 16)
        dve.tensor_scalar(self.onet[:, v % self.slots, :], self.brow[:, v % self.slots, :], self.c.part[:, 0:1], None, ALU.is_equal).then_inc(self.hot, 1)
        if self.heads == 1:
            dve.wait_ge(self.low[v % self.slots], self.uses(i, v) * 16)
            dve.tensor_scalar(self.lonet[:, v % self.slots, :], self.lrow[:, v % self.slots, :], self.c.part[:, 0:1], None, ALU.is_equal).then_inc(self.low_hot, 1)

    def finish(self, dve, i, v):
        n = i * self.per + v
        at = bass.ds((n + self.first) * U, U)
        if self.heads > 1:
            dve.wait_ge(self.matched, n + 1 + self.slots)
            for k in range(K2):
                for g in range(U):
                    last = dve.scalar_tensor_tensor(
                        out=self.pick[:, k, g, :], in0=self.rid[:].rearrange("p r h -> p (r h)"),
                        scalar=self.e.rel[:, k, bass.ds((n + self.first) * U + g, 1)],
                        in1=self.hits(v)[:, k, g, :], op0=ALU.is_equal, op1=ALU.mult)
            last.then_inc(self.chain, 1)
            dve.wait_ge(self.chain, n * 3 + 2)
            for k in range(K2):
                last = dve.tensor_reduce(self.red[:, k], self.pick[:, k].rearrange("p g (r h) -> p g h r", h=self.heads), AX.X, ALU.add)
            last.then_inc(self.chain, 1)
            dve.wait_ge(self.chain, n * 3 + 3)
            dve.wait_ge(self.gathered[v % self.slots], self.uses(i, v) * 16 * BT)
            dve.tensor_tensor(self.tot[:], self.red[:], self.rows[:, v % self.slots], ALU.add).then_inc(self.chain, 1)
            dve.wait_ge(self.chain, n * 3 + 4)
        else:
            dve.tensor_tensor(self.mask[:], self.c.iota[:, 0:NT].unsqueeze(1).unsqueeze(1).broadcast_to([P, K2, U, NT]),
                              self.high[:, :, at].unsqueeze(3).broadcast_to([P, K2, U, NT]), ALU.is_equal).then_inc(self.chain, 1)
            dve.wait_ge(self.matched, n + 1 + self.slots)
            dve.wait_ge(self.chain, n * 4 + 1)
            dve.tensor_tensor(self.mask2[:], self.mask[:], self.own_hits(v), ALU.mult)
            dve.tensor_reduce(self.red2[:], self.hits(v).rearrange("p k g (s w) -> p k g w s", w=2), AX.X, ALU.add).then_inc(self.chain, 1)
            dve.wait_ge(self.chain, n * 4 + 2)
            dve.tensor_reduce(self.red[:], self.mask2[:], AX.X, ALU.add).then_inc(self.chain, 1)
            dve.wait_ge(self.chain, n * 4 + 3)
            dve.tensor_copy(self.scores[:, :, at, 1:2], self.red2[:, :, :, 1:2])
            dve.tensor_tensor(self.tot[:], self.red[:], self.red2[:, :, :, 0:1], ALU.add).then_inc(self.chain, 1)
            dve.wait_ge(self.chain, n * 4 + 4)
        dve.scalar_tensor_tensor(out=self.scores[:, :, at, 0:self.heads].rearrange("p k g h -> p k (g h)") if self.heads > 1
                                 else self.scores[:, :, at, 0], in0=self.tot[:].rearrange("p k g h -> p k (g h)"), scalar=SLOPE,
                                 in1=self.tot[:].rearrange("p k g h -> p k (g h)"), op0=ALU.mult, op1=ALU.max).then_inc(self.scored, 1)

    def start_pe(self, pe):
        pe.sem_inc(self.matched, self.slots)

    def match(self, pe, i, v):
        n = i * self.per + v
        at = [pe.value_load(self.e.tile[0:1, bass.ds((n + self.first) * U + g, 1)], min_val=0, max_val=NT) for g in range(U)]
        pe.wait_ge(self.hot, n + 1 + self.slots)
        if self.heads == 1:
            pe.wait_ge(self.low_hot, n + 1 + self.slots)
        pe.wait_ge(self.scored, n - (1 if self.heads > 1 else before(v, 2, self.per)) + 1 + self.slots)
        for g, tile in enumerate(at):
            for k in range(K2):
                hot = slice((g * K2 + k) * P, (g * K2 + k + 1) * P)
                if self.heads > 1:
                    for s in range(PARTS):
                        last = pe.matmul(self.hits(v)[:, k, g, :], self.onet[:, v % self.slots, hot], self.target[:, tile, s, :],
                                         start=(s == 0), stop=(s == PARTS - 1))
                else:
                    pe.matmul(self.hits(v)[:, k, g, :], self.onet[:, v % self.slots, hot],
                              self.target[:, tile].rearrange("p s w -> p (s w)"), start=True, stop=True)
                    for s in range(PARTS):
                        last = pe.matmul(self.own_hits(v)[:, k, g, :], self.lonet[:, v % self.slots, hot], self.own[:, s, :],
                                         start=(s == 0), stop=(s == PARTS - 1))
        last.then_inc(self.matched, 1)


def run_steps(nc, tag, ride, bodies):
    with Mem(nc) as m, stage(nc, *ride[0].NAMES) as (block, *sems):
        steps = steps_beside(ride, m, sems, tag)
        per = range(steps.per)

        @block.sync
        def _(sp):
            if steps.loads:
                with sp.Fori(0, bodies) as i:
                    for v in per:
                        steps.load_rows(sp, i, v)

        @block.gpsimd
        def _(pool):
            if steps.gathers:
                steps.start_pool(pool)
                with pool.Fori(0, bodies) as i:
                    for v in per:
                        steps.gather(pool, i, v)

        @block.tensor
        def _(pe):
            steps.start_pe(pe)
            with pe.Fori(0, bodies) as i:
                for v in per:
                    steps.match(pe, i, v)

        @block.vector
        def _(dve):
            steps.start_dve(dve)
            with dve.Fori(0, bodies) as i:
                steps.prepare(dve, i, 0)
                for v in per:
                    if v + 1 < len(per):
                        steps.prepare(dve, i, v + 1)
                    steps.finish(dve, i, v)


def project0(nc, c, xnt, cat, values, keys, vals, ride):
    nb = len(CHUNKS0)
    with Mem(nc) as m, stage(nc, "staged", "used", "multiplied", "by_act", "by_dve", "stored0", "stored1", *names_beside(ride)) as (
            block, staged, used, multiplied, by_act, by_dve, stored0, stored1, *sems):
        steps = steps_beside(ride, m, sems, "es0_")
        stored = (stored0, stored1)
        slot = m.sb("xslot0", [P, U, DC, P])
        hv = m.sb("hv0", [P, 2, HV])
        acc = m.ps("acc0", [P, nb, 512])
        vrows = values.rearrange("(r t p) d -> t p r d", r=R0, p=P)

        @block.gpsimd
        def _(pool):
            steps.start_pool(pool)
            with pool.Fori(0, NT // U) as i:
                for u in range(U):
                    steps.gather(pool, i, u)

        @block.tensor
        def _(pe):
            pe.sem_inc(used, CREDIT)
            steps.start_pe(pe)
            with pe.Fori(0, NT // U) as i:
                for u in range(U):
                    t = i * U + u
                    pe.wait_ge(staged, t + 1)
                    pe.wait_ge(by_act, t + CREDIT)
                    pe.wait_ge(by_dve, t + CREDIT)
                    for b, (lo, hi) in enumerate(CHUNKS0):
                        for k in range(DC):
                            last = pe.matmul(acc[:, b, 0:hi - lo], slot[:, u, k, :], cat[:, k, lo:hi],
                                             start=(k == 0), stop=(k == DC - 1))
                        if b < nb - 1:
                            last.then_inc(multiplied, 1)
                    last.then_inc(used, 1)
                    steps.match(pe, i, u)

        @block.scalar
        def _(act):
            act.sem_inc(by_act, CREDIT)
            with act.Fori(0, NT // U) as i:
                for u in range(U):
                    t = i * U + u
                    act.wait_ge(used, t - U + 1 + CREDIT)
                    act.copy(slot[:, u], xnt[:, :, bass.ts(t, P)]).then_inc(staged, 1)
                    act.wait_ge(stored[u % 2], earlier(i, u, 2) * 16 + 16)
                    for b in range(2):
                        act.wait_ge(multiplied, t * (nb - 1) + b + 1)
                        last = act.copy(hv[:, u % 2, b * 512:(b + 1) * 512], acc[:, b, :])
                    last.then_inc(by_act, 1)

        @block.vector
        def _(dve):
            dve.sem_inc(by_dve, CREDIT)
            steps.start_dve(dve)
            with dve.Fori(0, NT // U) as i:
                for u in range(U):
                    t = i * U + u
                    steps.prepare(dve, i, u)
                    dve.wait_ge(stored[u % 2], earlier(i, u, 2) * 16 + 16)
                    for b in range(2, 4):
                        dve.wait_ge(multiplied, t * (nb - 1) + b + 1)
                        dve.tensor_copy(hv[:, u % 2, b * 512:(b + 1) * 512], acc[:, b, :])
                    dve.wait_ge(used, t + 1 + CREDIT)
                    dve.tensor_scalar(keys[:, t, :], acc[:, 4, CK - HV:CV - HV], c.mask[:, bass.ts(t, 1)], None, ALU.add)
                    dve.tensor_copy(vals[:, t, :], acc[:, 4, CV - HV:COLS0 - HV]).then_inc(by_dve, 1)
                    steps.finish(dve, i, u)

        @block.sync
        def _(sp):
            for q in stored:
                sp.sem_inc(q, 16)
            with sp.Fori(0, NT // U) as i:
                for u in range(U):
                    t = i * U + u
                    steps.load_rows(sp, i, u)
                    sp.wait_ge(by_act, t + 1 + CREDIT)
                    sp.wait_ge(by_dve, t + 1 + CREDIT)
                    sp.dma_start(vrows[t], hv[:, u % 2, :].rearrange("p (r d) -> p r d", r=R0)).then_inc(stored[u % 2], 16)
            for n, q in enumerate(stored):
                sp.wait_ge(q, 16 + 16 * (NT // U) * len(range(n, U, 2)))


def score_tables0(nc, sc, source_scores, target):
    with Mem(nc) as m, stage(nc, "zeroed", "chain", "stored") as (block, zeroed, chain, stored):
        rest = m.sb("st_rest", [P, NT, R0 * H0])

        @block.sync
        def _(sp):
            for r in range(R0):
                sp.dma_start(source_scores[r * NP:(r + 1) * NP].rearrange("(t p) h -> p t h", p=P),
                             sc[:, :, r * H0:(r + 1) * H0]).then_inc(stored, 16)
            sp.wait_ge(stored, 16 * R0)

        @block.vector
        def _(dve):
            dve.memset(target[:, NT], 0.0)
            split(dve, chain, 0, sc[:, :, R0 * H0:], lambda s: target[:, 0:NT, s, :], rest[:])


def segment_softmax(nc, tag, c, e, heads, channels, scores):
    step = 512 // BLK
    pairs = [(h, q) for h in range(2) for q in range(0, channels, step)]
    with Mem(nc) as m, stage(nc, "turned", "kept", "scanned", "ends", "ends_turned", "rows", "carried", "carry_turned",
                             "carry_kept", "spread", "shifted", "exped", "back_turned", "back_kept") as (
            block, turned, kept, scanned, ends, ends_turned, rows_kept, carried, carry_turned,
            carry_kept, spread, shifted, exped, back_turned, back_kept):
        s = m.sb(tag + "s", [HALF, 2, channels, BLK])
        fwd = m.sb(tag + "fwd", [HALF, 2, heads, BLK])
        top = m.sb(tag + "top", [HALF, 2, heads, BLK])
        tip = m.sb(tag + "tip", [HALF, 2, 2, heads])
        tips = m.sb(tag + "tips", [heads, 2, G])
        inc = m.sb(tag + "inc", [heads, 2, G])
        car = m.sb(tag + "car", [heads, 2, G])
        carg = m.sb(tag + "carg", [HALF, 2, 2, heads])
        turn = m.ps(tag + "turn", [P, 4, 512])
        small = m.ps(tag + "small", [P, 512])
        small2 = m.ps(tag + "small2", [P, 512])

        @block.tensor
        def _(pe):
            for n, (h, q) in enumerate(pairs):
                if n >= 4:
                    pe.wait_ge(kept, n - 3)
                for j in range(step):
                    for k in range(K2):
                        last = pe.transpose(turn[0:HALF, n % 4, j * BLK + k * P:j * BLK + (k + 1) * P],
                                            scores[:, k, h * HALF:(h + 1) * HALF, q + j], c.ident[:])
                last.then_inc(turned, 1)
            pe.wait_ge(ends, 1)
            for d in range(2):
                for h in range(2):
                    last = pe.transpose(small[0:heads, d * G + h * HALF:d * G + (h + 1) * HALF], tip[:, h, d, :],
                                        c.ident[0:HALF, 0:HALF])
            last.then_inc(ends_turned, 1)
            pe.wait_ge(carried, 2)
            for h in range(2):
                for d in range(2):
                    last = pe.transpose(small2[0:HALF, (h * 2 + d) * heads:(h * 2 + d + 1) * heads],
                                        car[:, d, h * HALF:(h + 1) * HALF], c.ident[0:heads, 0:heads])
            last.then_inc(carry_turned, 1)
            pe.wait_ge(kept, len(pairs))
            for n, (h, q) in enumerate(pairs):
                pe.wait_ge(exped, h + 1)
                if n >= 4:
                    pe.wait_ge(back_kept, n - 3)
                for j in range(step):
                    for k in range(K2):
                        last = pe.transpose(turn[:, n % 4, (j * K2 + k) * P:(j * K2 + k) * P + HALF],
                                            s[:, h, q + j, k * P:(k + 1) * P], c.ident[0:HALF, 0:HALF])
                last.then_inc(back_turned, 1)

        @block.scalar
        def _(act):
            for n, (h, q) in enumerate(pairs):
                act.wait_ge(turned, n + 1)
                act.copy(s[:, h, q:q + step, :], turn[0:HALF, n % 4, :].rearrange("p (j e) -> p j e", j=step)).then_inc(kept, 1)
            for h in range(2):
                act.wait_ge(shifted, h + 1)
                act.activation(s[:, h], s[:, h], ACT.Exp, scale=-1.0).then_inc(exped, 1)
            for n, (h, q) in enumerate(pairs):
                act.wait_ge(back_turned, n + 1)
                src = turn[:, n % 4, :].rearrange("p (j k g) -> p j k g", j=step, k=K2)
                for j in range(step):
                    last = act.copy(scores[:, :, h * HALF:(h + 1) * HALF, q + j], src[:, j, :, 0:HALF])
                last.then_inc(back_kept, 1)

        @block.vector
        def _(dve):
            per = len(pairs) // 2
            for h in range(2):
                for q in range(heads):
                    dve.wait_ge(kept, h * per + q // step + 1)
                    dve.tensor_tensor_scan(fwd[:, h, q, :], e.step[:, h, :], s[:, h, q, :], 0.0, ALU.add, ALU.max).then_inc(scanned, 1)
            for h in range(2):
                for q in range(heads):
                    dve.wait_ge(scanned, h * heads + q + 1)
                    dve.tensor_tensor_scan(top[:, h, q, ::-1], e.back[:, h, ::-1], fwd[:, h, q, ::-1], 0.0,
                                           ALU.add, ALU.max).then_inc(scanned, 1)
            dve.wait_ge(scanned, 4 * heads)
            for h in range(2):
                dve.tensor_copy(tip[:, h, 0, :], fwd[:, h, :, BLK - 1])
                last = dve.tensor_copy(tip[:, h, 1, :], top[:, h, :, 0])
            last.then_inc(ends, 1)
            dve.wait_ge(ends_turned, 1)
            dve.tensor_copy(tips[:], small[0:heads, 0:2 * G].rearrange("p (d g) -> p d g", d=2)).then_inc(rows_kept, 1)
            dve.wait_ge(rows_kept, 1)
            dve.tensor_tensor(inc[:, 0, 1:G], tips[:, 0, 0:G - 1], e.cont[0:heads, 1:G], ALU.add)
            dve.tensor_tensor(inc[:, 1, 1:G], tips[:, 1, 1:G], e.cont[0:heads, 1:G], ALU.add)
            dve.memset(car[:, 0, 0:1], NEG)
            dve.memset(car[:, 1, G - 1:G], NEG).then_inc(rows_kept, 1)
            dve.wait_ge(rows_kept, 2)
            dve.tensor_tensor_scan(car[:, 0, 1:G], e.over_prev[0:heads, 1:G], inc[:, 0, 1:G], NEG, ALU.add, ALU.max).then_inc(carried, 1)
            dve.tensor_tensor_scan(car[:, 1, 0:G - 1][:, ::-1], e.over_this[0:heads, 1:G][:, ::-1], inc[:, 1, 1:G][:, ::-1],
                                   NEG, ALU.add, ALU.max).then_inc(carried, 1)
            dve.wait_ge(carry_turned, 1)
            dve.tensor_copy(carg[:], small2[0:HALF, 0:4 * heads].rearrange("p (h d q) -> p h d q", h=2, d=2)).then_inc(carry_kept, 1)
            dve.wait_ge(carry_kept, 1)
            for h in range(2):
                for q in range(heads):
                    dve.scalar_tensor_tensor(out=fwd[:, h, q, :], in0=e.first[:, h, :], scalar=carg[:, h, 0, q:q + 1],
                                             in1=top[:, h, q, :], op0=ALU.add, op1=ALU.max).then_inc(spread, 1)
                for q in range(heads):
                    dve.wait_ge(spread, 2 * heads * h + q + 1)
                    dve.scalar_tensor_tensor(out=top[:, h, q, :], in0=e.last[:, h, :], scalar=carg[:, h, 1, q:q + 1],
                                             in1=fwd[:, h, q, :], op0=ALU.add, op1=ALU.max).then_inc(spread, 1)
                dve.wait_ge(spread, 2 * heads * (h + 1))
                if heads == channels:
                    dve.scalar_tensor_tensor(out=s[:, h].rearrange("p q e -> p (q e)"), in0=top[:, h].rearrange("p q e -> p (q e)"),
                                             scalar=0.0, in1=s[:, h].rearrange("p q e -> p (q e)"),
                                             op0=ALU.max, op1=ALU.subtract).then_inc(shifted, 1)
                else:
                    dve.tensor_tensor(fwd[:, h, 0, :], top[:, h, 0, :], s[:, h, 1, :], ALU.max).then_inc(carry_kept, 1)
                    dve.wait_ge(carry_kept, h + 2)
                    dve.tensor_tensor(s[:, h], fwd[:, h, 0:1, :].broadcast_to([HALF, 2, BLK]), s[:, h], ALU.subtract).then_inc(shifted, 1)


class AggregateSteps:

    NAMES = ("indexed", "hot", "weighted", "matched", "summed", "filled", "begun", *(f"row{s}" for s in range(U)))

    def __init__(self, m, sems, tag, c, e, index, table, heads, weights, extra, acc, first, per):
        assert per % (2 * U) == 0
        (self.indexed, self.hot, self.weighted, self.multiplied, self.summed, self.chain, self.begun, *self.gathered) = sems
        self.c, self.e, self.index, self.table, self.heads, self.weights = c, e, index, table, heads, weights
        self.acc, self.first, self.per, self.wide = acc, first, per, D + extra
        self.loads, self.gathers = False, True
        self.idx = m.sb(tag + "idx", [P, 2, K2, U], I32)
        self.rows = m.sb(tag + "rows", [P, U, K2, D])
        self.one = m.sb(tag + "one", [P, 2, K2, P])
        self.msg = m.sb(tag + "msg", [P, 2, K2, self.wide]) if weights is not None else None
        self.part = m.ps(tag + "part", [P, 2, 512])

    def have_rows(self, engine, i, v):
        engine.wait_ge(self.gathered[v % U], (i * (self.per // U) + v // U + 1) * 16 * K2)

    def start_pool(self, pool):
        pool.sem_inc(self.summed, CREDIT)

    def gather(self, pool, i, v):
        n = i * self.per + v
        half = v // U % 2
        pool.wait_ge(self.summed, n - U + 1 + CREDIT)
        if v % U == 0:
            pool.tensor_copy(self.idx[:, half], self.index[:, :, bass.ds(n + self.first, U)]).then_inc(self.indexed, 1)
            pool.wait_ge(self.indexed, i * (self.per // U) + v // U + 1)
        pool.sem_inc(self.begun, 1)
        for k in range(K2):
            pool.indirect_dma_start(self.rows[:, v % U, k, :], None, self.table,
                                    bass.IndirectOffsetOnAxis(self.idx[:, half, k, v % U:v % U + 1], 0)).then_inc(self.gathered[v % U], 16)

    def start_pe(self, pe):
        pe.sem_inc(self.multiplied, CREDIT)

    def match(self, pe, i, v):
        n = i * self.per + v
        pe.wait_ge(self.hot, n + 1)
        if self.weights is None:
            self.have_rows(pe, i, v)
        else:
            pe.wait_ge(self.weighted, n + 1)
        pe.wait_ge(self.summed, n - 2 + 1 + CREDIT)
        for k in range(K2):
            rhs = self.rows[:, v % U, k, :] if self.weights is None else self.msg[:, v % 2, k, :]
            last = pe.matmul(self.part[:, v % 2, 0:self.wide], self.one[:, v % 2, k, :], rhs, start=(k == 0), stop=(k == K2 - 1))
        last.then_inc(self.multiplied, 1)

    def start_dve(self, dve):
        if self.weights is not None:
            dve.memset(self.msg[:], 1.0).then_inc(self.chain, 1)
            dve.wait_ge(self.chain, 1)

    def prepare(self, dve, i, v):
        n = i * self.per + v
        dve.wait_ge(self.multiplied, n - 2 + 1 + CREDIT)
        for k in range(K2):
            last = dve.tensor_scalar(self.one[:, v % 2, k, :], self.c.iota[:], self.e.local[:, k, bass.ds(n + self.first, 1)], None, ALU.is_equal)
        last.then_inc(self.hot, 1)
        if self.weights is None:
            return
        self.have_rows(dve, i, v)
        weight = self.weights[:, :, bass.ds(n + self.first, 1), :].squeeze(2)
        dve.tensor_copy(self.msg[:, v % 2, :, D:D + self.weights.shape[3]], weight)
        for k in range(K2):
            if self.heads == 1:
                last = dve.tensor_scalar(self.msg[:, v % 2, k, 0:D], self.rows[:, v % U, k, :], weight[:, k, 0:1], None, ALU.mult)
            else:
                last = dve.tensor_tensor(
                    self.msg[:, v % 2, k, 0:D].rearrange("p (h d) -> p h d", h=self.heads),
                    self.rows[:, v % U, k, :].rearrange("p (h d) -> p h d", h=self.heads),
                    weight[:, k, :].unsqueeze(2).broadcast_to([P, self.heads, D // self.heads]), ALU.mult)
        last.then_inc(self.weighted, 1)

    def finish(self, dve, i, v):
        n = i * self.per + v
        tile = dve.value_load(self.e.tile[0:1, bass.ds(n + self.first, 1)], min_val=0, max_val=NT)
        dve.wait_ge(self.multiplied, n + 1 + CREDIT)
        dve.wait_ge(self.summed, n + CREDIT)
        dve.tensor_tensor(self.acc[:, tile, :], self.acc[:, tile, :], self.part[:, v % 2, 0:self.wide], ALU.add).then_inc(self.summed, 1)


def clear(nc, *tensors):
    with stage(nc) as (block,):
        @block.gpsimd
        def _(pool):
            for t in tensors:
                pool.memset(t, 0.0)


def finish_attention0(nc, acc, x, degree):
    with Mem(nc) as m, stage(nc, "chain") as (block, chain):
        den = m.sb("f0_den", [P, NT, H0])
        inv = m.sb("f0_inv", [P, NT, H0])

        @block.vector
        def _(dve):
            dve.tensor_copy(degree[:], acc[:, 0:NT, D + H0])
            dve.tensor_scalar(den[:], acc[:, 0:NT, D:D + H0], 1e-12, None, ALU.add).then_inc(chain, 1)
            dve.wait_ge(chain, 1)
            dve.reciprocal(inv[:], den[:]).then_inc(chain, 1)
            dve.wait_ge(chain, 2)
            v = acc[:, 0:NT, 0:D].rearrange("p t (h d) -> p t h d", h=H0)
            dve.tensor_tensor(v, v, inv[:].unsqueeze(3).broadcast_to([P, NT, H0, D0]), ALU.mult).then_inc(chain, 1)
            dve.wait_ge(chain, 3)
            dve.tensor_tensor(x[:], x[:], acc[:, 0:NT, 0:D], ALU.add)


def project(nc, tag, c, xnt, w, width, out, bias=None, masked=0, ride=None):
    with Mem(nc) as m, stage(nc, "staged", "multiplied", "kept", *names_beside(ride)) as (block, staged, multiplied, kept, *sems):
        steps = steps_beside(ride, m, sems, tag)
        slot = m.sb(tag + "slot", [P, U, DC, P])
        acc = m.ps(tag + "acc", [P, U, 512])

        assert steps is None or not steps.loads

        @block.gpsimd
        def _(pool):
            if steps is not None and steps.gathers:
                steps.start_pool(pool)
                with pool.Fori(0, NT // U) as i:
                    for v in range(steps.per):
                        steps.gather(pool, i, v)

        @block.scalar
        def _(act):
            with act.Fori(0, NT // U) as i:
                for u in range(U):
                    t = i * U + u
                    act.wait_ge(multiplied, t - U + 1 + CREDIT)
                    act.copy(slot[:, u], xnt[:, :, bass.ts(t, P)]).then_inc(staged, 1)

        @block.tensor
        def _(pe):
            pe.sem_inc(multiplied, CREDIT)
            if steps is not None:
                steps.start_pe(pe)
            with pe.Fori(0, NT // U) as i:
                for u in range(U):
                    t = i * U + u
                    pe.wait_ge(staged, t + 1)
                    pe.wait_ge(kept, t - U + 1 + CREDIT)
                    for k in range(DC):
                        last = pe.matmul(acc[:, u, 0:width], slot[:, u, k, :], w[:, k, :], start=(k == 0),
                                         stop=(k == DC - 1 and bias is None))
                    if bias is not None:
                        last = pe.matmul(acc[:, u, 0:width], c.ones[0:1, :], bias[:], start=False, stop=True)
                    last.then_inc(multiplied, 1)
                    for v in beside(steps, u, U):
                        steps.match(pe, i, v)

        @block.vector
        def _(dve):
            dve.sem_inc(kept, CREDIT)
            if steps is not None:
                steps.start_dve(dve)
            with dve.Fori(0, NT // U) as i:
                for u in range(U):
                    t = i * U + u
                    dve.wait_ge(multiplied, t + 1 + CREDIT)
                    if masked:
                        last = dve.tensor_scalar(out[:, t, 0:masked], acc[:, u, 0:masked], c.valid[:, bass.ts(t, 1)], None, ALU.mult)
                    if masked < width:
                        last = dve.tensor_copy(out[:, t, masked:width], acc[:, u, masked:width])
                    last.then_inc(kept, 1)
                    dve_beside(steps, dve, i, u, U)


NX = 8
TOP_BIG = 1.0e6


def route(nc, c, logits, one, best):
    with Mem(nc) as m, stage(nc, "chain", "exped") as (block, chain, exped):
        top = m.sb("r_top", [P, NT])
        total = m.sb("r_total", [P, NT])
        inv = m.sb("r_inv", [P, NT])
        rw = m.sb("r_rw", [P, NT, NX])
        same = m.sb("r_same", [P, NT, NX])
        place = m.sb("r_place", [P, NT, NX])
        first = m.sb("r_first", [P, NT])

        def wide(v):
            return v.unsqueeze(2).broadcast_to([P, NT, NX])

        numbers = c.iota[:, 0:NX].unsqueeze(1).broadcast_to([P, NT, NX])

        @block.scalar
        def _(act):
            act.wait_ge(chain, 2)
            act.activation(logits[:], logits[:], ACT.Exp).then_inc(exped, 1)

        @block.vector
        def _(dve):
            done = [0]

            def link(ins):
                done[0] += 1
                ins.then_inc(chain, 1)
                dve.wait_ge(chain, done[0])

            link(dve.tensor_reduce(top[:], logits[:], AX.X, ALU.max))
            link(dve.tensor_tensor(logits[:], logits[:], wide(top[:]), ALU.subtract))
            dve.wait_ge(exped, 1)
            link(dve.tensor_reduce(total[:], logits[:], AX.X, ALU.add))
            link(dve.reciprocal(inv[:], total[:]))
            link(dve.tensor_tensor(rw[:], logits[:], wide(inv[:]), ALU.mult))
            for n in range(2):
                link(dve.tensor_reduce(best[:, n], rw[:], AX.X, ALU.max))
                link(dve.tensor_tensor(same[:], rw[:], wide(best[:, n]), ALU.is_equal))
                link(dve.scalar_tensor_tensor(out=place[:], in0=same[:], scalar=-TOP_BIG, in1=numbers, op0=ALU.mult, op1=ALU.add))
                link(dve.tensor_reduce(first[:], place[:], AX.X, ALU.min))
                link(dve.tensor_scalar(first[:], first[:], TOP_BIG, None, ALU.add))
                link(dve.tensor_tensor(one[:, n], wide(first[:]), numbers, ALU.is_equal))
                if n == 0:
                    link(dve.scalar_tensor_tensor(out=rw[:], in0=one[:, 0], scalar=-4.0, in1=rw[:], op0=ALU.mult, op1=ALU.add))
            link(dve.tensor_tensor(total[:], best[:, 0], best[:, 1], ALU.add))
            link(dve.reciprocal(inv[:], total[:]))
            dve.tensor_tensor(best[:], best[:], inv[:].unsqueeze(1).broadcast_to([P, 2, NT]), ALU.mult)


GM = 256
NG = 2 * N // GM + NX
NSLOT = NG * GM
assert NG % 2 == 0


def place_tokens(nc, c, one, slots, expert):
    with Mem(nc) as m, stage(nc, "chain", "summed") as (block, chain, summed):
        tri = m.sb("pl_tri", [P, P])
        cnt = m.sb("pl_cnt", [P, NT, NX])
        keep = m.sb("pl_keep", [P, NX, NT])
        tot = m.sb("pl_tot", [P, NX, NT])
        cum = m.sb("pl_cum", [P, NX, NT])
        ng1, ng2, cumg, base, gid = (m.sb("pl_" + n, [P, NG]) for n in ("ng1", "ng2", "cumg", "base", "gid"))
        ngi = m.sb("pl_ngi", [P, NX], I32)
        pos = m.sb("pl_pos", [P, NX, NT])
        mine = m.sb("pl_mine", [P, 2, NT, NX])
        row = m.sb("pl_row", [P, 2, NT])
        spare = m.sb("pl_spare", [P, 2, NT])
        less = m.sb("pl_less", [P, NG, NX])
        ps = m.ps("pl_ps", [P, 2, 512])

        @block.tensor
        def _(pe):
            pe.wait_ge(chain, 3)
            flat = cnt[:].rearrange("p t e -> p (t e)")
            pe.matmul(ps[:, 0, 0:NT * NX], tri[:], flat, start=True, stop=True)
            pe.matmul(ps[:, 1, 0:NT * NX], c.ones[:], flat, start=True, stop=True).then_inc(summed, 1)

        @block.vector
        def _(dve):
            done = [0]

            def link(ins):
                done[0] += 1
                ins.then_inc(chain, 1)
                dve.wait_ge(chain, done[0])

            link(dve.tensor_scalar(tri[:], c.iota[:], c.part[:, 0:1], None, ALU.is_gt))
            link(dve.tensor_tensor(cnt[:], one[:, 0], one[:, 1], ALU.add))
            link(dve.tensor_tensor(cnt[:], cnt[:], c.valid[:].unsqueeze(2).broadcast_to([P, NT, NX]), ALU.mult))
            link(dve.memset(keep[:], 1.0))
            link(dve.memset(keep[:, :, 0:1], 0.0))
            dve.wait_ge(summed, 1)
            link(dve.tensor_copy(tot[:], ps[:, 1, 0:NT * NX].rearrange("p (t e) -> p e t", e=NX)))
            link(dve.tensor_tensor_scan(cum[:].rearrange("p e t -> p (e t)"), keep[:].rearrange("p e t -> p (e t)"),
                                        tot[:].rearrange("p e t -> p (e t)"), 0.0, ALU.mult, ALU.add))
            link(dve.tensor_scalar(ng1[:, 0:NX], cum[:, :, NT - 1], float(GM - 1), None, ALU.add))
            link(dve.tensor_copy(ngi[:], ng1[:, 0:NX]))
            link(dve.tensor_scalar(ngi[:], ngi[:], GM.bit_length() - 1, None, ALU.arith_shift_right))
            link(dve.tensor_copy(ng2[:, 0:NX], ngi[:]))
            link(dve.tensor_tensor_scan(cumg[:, 0:NX], c.ones[:, 0:NX], ng2[:, 0:NX], 0.0, ALU.mult, ALU.add))
            link(dve.tensor_tensor(base[:, 0:NX], cumg[:, 0:NX], ng2[:, 0:NX], ALU.subtract))
            link(dve.tensor_scalar(base[:, 0:NX], base[:, 0:NX], float(GM), None, ALU.mult))
            link(dve.tensor_tensor(pos[:], cum[:], tot[:], ALU.subtract))
            link(dve.tensor_tensor(pos[:], pos[:], base[:, 0:NX].unsqueeze(2).broadcast_to([P, NX, NT]), ALU.add))
            link(dve.tensor_tensor(pos[:], pos[:], ps[:, 0, 0:NT * NX].rearrange("p (t e) -> p e t", e=NX), ALU.add))
            for n in range(2):
                link(dve.tensor_tensor(mine[:, n], one[:, n], pos[:].rearrange("p e t -> p t e"), ALU.mult))
            link(dve.tensor_reduce(row[:], mine[:], AX.X, ALU.add))
            for n in range(2):
                link(dve.tensor_scalar(spare[:, n], c.token[:], float(NSLOT - N + n * P), None, ALU.add))
                link(dve.tensor_tensor(row[:, n], row[:, n], spare[:, n], ALU.subtract))
                link(dve.tensor_tensor(row[:, n], row[:, n], c.valid[:], ALU.mult))
                link(dve.tensor_tensor(row[:, n], row[:, n], spare[:, n], ALU.add))
            link(dve.tensor_copy(slots[:], row[:]))
            link(dve.tensor_tensor(less[:], cumg[:, 0:NX].unsqueeze(1).broadcast_to([P, NG, NX]),
                                   c.iota[:, 0:NG].unsqueeze(2).broadcast_to([P, NG, NX]), ALU.is_le))
            link(dve.tensor_reduce(gid[:], less[:], AX.X, ALU.add))
            dve.tensor_scalar(expert[:], gid[:], float(NX - 1), None, ALU.min)


def zero_rows(nc, rows, out_rows):
    with Mem(nc) as m, stage(nc, "zeroed", "stored") as (block, zeroed, stored):
        z = m.sb("z_z", [P, 8, D])

        @block.gpsimd
        def _(pool):
            pool.memset(z[:], 0.0).then_inc(zeroed, 1)
            pool.wait_ge(zeroed, 1)
            for q in range(NSLOT // (8 * P)):
                pool.dma_start(rows[q * 8 * P:(q + 1) * 8 * P].rearrange("(k p) d -> p k d", p=P), z[:]).then_inc(stored, 16)
            pool.dma_start(out_rows[NSLOT:].rearrange("(k p) d -> p k d", p=P), z[:, 0:2]).then_inc(stored, 16)
            pool.wait_ge(stored, 16 * (NSLOT // (8 * P) + 1))


def scatter_tokens(pool, xn, slots, rows, scattered):
    for n in range(2):
        for t in range(NT):
            pool.indirect_dma_start(rows, bass.IndirectOffsetOnAxis(slots[:, n, t:t + 1], 0), xn[:, t, :], None).then_inc(scattered, 16)
    pool.wait_ge(scattered, 16 * 2 * NT)


def run_experts(nc, c, rows, out_rows, expert, w1p, b1p, w2p, b2p, hidden):
    fb = hidden // P
    gt = GM // P
    with Mem(nc) as m, stage(nc, "loaded0", "loaded1", "turned", "kept", "up", "shaped", "down", "out0", "out1",
                             "stored0", "stored1", "rows0", "rows1") as (
            block, loaded0, loaded1, turned, kept, up, shaped, down, out0, out1, stored0, stored1, rows0, rows1):
        loaded, out_made, stored = (loaded0, loaded1), (out0, out1), (stored0, stored1)
        have_rows = (rows0, rows1)
        w1 = m.sb("x_w1", [P, 2, DC, hidden])
        w2 = m.sb("x_w2", [P, 2, fb, D])
        b1 = m.sb("x_b1", [P, 2, fb])
        b2 = m.sb("x_b2", [P, 2, D])
        xr = m.sb("x_xr", [P, 2, gt, D])
        xt = m.sb("x_xt", [P, 2, DC, GM])
        hid = m.sb("x_hid", [P, fb, GM])
        y = m.sb("x_y", [P, 2, gt, D])
        turn = m.ps("x_turn", [P, DC, GM])
        up_ps = m.ps("x_up", [P, 3, 512])
        down_ps = m.ps("x_down", [P, gt, 512])

        @block.sync
        def _(sp):
            def load(b, g):
                e = sp.value_load(expert[0:1, bass.ds(g, 1)], min_val=0, max_val=NX - 1)
                sp.dma_start(xr[:, b], rows[bass.ds(g * GM, GM)].rearrange("(k p) d -> p k d", p=P)).then_inc(have_rows[b], 16)
                sp.dma_start(w1[:, b], w1p[e].rearrange("(k p) f -> p k f", p=P)).then_inc(loaded[b], 16)
                sp.dma_start(b1[:, b], b1p[e].rearrange("(k p) -> p k", p=P), allow_slow_non_contiguous=True).then_inc(loaded[b], 16)
                sp.dma_start(w2[:, b], w2p[e].rearrange("(k p) f -> p k f", p=P)).then_inc(loaded[b], 16)
                sp.dma_start(b2[:, b], b2p[e].rearrange("(a d) -> a d", a=1).broadcast_to([P, D])).then_inc(loaded[b], 16)

            def save(b, g, i):
                sp.wait_ge(out_made[b], i + 1 + b)
                sp.dma_start(out_rows[bass.ds(g * GM, GM)].rearrange("(k p) d -> p k d", p=P), y[:, b]).then_inc(stored[b], 16)

            for b in range(2):
                sp.sem_inc(stored[b], 16)
                load(b, b)
            with sp.Fori(0, NG // 2 - 1) as i:
                for b in range(2):
                    save(b, i * 2 + b, i)
                    load(b, i * 2 + 2 + b)
            for b in range(2):
                save(b, NG - 2 + b, NG // 2 - 1)
            for b in range(2):
                sp.wait_ge(stored[b], 16 * (NG // 2 + 1))

        @block.tensor
        def _(pe):
            def turn_rows(i, b):
                g = i * 2 + b
                pe.wait_ge(have_rows[b], (i + 1) * 16)
                pe.wait_ge(kept, g + 1)
                for k in range(DC):
                    for j in range(gt):
                        last = pe.transpose(turn[:, k, j * P:(j + 1) * P], xr[:, b, j, k * P:(k + 1) * P], c.ident[:])
                last.then_inc(turned, 1)

            def body(i, more):
                for b in range(2):
                    g = i * 2 + b
                    pe.wait_ge(loaded[b], (i + 1) * 64)
                    pe.wait_ge(kept, g + 2)
                    for f in range(fb):
                        pe.wait_ge(shaped, g * fb + f + 1 - before(f, 3, fb) + CREDIT)
                        for k in range(DC):
                            last = pe.matmul(up_ps[:, f % 3, 0:GM], w1[:, b, k, f * P:(f + 1) * P], xt[:, b, k, :], start=(k == 0), stop=(k == DC - 1))
                        last.then_inc(up, 1)
                    if b == 0:
                        turn_rows(i, 1)
                    elif more:
                        turn_rows(i + 1, 0)
                    pe.wait_ge(shaped, (g + 1) * fb + CREDIT)
                    for j in range(gt):
                        pe.wait_ge(out_made[1 - b], i + 1)
                        for f in range(fb):
                            last = pe.matmul(down_ps[:, j, 0:D], hid[:, f, j * P:(j + 1) * P], w2[:, b, f, :], start=(f == 0), stop=(f == fb - 1))
                        last.then_inc(down, 1)

            turn_rows(0, 0)
            with pe.Fori(0, NG // 2 - 1) as i:
                body(i, True)
            body(NG // 2 - 1, False)

        @block.scalar
        def _(act):
            def keep_rows(g, b):
                act.wait_ge(turned, g + 1)
                act.copy(xt[:, b], turn[:]).then_inc(kept, 1)

            def body(i, more):
                for b in range(2):
                    g = i * 2 + b
                    for f in range(fb):
                        act.wait_ge(up, g * fb + f + 1)
                        act.activation(hid[:, f, :], up_ps[:, f % 3, 0:GM], ACT.Gelu, bias=b1[:, b, f:f + 1]).then_inc(shaped, 1)
                    if b == 0 or more:
                        keep_rows(g + 1, 1 - b)

            act.sem_inc(kept, 1)
            act.sem_inc(shaped, CREDIT)
            keep_rows(0, 0)
            with act.Fori(0, NG // 2 - 1) as i:
                body(i, True)
            body(NG // 2 - 1, False)

        @block.vector
        def _(dve):
            dve.sem_inc(out_made[1], 1)
            with dve.Fori(0, NG // 2) as i:
                for b in range(2):
                    g = i * 2 + b
                    dve.wait_ge(stored[b], (i + 1) * 16)
                    for j in range(gt):
                        dve.wait_ge(down, g * gt + j + 1)
                        last = dve.tensor_tensor(y[:, b, j, :], down_ps[:, j, 0:D], b2[:, b, :], ALU.add)
                    last.then_inc(out_made[b], 1)


def gather_experts(nc, x, slots, best, out_rows):
    depth = 4
    with Mem(nc) as m, stage(nc, "added", *(f"got{s}" for s in range(depth))) as (block, added, *got):
        y = m.sb("y_y", [P, depth, 2, D])

        @block.gpsimd
        def _(pool):
            for t in range(NT):
                if t >= depth:
                    pool.wait_ge(added, 2 * (t - depth + 1))
                for n in range(2):
                    pool.indirect_dma_start(y[:, t % depth, n, :], None, out_rows,
                                            bass.IndirectOffsetOnAxis(slots[:, n, t:t + 1], 0)).then_inc(got[t % depth], 16)

        @block.vector
        def _(dve):
            for t in range(NT):
                dve.wait_ge(got[t % depth], 32 * (t // depth + 1))
                for n in range(2):
                    if n:
                        dve.wait_ge(added, 2 * t + 1)
                    dve.scalar_tensor_tensor(out=x[:, t, :], in0=y[:, t % depth, n, :], scalar=best[:, n, t:t + 1],
                                             in1=x[:, t, :], op0=ALU.mult, op1=ALU.add).then_inc(added, 1)


def mlp_weights(m, tag, hidden, w1, b1, w2, b2):
    t1 = m.sb(tag + "w1", [P, DC, hidden])
    t2 = m.sb(tag + "w2", [P, hidden // P, D])
    s1 = m.sb(tag + "b1", [P, hidden // P])
    s2 = m.sb(tag + "b2", [P, D])
    return (t1, s1, t2, s2), ((t1[:], w1.rearrange("(k p) f -> p k f", p=P)), (s1[:], columns_of(b1)),
                              (t2[:], w2.rearrange("(k p) f -> p k f", p=P)), (s2[:], row_of(b2).broadcast_to([P, D])))


def mlp(nc, tag, c, xnt, x, act_func, weights, scatter=None, ride=None):
    w1, b1, w2, b2 = weights
    fb = w2.shape[1]
    chunk = U * P
    half = chunk // 2
    with Mem(nc) as m, stage(nc, "up", "shaped", "down", "added", "biased", "scattered", *names_beside(ride)) as (
            block, up, shaped, down, added, biased, scattered, *sems):
        steps = steps_beside(ride, m, sems, tag)
        points = fb + U
        hid = m.sb(tag + "hid", [P, fb, chunk])
        up_ps = m.ps(tag + "up", [P, 2, 2, 512])
        down_ps = m.ps(tag + "down", [P, 2, 512])

        @block.gpsimd
        def _(pool):
            if scatter is not None:
                scatter_tokens(pool, *scatter, scattered)
            if steps is not None and steps.gathers:
                steps.start_pool(pool)
                with pool.Fori(0, NT // U) as j:
                    for v in range(steps.per):
                        steps.gather(pool, j, v)

        @block.sync
        def _(sp):
            if steps is not None and steps.loads:
                with sp.Fori(0, NT // U) as j:
                    for v in range(steps.per):
                        steps.load_rows(sp, j, v)

        @block.tensor
        def _(pe):
            if steps is not None:
                steps.start_pe(pe)
            with pe.Fori(0, NT // U) as j:
                for f in range(fb):
                    pe.wait_ge(shaped, j * fb + f - 2 + 1 + CREDIT)
                    for n in range(2):
                        for k in range(DC):
                            last = pe.matmul(up_ps[:, f % 2, n, 0:half], w1[:, k, f * P:(f + 1) * P],
                                             xnt[:, k, bass.ds(j * chunk + n * half, half)], start=(k == 0), stop=(k == DC - 1))
                    last.then_inc(up, 1)
                    for v in beside(steps, f, points):
                        steps.match(pe, j, v)
                pe.wait_ge(shaped, (j + 1) * fb + CREDIT)
                for u in range(U):
                    pe.wait_ge(added, j * U + u - before(u, 2) + 1 + CREDIT)
                    for f in range(fb):
                        last = pe.matmul(down_ps[:, u % 2, 0:D], hid[:, f, u * P:(u + 1) * P], w2[:, f, :],
                                         start=(f == 0), stop=(f == fb - 1))
                    last.then_inc(down, 1)
                    for v in beside(steps, fb + u, points):
                        steps.match(pe, j, v)

        @block.scalar
        def _(act):
            act.sem_inc(shaped, CREDIT)
            with act.Fori(0, NT // U) as j:
                for f in range(fb):
                    act.wait_ge(up, j * fb + f + 1)
                    act.activation(hid[:, f, :].rearrange("p (n t) -> p n t", n=2), up_ps[:, f % 2, :, 0:half],
                                   act_func, bias=b1[:, f:f + 1]).then_inc(shaped, 1)

        @block.vector
        def _(dve):
            dve.sem_inc(added, CREDIT)
            if steps is not None:
                steps.start_dve(dve)
            with dve.Fori(0, NT // U) as j:
                for f in range(fb):
                    dve_beside(steps, dve, j, f, points)
                for u in range(U):
                    t = j * U + u
                    dve.tensor_tensor(x[:, t, :], x[:, t, :], b2[:], ALU.add).then_inc(biased, 1)
                    dve.wait_ge(biased, t + 1)
                    dve.wait_ge(down, t + 1)
                    dve.tensor_tensor(x[:, t, :], x[:, t, :], down_ps[:, u % 2, 0:D], ALU.add).then_inc(added, 1)
                    dve_beside(steps, dve, j, fb + u, points)


def load(nc, *pairs):
    with stage(nc, "loaded") as (block, loaded):
        @block.sync
        def _(sp):
            for dst, src in pairs:
                sp.dma_start(dst, src, allow_slow_non_contiguous=True).then_inc(loaded, 16)
            sp.wait_ge(loaded, 16 * len(pairs))


def row_of(v):
    return v.rearrange("(a d) -> a d", a=1)


def columns_of(v):
    return v.rearrange("(k p) -> p k", p=P)


def turn_tokens(nc, tag, c, x, xt):
    with Mem(nc) as m, stage(nc, "staged", "turned", "kept") as (block, staged, turned, kept):
        slot = m.sb(tag + "slot", [P, U, D])
        turn = m.ps(tag + "turn", [P, U, 512])

        @block.vector
        def _(dve):
            with dve.Fori(0, NT // U) as i:
                for u in range(U):
                    t = i * U + u
                    dve.wait_ge(turned, t - U + 1 + CREDIT)
                    dve.tensor_copy(slot[:, u, :], x[:, t, :]).then_inc(staged, 1)

        @block.tensor
        def _(pe):
            pe.sem_inc(turned, CREDIT)
            with pe.Fori(0, NT // U) as i:
                for u in range(U):
                    t = i * U + u
                    pe.wait_ge(staged, t + 1)
                    pe.wait_ge(kept, t - U + 1 + CREDIT)
                    for k in range(DC):
                        last = pe.transpose(turn[:, u, k * P:(k + 1) * P], slot[:, u, k * P:(k + 1) * P], c.ident[:])
                    last.then_inc(turned, 1)

        @block.scalar
        def _(act):
            act.sem_inc(kept, CREDIT)
            with act.Fori(0, NT // U) as i:
                for u in range(U):
                    t = i * U + u
                    act.wait_ge(turned, t + 1 + CREDIT)
                    act.copy(xt[:, :, bass.ts(t, P)], turn[:, u, 0:D].rearrange("p (k t) -> p k t", k=DC)).then_inc(kept, 1)


def source_table1(nc, h, degree, dinv, table):
    with Mem(nc) as m, stage(nc, "chain", "rooted", "stored") as (block, chain, rooted, stored):
        deg, root, r0, r1, r2, r3 = (m.sb("d_" + n, [P, NT]) for n in ("deg", "root", "r0", "r1", "r2", "r3"))

        @block.scalar
        def _(act):
            act.wait_ge(chain, 1)
            act.activation(root[:], deg[:], ACT.Sqrt).then_inc(rooted, 1)

        @block.vector
        def _(dve):
            dve.tensor_scalar(deg[:], degree[:], 1.0, None, ALU.add).then_inc(chain, 1)
            dve.wait_ge(rooted, 1)
            dve.reciprocal(r0[:], root[:]).then_inc(chain, 1)
            dve.wait_ge(chain, 2)
            dve.tensor_tensor(r1[:], r0[:], r0[:], ALU.mult).then_inc(chain, 1)
            dve.wait_ge(chain, 3)
            dve.tensor_tensor(r2[:], r1[:], deg[:], ALU.mult).then_inc(chain, 1)
            dve.wait_ge(chain, 4)
            dve.tensor_scalar(r3[:], r2[:], -0.5, 1.5, ALU.mult, ALU.add).then_inc(chain, 1)
            dve.wait_ge(chain, 5)
            dve.tensor_tensor(dinv[:], r0[:], r3[:], ALU.mult).then_inc(chain, 1)
            dve.wait_ge(chain, 6)
            dve.tensor_tensor(h[:], h[:], dinv[:].unsqueeze(2).broadcast_to([P, NT, D]), ALU.mult).then_inc(chain, 1)

        @block.sync
        def _(sp):
            sp.wait_ge(chain, 7)
            sp.dma_start(table.rearrange("(t p) d -> p t d", p=P), h[:]).then_inc(stored, 16)
            sp.wait_ge(stored, 16)


def finish_gcn(nc, h, dinv, bias):
    with stage(nc, "chain") as (block, chain):
        @block.vector
        def _(dve):
            dve.tensor_tensor(h, h, dinv[:].unsqueeze(2).broadcast_to([P, NT, D]), ALU.mult).then_inc(chain, 1)
            dve.wait_ge(chain, 1)
            dve.tensor_tensor(h, h, bias[:].unsqueeze(1).broadcast_to([P, NT, D]), ALU.add).then_inc(chain, 1)
            dve.wait_ge(chain, 2)
            dve.tensor_scalar(h, h, 0.0, None, ALU.max)


def tables2(nc, e, h, att, own, high, target, table):
    with Mem(nc) as m, stage(nc, "chain", "stored", "split_up") as (block, chain, stored, split_up):
        tmp = m.sb("t2_tmp", [P, NT, D])
        sc = m.sb("t2_sc", [P, 2, NT])
        tgt = m.sb("t2_tgt", [P, NT, 2])
        rest = m.sb("t2_rest", [P, NT])
        rest2 = m.sb("t2_rest2", [P, NT, 2])
        highi = m.sb("t2_highi", [P, K2, G], I32)
        both = m.sb("t2_both", [P, NT])

        @block.vector
        def _(dve):
            dve.memset(target[:, NT], 0.0)
            for s in range(2):
                if s:
                    dve.wait_ge(chain, 2)
                dve.tensor_tensor(tmp[:], h[:], att[:, s, :].unsqueeze(1).broadcast_to([P, NT, D]), ALU.mult).then_inc(chain, 1)
                dve.wait_ge(chain, 2 * s + 1)
                dve.tensor_reduce(sc[:, s, :], tmp[:], AX.X, ALU.add).then_inc(chain, 1)
            dve.wait_ge(chain, 4)
            dve.tensor_copy(tgt[:, :, 0], sc[:, 1, :])
            dve.tensor_tensor(both[:], sc[:, 0, :], sc[:, 1, :], ALU.add).then_inc(chain, 1)
            dve.wait_ge(chain, 5)
            dve.scalar_tensor_tensor(out=tgt[:, :, 1], in0=both[:], scalar=SLOPE, in1=both[:], op0=ALU.mult, op1=ALU.max).then_inc(chain, 1)
            dve.tensor_scalar(highi[:], e.src[:], P.bit_length() - 1, None, ALU.arith_shift_right).then_inc(chain, 1)
            dve.wait_ge(chain, 7)
            dve.tensor_copy(high[:], highi[:])
            split(dve, split_up, 0, sc[:, 0, :], lambda s: own[:, s, :], rest[:])
            split(dve, split_up, 2 * PARTS - 1, tgt[:], lambda s: target[:, 0:NT, s, :], rest2[:])

        @block.sync
        def _(sp):
            sp.dma_start(table.rearrange("(t p) d -> p t d", p=P), h[:]).then_inc(stored, 16)
            sp.wait_ge(stored, 16)


def finish_gat(nc, acc, h, degree, bias, x):
    with Mem(nc) as m, stage(nc, "chain") as (block, chain):
        some, n, inv_n, own, own2, own3, own4, den, den2, inv = (
            m.sb("fg_" + k, [P, NT]) for k in ("some", "n", "inv_n", "own", "own2", "own3", "own4", "den", "den2", "inv"))

        @block.vector
        def _(dve):
            done = [0]

            def link(ins):
                done[0] += 1
                ins.then_inc(chain, 1)
                dve.wait_ge(chain, done[0])

            def wide(v):
                return v[:].unsqueeze(2).broadcast_to([P, NT, D])

            link(dve.tensor_scalar(some[:], degree[:], 1.0, None, ALU.is_lt))
            link(dve.tensor_scalar(n[:], degree[:], 1.0, None, ALU.max))
            link(dve.reciprocal(inv_n[:], n[:]))
            link(dve.tensor_tensor(own[:], acc[:, 0:NT, D + 1], inv_n[:], ALU.mult))
            link(dve.tensor_tensor(own2[:], own[:], some[:], ALU.add))
            link(dve.tensor_tensor(den[:], acc[:, 0:NT, D], own2[:], ALU.add))
            link(dve.tensor_scalar(den2[:], den[:], 1e-16, None, ALU.add))
            link(dve.reciprocal(inv[:], den2[:]))
            link(dve.tensor_tensor(h[:], h[:], wide(own2), ALU.mult))
            link(dve.tensor_tensor(h[:], h[:], acc[:, 0:NT, 0:D], ALU.add))
            link(dve.tensor_tensor(h[:], h[:], wide(inv), ALU.mult))
            link(dve.tensor_tensor(h[:], h[:], bias[:].unsqueeze(1).broadcast_to([P, NT, D]), ALU.add))
            link(dve.scalar_tensor_tensor(out=x[:].rearrange("p t d -> p (t d)"), in0=h[:].rearrange("p t d -> p (t d)"), scalar=0.0,
                                          in1=x[:].rearrange("p t d -> p (t d)"), op0=ALU.max, op1=ALU.add))


H1, D1 = 4, 64


def channel_attention1(nc, c, kv, wq, bq, g, bias):
    with Mem(nc) as m, stage(nc, "dve_did", "pe_did", "exped") as (block, dve_did, pe_did, exped):
        wqt = m.sb("c_wqt", [P, DC, D])
        high = m.sb("c_high", [P, 1])
        highs = m.sb("c_highs", [P, P])
        own = m.sb("c_own", [P, P])
        off = m.sb("c_off", [P, P])
        att = m.sb("c_att", [P, DC, P])
        att2 = m.sb("c_att2", [P, DC, P])
        top = m.sb("c_top", [P, DC])
        total = m.sb("c_total", [P, DC])
        inv = m.sb("c_inv", [P, DC])
        attt = m.sb("c_attt", [P, DC, P])
        acc = m.ps("c_acc", [P, DC, 512])
        turn = m.ps("c_turn", [P, 512])
        turn2 = m.ps("c_turn2", [P, 512])
        gps = m.ps("c_g", [P, DC, D])
        bps = m.ps("c_b", [1, 512])

        @block.tensor
        def _(pe):
            for q in range(DC):
                for k in range(DC):
                    last = pe.transpose(turn[:, (q * DC + k) * P:(q * DC + k + 1) * P], wq[:, k, q * P:(q + 1) * P], c.ident[:])
            last.then_inc(pe_did, 1)
            for q in range(DC):
                for t in range(NT):
                    last = pe.matmul(acc[:, q, 0:P], kv[:, t, q * P:(q + 1) * P], kv[:, t, D + q * P:D + (q + 1) * P],
                                     start=(t == 0), stop=(t == NT - 1))
            last.then_inc(pe_did, 1)
            pe.wait_ge(dve_did, 6)
            for q in range(DC):
                last = pe.transpose(turn2[:, q * P:(q + 1) * P], att2[:, q, :], c.ident[:])
            last.then_inc(pe_did, 1)
            pe.wait_ge(dve_did, 7)
            for k in range(DC):
                for q in range(DC):
                    pe.matmul(gps[:, k, q * P:(q + 1) * P], wqt[:, q, k * P:(k + 1) * P], attt[:, q, :], start=True, stop=True)
            for q in range(DC):
                last = pe.matmul(bps[:, q * P:(q + 1) * P], bq[:, q:q + 1], attt[:, q, :], start=True, stop=True)
            last.then_inc(pe_did, 1)

        @block.scalar
        def _(act):
            act.wait_ge(dve_did, 4)
            act.activation(att[:], att[:], ACT.Exp).then_inc(exped, 1)

        @block.vector
        def _(dve):
            dve.tensor_scalar(high[:], c.part[:], float(D1), None, ALU.is_ge)
            dve.tensor_scalar(highs[:], c.iota[:], float(D1), None, ALU.is_ge).then_inc(dve_did, 1)
            dve.wait_ge(dve_did, 1)
            dve.tensor_scalar(own[:], highs[:], high[:, 0:1], None, ALU.is_equal).then_inc(dve_did, 1)
            dve.wait_ge(dve_did, 2)
            dve.tensor_scalar(off[:], own[:], -1.0, -NEG, ALU.add, ALU.mult)
            dve.wait_ge(pe_did, 1)
            dve.tensor_copy(wqt[:], turn[:].rearrange("p (q f) -> p q f", q=DC)).then_inc(dve_did, 1)
            dve.wait_ge(pe_did, 2)
            dve.wait_ge(dve_did, 3)
            for q in range(DC):
                last = dve.scalar_tensor_tensor(out=att[:, q, :], in0=acc[:, q, 0:P], scalar=D1 ** -0.5, in1=off[:], op0=ALU.mult, op1=ALU.add)
            last.then_inc(exped, 1)
            dve.wait_ge(exped, 1)
            dve.tensor_reduce(top[:], att[:], AX.X, ALU.max).then_inc(exped, 1)
            dve.wait_ge(exped, 2)
            dve.tensor_tensor(att[:], att[:], top[:].unsqueeze(2).broadcast_to([P, DC, P]), ALU.subtract).then_inc(dve_did, 1)
            dve.wait_ge(exped, 3)
            dve.tensor_reduce(total[:], att[:], AX.X, ALU.add).then_inc(exped, 1)
            dve.wait_ge(exped, 4)
            dve.reciprocal(inv[:], total[:]).then_inc(dve_did, 1)
            dve.wait_ge(dve_did, 5)
            dve.tensor_tensor(att2[:], att[:], inv[:].unsqueeze(2).broadcast_to([P, DC, P]), ALU.mult).then_inc(dve_did, 1)
            dve.wait_ge(pe_did, 3)
            dve.tensor_copy(attt[:], turn2[:, 0:DC * P].rearrange("p (q d) -> p q d", q=DC)).then_inc(dve_did, 1)
            dve.wait_ge(pe_did, 4)
            dve.tensor_copy(g[:], gps[:])
            dve.tensor_copy(bias[:], bps[:, 0:D])


TAKEN = max(1, N // 2) - 1


def token_weights(nc, c, xnt, wr, br, wide, w):
    chunks = [(lo, min(lo + 512, N)) for lo in range(0, N, 512)]
    with Mem(nc) as m, stage(nc, "copied", "multiplied", "kept", "picked") as (block, copied, multiplied, kept, picked):
        wrb = m.sb("tw_wrb", [P, DC, P])
        diag = m.sb("tw_diag", [P, NT, P])
        acc = m.ps("tw_acc", [P, len(chunks), 512])

        @block.tensor
        def _(pe):
            pe.wait_ge(copied, 1)
            for q, (lo, hi) in enumerate(chunks):
                for k in range(DC):
                    last = pe.matmul(acc[:, q, 0:hi - lo], wrb[:, k, :], xnt[:, k, lo:hi], start=(k == 0), stop=(k == DC - 1))
                last.then_inc(multiplied, 1)

        @block.scalar
        def _(act):
            for q, (lo, hi) in enumerate(chunks):
                act.wait_ge(multiplied, q + 1)
                act.activation(wide[:, lo:hi], acc[:, q, 0:hi - lo], ACT.Identity, bias=br[:, 0:1]).then_inc(kept, 1)

        @block.vector
        def _(dve):
            dve.tensor_copy(wrb[:], wr[:].broadcast_to([P, DC, P])).then_inc(copied, 1)
            dve.memset(wide[:, N:NP], NEG).then_inc(copied, 1)
            dve.wait_ge(copied, 2)
            dve.wait_ge(kept, len(chunks))
            dve.tensor_tensor(diag[:], wide[:].rearrange("p (t q) -> p t q", q=P),
                              c.ident[:].unsqueeze(1).broadcast_to([P, NT, P]), ALU.mult).then_inc(picked, 1)
            dve.wait_ge(picked, 1)
            dve.tensor_reduce(w[:], diag[:], AX.X, ALU.add)


class CountSteps:

    NAMES = ("counted",)

    def __init__(self, m, sems, tag, wide, w, cnt, per):
        self.counted, = sems
        self.wide, self.w, self.cnt, self.per = wide, w, cnt, per
        self.loads, self.gathers = False, False
        self.above = m.sb(tag + "above", [P, NP])

    def start_pe(self, pe):
        pass

    def match(self, pe, i, v):
        pass

    def start_dve(self, dve):
        dve.sem_inc(self.counted, 1)

    def prepare(self, dve, i, v):
        pass

    def finish(self, dve, i, v):
        t = i * self.per + v
        dve.wait_ge(self.counted, t + 1)
        dve.tensor_scalar(self.above[:], self.wide[:], self.w[:, bass.ds(t, 1)], 0.0, ALU.is_gt, ALU.add,
                          accum_out=self.cnt[:, bass.ds(t, 1)]).then_inc(self.counted, 1)


def select_top(nc, c, w, cnt, gate, y, x, out):
    with Mem(nc) as m, stage(nc, "chain", "turned", "added", "stored") as (block, chain, turned, added, stored):
        low, cand, ind, scan, excl, pos, pos2, early, less, tie, sel = (
            m.sb("k_" + n, [P, NT]) for n in ("low", "cand", "ind", "scan", "excl", "pos", "pos2", "early", "less", "tie", "sel"))
        best = m.sb("k_best", [P, 1])
        edge1 = m.sb("k_edge1", [1, 1])
        edge = m.sb("k_edge", [P, 1])
        quota = m.sb("k_quota", [P, 1])
        tri = m.sb("k_tri", [P, P])
        tp = m.ps("k_tp", [P, 512])
        bp = m.ps("k_bp", [P, 512])
        pp = m.ps("k_pp", [P, 2, 512])

        @block.tensor
        def _(pe):
            pe.wait_ge(chain, 3)
            pe.transpose(tp[0:1, 0:P], best[:], c.ident[:]).then_inc(turned, 1)
            pe.wait_ge(chain, 4)
            pe.matmul(bp[:, 0:1], c.ones[0:1, :], edge1[:], start=True, stop=True).then_inc(turned, 1)
            pe.wait_ge(chain, 8)
            pe.matmul(pp[:, 0, 0:NT], tri[:], ind[:], start=True, stop=True)
            pe.matmul(pp[:, 1, 0:NT], c.ones[:], ind[:], start=True, stop=True).then_inc(turned, 1)

        @block.vector
        def _(dve):
            done = [0]

            def link(ins):
                done[0] += 1
                ins.then_inc(chain, 1)
                dve.wait_ge(chain, done[0])

            link(dve.tensor_scalar(low[:], cnt[:], float(TAKEN), None, ALU.is_lt))
            link(dve.scalar_tensor_tensor(out=cand[:], in0=cnt[:], scalar=1.0, in1=low[:], op0=ALU.add, op1=ALU.mult))
            link(dve.tensor_reduce(best[:], cand[:], AX.X, ALU.max))
            dve.wait_ge(turned, 1)
            link(dve.tensor_reduce(edge1[:], tp[0:1, 0:P], AX.X, ALU.max))
            dve.wait_ge(turned, 2)
            link(dve.tensor_scalar(edge[:], bp[:, 0:1], -1.0, None, ALU.add))
            link(dve.tensor_scalar(quota[:], edge[:], -1.0, float(TAKEN), ALU.mult, ALU.add))
            link(dve.tensor_scalar(ind[:], cnt[:], edge[:, 0:1], None, ALU.is_equal))
            link(dve.tensor_scalar(tri[:], c.iota[:], c.part[:, 0:1], None, ALU.is_gt))
            dve.wait_ge(turned, 3)
            link(dve.tensor_tensor_scan(scan[:], c.ones[:, 0:NT], pp[:, 1, 0:NT], 0.0, ALU.mult, ALU.add))
            link(dve.tensor_tensor(excl[:], scan[:], pp[:, 1, 0:NT], ALU.subtract))
            link(dve.tensor_tensor(pos[:], excl[:], pp[:, 0, 0:NT], ALU.add))
            link(dve.tensor_scalar(early[:], pos[:], quota[:, 0:1], None, ALU.is_lt))
            link(dve.tensor_scalar(less[:], cnt[:], edge[:, 0:1], None, ALU.is_lt))
            link(dve.tensor_tensor(tie[:], early[:], ind[:], ALU.mult))
            link(dve.tensor_tensor(sel[:], tie[:], less[:], ALU.add))
            link(dve.tensor_tensor(gate[:], sel[:].unsqueeze(2), w[:].unsqueeze(2), ALU.mult))
            for t in range(NT):
                dve.scalar_tensor_tensor(out=x[:, t, :], in0=y[:, t, :], scalar=gate[:, t, 0:1], in1=x[:, t, :],
                                         op0=ALU.mult, op1=ALU.add).then_inc(added, 1)

        @block.sync
        def _(sp):
            full = NT - U
            for lo in range(0, full, U):
                sp.wait_ge(added, lo + U)
                sp.dma_start(out[lo * P:(lo + U) * P].rearrange("(t p) d -> p t d", p=P), x[:, lo:lo + U, :]).then_inc(stored, 16)
            sp.wait_ge(added, NT)
            sp.dma_start(out[full * P:(NT - 1) * P].rearrange("(t p) d -> p t d", p=P), x[:, full:NT - 1, :]).then_inc(stored, 16)
            sp.dma_start(out[(NT - 1) * P:N], x[0:TAIL, NT - 1, :]).then_inc(stored, 16)
            sp.wait_ge(stored, (full // U + 2) * 16)


def add(nc, x, y):
    with stage(nc, "added") as (block, added):
        @block.gpsimd
        def _(pool):
            pool.tensor_tensor(x[:], x[:], y[:], ALU.add)


def program(nc, a, out):
    packed = nc.dram_tensor("packed", [NB, BLK], I32).ap()
    local_row = nc.dram_tensor("local_row", [G, BLK], BF16).ap()
    low_row = nc.dram_tensor("low_row", [G, BLK], BF16).ap()
    tiles = nc.dram_tensor("tiles", [1, G], I32).ap()
    expert_in = nc.dram_tensor("expert_in", [NSLOT + 2 * P, D], F32).ap()
    expert_out = nc.dram_tensor("expert_out", [NSLOT + 2 * P, D], F32).ap()
    rows1 = nc.dram_tensor("rows1", [NP, D], F32).ap()
    rows2 = nc.dram_tensor("rows2", [NP, D], F32).ap()
    values = nc.dram_tensor("values0", [R0 * NP, D], F32).ap()
    source_scores = nc.dram_tensor("source_scores0", [R0 * NP, H0], F32).ap()
    with Mem(nc) as m:
        c = Consts(m)
        x = m.sb("x", [P, NT, D])
        xnt = m.sb("xnt", [P, DC, NP])
        e = Edges(m)
        degree = m.sb("degree", [P, NT])
        constants(nc, c, x, a["x"])
        with Mem(nc) as m0:
            scores = m0.sb("scores0", [P, K2, G, H0])
            with Mem(nc) as m1:
                target = m1.sb("target0", [P, NT + 1, PARTS, R0 * H0], BF16)
                cat = m1.sb("cat0", [P, DC, CEND])
                g = m1.sb("g0", [P, DC, D])
                bo = m1.sb("bo0", [1, D])
                with together(nc):
                    zero_rows(nc, expert_in, expert_out)
                    layer_norm(nc, "ln0_", c, x, xnt)
                    weights0(nc, c, a, cat)
                    load(nc, (bo[:], row_of(a["L0_mix_b_out"])))
                find_groups(nc, c, a, e, packed, tiles, local_row, low_row)
                with Mem(nc) as m2:
                    sc = m2.sb("sc0", [P, NT, 2 * R0 * H0])
                    project(nc, "ps_", c, xnt, cat[:, :, CS:CEND], 2 * R0 * H0, sc)
                    score_tables0(nc, sc, source_scores, target)

                def score(**which):
                    return ScoreSteps, (c, e, H0, target, scores, local_row), dict(index=e.value_row, table=source_scores, **which)
                with Mem(nc) as m2:
                    keys = m2.sb("keys0", [P, NT, P])
                    vals = m2.sb("vals0", [P, NT, P])
                    project0(nc, c, xnt, cat, values, keys, vals, score(first=0, per=U))
                    done = NT + 2 * (NT // U)
                    with together(nc):
                        linear_attention0(nc, c, a, keys, vals, g)
                        run_steps(nc, "es0b_", score(first=done, per=3), (G // U - done) // 3)
                add_product(nc, "mix0_", xnt, g, bo, c, x, score(first=NT, per=2))
            with Mem(nc) as m1:
                acc = m1.sb("acc_0", [P, NT + 1, D + H0 + 1])
                with together(nc):
                    clear(nc, acc[:])
                    segment_softmax(nc, "sm0_", c, e, H0, H0, scores)
                run_steps(nc, "ag0_", (AggregateSteps, (c, e, e.value_row, values, H0, scores, H0 + 1, acc), dict(first=0, per=2 * U)), G // (2 * U))
                finish_attention0(nc, acc, x, degree)
        with Mem(nc) as m0:
            wr = m0.sb("wr0", [P, DC, NX])
            logits = m0.sb("logits", [P, NT, NX])
            one = m0.sb("one", [P, 2, NT, NX])
            best = m0.sb("best", [P, 2, NT])
            slots = m0.sb("slots", [P, 2, NT], I32)
            expert = m0.sb("expert", [P, NG], I32)
            with Mem(nc) as m1:
                xn = m1.sb("xn0", [P, NT, D])
                weights, loads = mlp_weights(m1, "ff0_", 1024, *(a["L0_ffn_" + n] for n in ("W1s", "b1s", "W2s", "b2s")))
                with together(nc):
                    load(nc, (wr[:], a["L0_ffn_Wr"].rearrange("(k p) e -> p k e", p=P)), *loads)
                    layer_norm(nc, "ln1_", c, x, xnt, xn)
                project(nc, "rt_", c, xnt, wr, NX, logits)
                route(nc, c, logits, one, best)
                place_tokens(nc, c, one, slots, expert)
                mlp(nc, "ff0_", c, xnt, x, ACT.Gelu, weights, scatter=(xn, slots, expert_in))
            run_experts(nc, c, expert_in, expert_out, expert, *(a["L0_ffn_" + n] for n in ("W1p", "b1p", "W2p", "b2p")), 1024)
            gather_experts(nc, x, slots, best, expert_out)
        with Mem(nc) as m0:
            h1 = m0.sb("h1", [P, NT + 1, D])
            h = h1[:, 0:NT, :]
            dinv = m0.sb("dinv", [P, NT])
            with Mem(nc) as m1:
                xn = m1.sb("xn1", [P, NT, D])
                with Mem(nc) as m2:
                    w1 = m2.sb("gw1", [P, DC, D])
                    with together(nc):
                        load(nc, (w1[:], a["L1_gnn_W1"].rearrange("(k p) d -> p k d", p=P)))
                        clear(nc, h1[:, NT, :])
                        layer_norm(nc, "ln2_", c, x, xnt, xn)
                    project(nc, "p1_", c, xnt, w1, D, h)
                per = 4 * U

                def gather1(**which):
                    return AggregateSteps, (c, e, e.src, rows1, 0, None, 0, h1), which
                with Mem(nc) as m2:
                    wqkv = m2.sb("wqkv1", [P, DC, 3 * D])
                    bkv = m2.sb("bkv1", [1, 2 * D])
                    bq = m2.sb("bq1", [P, DC])
                    kv = m2.sb("kv1", [P, NT, 2 * D])
                    g = m2.sb("g1", [P, DC, D])
                    gb = m2.sb("gb1", [1, D])
                    with together(nc):
                        load(nc, (wqkv[:], a["L1_mix_w_qkv"].rearrange("(k p) j -> p k j", p=P)),
                             (bkv[:], row_of(a["L1_mix_b_qkv"][D:3 * D])), (bq[:], columns_of(a["L1_mix_b_qkv"][0:D])))
                        source_table1(nc, h, degree, dinv, rows1)
                    project(nc, "kv_", c, xnt, wqkv[:, :, D:3 * D], 2 * D, kv, bkv, D, ride=gather1(first=0, per=per))
                    done = 2 * per * (NT // U)
                    with together(nc):
                        channel_attention1(nc, c, kv, wqkv[:, :, 0:D], bq, g, gb)
                        run_steps(nc, "ag1_", gather1(first=done, per=2 * U), (G - done) // (2 * U))
                    add_product(nc, "mix1_", xnt, g, gb, c, xn, ride=gather1(first=per * (NT // U), per=per))
                bias1 = m1.sb("bias1", [P, D])
                w2 = m1.sb("gw2", [P, DC, D])
                att = m1.sb("att2", [P, 2, D])
                bias2 = m1.sb("bias2", [P, D])
                target = m1.sb("target2", [P, NT + 1, PARTS, 2], BF16)
                own = m1.sb("own2", [P, PARTS, NT], BF16)
                high = m1.sb("high2", [P, K2, G])
                scores = m1.sb("scores2", [P, K2, G, 2])
                gain = m1.sb("gain1", [P, DC])
                shift = m1.sb("shift1", [P, DC])
                weights, loads = mlp_weights(m1, "ff1_", 768, *(a["L1_mix_" + n] for n in ("w_fc1", "b_fc1", "w_fc2", "b_fc2")))
                load(nc, (bias1[:], row_of(a["L1_gnn_b1"]).broadcast_to([P, D])))
                with together(nc):
                    load(nc, (w2[:], a["L1_gnn_W2"].rearrange("(k p) d -> p k d", p=P)),
                         (att[:, 0, :], row_of(a["L1_gnn_att_src"]).broadcast_to([P, D])),
                         (att[:, 1, :], row_of(a["L1_gnn_att_dst"]).broadcast_to([P, D])),
                         (bias2[:], row_of(a["L1_gnn_b2"]).broadcast_to([P, D])),
                         (gain[:], columns_of(a["L1_mix_norm_g"])), (shift[:], columns_of(a["L1_mix_norm_b"])), *loads)
                    finish_gcn(nc, h, dinv, bias1)
                    add(nc, x, xn)
                turn_tokens(nc, "tt_", c, h, xnt)
                project(nc, "p2_", c, xnt, w2, D, h)
                with together(nc):
                    tables2(nc, e, h, att, own, high, target, rows2)
                    layer_norm(nc, "ln3_", c, xn, xnt, None, gain, shift)

                def score2(**which):
                    return (ScoreSteps, (c, e, 1, target, scores, local_row),
                            dict(low_row=low_row, own=own, high=high, **which))
                mlp(nc, "ff1_", c, xnt, x, ACT.Gelu, weights, ride=score2(first=0, per=8, slots=4))
                done = 8 * (NT // U)
                run_steps(nc, "es2_", score2(first=done, per=G // U - done), 1)
                segment_softmax(nc, "sm2_", c, e, 1, 2, scores)
                with Mem(nc) as m2:
                    acc = m2.sb("acc_2", [P, NT + 1, D + 2])
                    clear(nc, acc[:])
                    run_steps(nc, "ag2_", (AggregateSteps, (c, e, e.src, rows2, 1, scores, 2, acc), dict(first=0, per=2 * U)), G // (2 * U))
                    finish_gat(nc, acc, h, degree, bias2, x)
        with Mem(nc) as m0:
            xn = m0.sb("xn2", [P, NT, D])
            wr = m0.sb("wr2", [P, DC, 1])
            br = m0.sb("br2", [P, 1])
            w = m0.sb("w2", [P, NT])
            wide = m0.sb("wide2", [P, NP])
            gate = m0.sb("gate2", [P, NT, 1])
            weights, loads = mlp_weights(m0, "ff2_", 1024, *(a["L1_ffn_" + n] for n in ("w1", "b1", "w2", "b2")))
            with together(nc):
                load(nc, (wr[:], a["L1_ffn_wr"].rearrange("(k p) e -> p k e", p=P)), (br[:], row_of(a["L1_ffn_br"]).broadcast_to([P, 1])), *loads)
                layer_norm(nc, "ln4_", c, x, xnt, xn)
            cnt = m0.sb("cnt2", [P, NT])
            y = m0.sb("y2", [P, NT, D])
            with together(nc):
                token_weights(nc, c, xnt, wr, br, wide, w)
                clear(nc, y[:])
                add(nc, x, xn)
            mlp(nc, "ff2_", c, xnt, y, ACT.Gelu_apprx_tanh, weights, ride=(CountSteps, (wide, w, cnt), dict(per=U)))
            select_top(nc, c, w, cnt, gate, y, x, out)


INPUTS = ["x", "src", "dst", "edge_type_8"] + ["L0_gnn_" + n for n in ("W", "attn_src", "attn_dst")] + [
    "L0_mix_" + n for n in ("W_qkv", "W_out", "b_out")] + [
    "L0_ffn_" + n for n in ("Wr", "W1s", "b1s", "W2s", "b2s", "W1p", "b1p", "W2p", "b2p")] + [
    "L1_gnn_" + n for n in ("W1", "b1", "W2", "att_src", "att_dst", "b2")] + [
    "L1_mix_" + n for n in ("w_qkv", "b_qkv", "norm_g", "norm_b", "w_fc1", "b_fc1", "w_fc2", "b_fc2")] + [
    "L1_ffn_" + n for n in ("wr", "br", "w1", "b1", "w2", "b2")]


def kernel(**inputs):
    import numpy as _np
    import concourse.bacc as _bacc
    from concourse import mybir as _mybir
    from concourse.bass_utils import run_bass_kernel_spmd as _run

    nc = _bacc.Bacc("TRN2", target_bir_lowering=False, num_devices=1)
    arrays, args = {}, {}
    for name in INPUTS:
        a = _np.ascontiguousarray(inputs[name])
        arrays[f"in_{name}"] = a
        args[name] = nc.dram_tensor(f"in_{name}", a.shape, _mybir.dt.from_np(a.dtype), kind="ExternalInput").ap()
    out = nc.dram_tensor("out_dram", (N, D), _mybir.dt.float32, kind="ExternalOutput").ap()
    program(nc, args, out)
    r = _run(nc, [arrays], core_ids=[0])
    return r.results[0]["out_dram"]
```
